# Optimizing a Trainium2 kernel written in Bass

```python
import numpy as np
import jax
import jax.numpy as jnp

def _softmax(x, axis=-1):
    return jax.nn.softmax(x, axis=axis)

def _gelu(x):
    return jax.nn.gelu(x, approximate=True)

def _silu(x):
    return jax.nn.silu(x)

def _sigmoid(x):
    return jax.nn.sigmoid(x)

def _layernorm(x, axis=-1, eps=1e-05):
    m = jnp.mean(x, axis=axis, keepdims=True)
    v = jnp.var(x, axis=axis, keepdims=True)
    return (x - m) / jnp.sqrt(v + eps)

def _scatter_add(tgt, idx, src, axis=0):
    return tgt.at[idx].add(src)

def _segment_sum(src, seg, n):
    return jax.ops.segment_sum(src, seg, n)
kernel_name = 'mk_conv_preact_d4_conv_nhwc128_r2_4ae4ec'

def setup_inputs(seed: int=0):
    np.random.seed(seed)
    _w = jnp.asarray

    def _rec_inputs():
        import jax
        import jax.numpy as jnp
        _gk = jax.random.key(seed)
        x = -0.000125 + 0.9999 * jax.random.normal(jax.random.fold_in(_gk, 1), (32, 32, 32, 64), jnp.float32)
        return x
    x = _rec_inputs()

    def _L0_conv_setup():
        import jax, jax.numpy as jnp
        import numpy as np
        BN_EPS = 1e-05
        key = jax.random.key(seed)
        k1, k2, k3 = jax.random.split(key, 3)
        B, IN, NEST, P2, OUT = (32, 32, 32, 64, 32)
        ini = float(np.sqrt(3.0 / OUT / IN))
        A = jax.random.normal(k1, (B, IN, NEST, P2), dtype=jnp.float32)
        P1 = jax.random.uniform(k2, (NEST, OUT, IN), dtype=jnp.float32, minval=-ini, maxval=ini)
        P3 = jax.random.uniform(k3, (NEST, OUT, IN), dtype=jnp.float32, minval=-ini, maxval=ini)
        gamma = jnp.ones((OUT,), dtype=jnp.float32)
        beta = jnp.zeros((OUT,), dtype=jnp.float32)
        return {'A': A, 'P1': P1, 'P3': P3, 'gamma': gamma, 'beta': beta, 'permutation_size1': NEST, 'permutation_size2': P2, 'BATCH_SIZE': B}
    _L0_conv_all = _L0_conv_setup()
    _L0_conv_in = {k: v for k, v in _L0_conv_all.items() if k in ('P1', 'P3', 'gamma', 'beta')}
    del _L0_conv_all

    def _L1_conv_setup():
        import jax, jax.numpy as jnp
        import numpy as np
        H = 64

        def dense(x, W, b):
            return jax.nn.silu(x @ W + b)

        def mlp2(x, Ws, bs):
            h = dense(x, Ws[0], bs[0])
            return dense(h, Ws[1], bs[1])

        def residual(x, Ws, bs):
            return x + mlp2(x, Ws, bs)
        key = jax.random.key(seed)
        ks = jax.random.split(key, 7)
        B, N = (4, 128)
        scale = 1.0 / np.sqrt(H)
        kemb = jax.random.normal(ks[0], (B, N, N, H), dtype=jnp.float32)
        emb_W = jax.random.normal(ks[1], (3, 2, H, H), dtype=jnp.float32) * scale
        emb_b = jnp.zeros((3, 2, H), dtype=jnp.float32)
        mult_W = jax.random.normal(ks[2], (2, 2, H, H), dtype=jnp.float32) * scale
        mult_b = jnp.zeros((2, 2, H), dtype=jnp.float32)
        out_W = jax.random.normal(ks[3], (2, H, H), dtype=jnp.float32) * scale
        out_b = jnp.zeros((2, H), dtype=jnp.float32)
        return {'kemb': kemb, 'emb_W': emb_W, 'emb_b': emb_b, 'mult_W': mult_W, 'mult_b': mult_b, 'out_W': out_W, 'out_b': out_b}
    _L1_conv_all = _L1_conv_setup()
    _L1_conv_in = {k: v for k, v in _L1_conv_all.items() if k in ('emb_W', 'emb_b', 'mult_W', 'mult_b', 'out_W', 'out_b')}
    del _L1_conv_all

    def _L2_conv_setup():
        import jax
        import jax.numpy as jnp
        import numpy as np
        from jax import lax
        B, L, A, C = (32, 64, 32, 64)
        KT = 3
        key = jax.random.key(seed)
        k1, k2, k3 = jax.random.split(key, 3)
        x = jax.random.normal(k1, (B, L, A, C), dtype=jnp.float32)
        W = jax.random.normal(k2, (C, C, KT, 1), dtype=jnp.float32) * (1.0 / np.sqrt(C * KT))
        b = jax.random.normal(k3, (C,), dtype=jnp.float32) * 0.01
        return {'x': x, 'W': W, 'b': b}
    _L2_conv_all = _L2_conv_setup()
    _L2_conv_in = {k: v for k, v in _L2_conv_all.items() if k in ('W', 'b')}
    del _L2_conv_all

    def _L3_conv_setup():
        import jax, jax.numpy as jnp
        import numpy as np
        B, H, W, C = (16, 48, 48, 64)
        FOCAL_LEVEL = 3
        FOCAL_WINDOW = 3
        FOCAL_FACTOR = 2
        LN_EPS = 0.001

        def dwconv_same(x, k):
            return jax.lax.conv_general_dilated(x, k, window_strides=(1, 1), padding='SAME', dimension_numbers=('NHWC', 'HWIO', 'NHWC'), feature_group_count=x.shape[-1])
        key = jax.random.key(seed)
        ks = jax.random.split(key, 12)
        s = 0.02
        out_f = 2 * C + (FOCAL_LEVEL + 1)
        inp = {'x': jax.random.normal(ks[0], (B, H, W, C), dtype=jnp.float32), 'Wf': jax.random.normal(ks[1], (C, out_f), dtype=jnp.float32) * s, 'bf': jnp.zeros((out_f,), dtype=jnp.float32), 'Wh': jax.random.normal(ks[2], (C, C), dtype=jnp.float32) * s, 'bh': jnp.zeros((C,), dtype=jnp.float32), 'gamma': jnp.ones((C,), dtype=jnp.float32), 'beta': jnp.zeros((C,), dtype=jnp.float32), 'Wp': jax.random.normal(ks[3], (C, C), dtype=jnp.float32) * s, 'bp': jnp.zeros((C,), dtype=jnp.float32)}
        for l in range(FOCAL_LEVEL):
            kk = FOCAL_FACTOR * l + FOCAL_WINDOW
            inp[f'k{l}'] = jax.random.normal(ks[4 + l], (kk, kk, 1, C), dtype=jnp.float32) * s
        return inp
    _L3_conv_all = _L3_conv_setup()
    _L3_conv_in = {k: v for k, v in _L3_conv_all.items() if k in ('Wf', 'bf', 'k0', 'k1', 'k2', 'Wh', 'bh', 'gamma', 'beta', 'Wp', 'bp')}
    del _L3_conv_all
    return {'x': x, 'L0_conv_P1': _L0_conv_in['P1'], 'L0_conv_P3': _L0_conv_in['P3'], 'L0_conv_gamma': _L0_conv_in['gamma'], 'L0_conv_beta': _L0_conv_in['beta'], 'L1_conv_emb_W': _L1_conv_in['emb_W'], 'L1_conv_emb_b': _L1_conv_in['emb_b'], 'L1_conv_mult_W': _L1_conv_in['mult_W'], 'L1_conv_mult_b': _L1_conv_in['mult_b'], 'L1_conv_out_W': _L1_conv_in['out_W'], 'L1_conv_out_b': _L1_conv_in['out_b'], 'L2_conv_W': _L2_conv_in['W'], 'L2_conv_b': _L2_conv_in['b'], 'L3_conv_Wf': _L3_conv_in['Wf'], 'L3_conv_bf': _L3_conv_in['bf'], 'L3_conv_k0': _L3_conv_in['k0'], 'L3_conv_k1': _L3_conv_in['k1'], 'L3_conv_k2': _L3_conv_in['k2'], 'L3_conv_Wh': _L3_conv_in['Wh'], 'L3_conv_bh': _L3_conv_in['bh'], 'L3_conv_gamma': _L3_conv_in['gamma'], 'L3_conv_beta': _L3_conv_in['beta'], 'L3_conv_Wp': _L3_conv_in['Wp'], 'L3_conv_bp': _L3_conv_in['bp']}

def reference(x, L0_conv_P1, L0_conv_P3, L0_conv_gamma, L0_conv_beta, L1_conv_emb_W, L1_conv_emb_b, L1_conv_mult_W, L1_conv_mult_b, L1_conv_out_W, L1_conv_out_b, L2_conv_W, L2_conv_b, L3_conv_Wf, L3_conv_bf, L3_conv_k0, L3_conv_k1, L3_conv_k2, L3_conv_Wh, L3_conv_bh, L3_conv_gamma, L3_conv_beta, L3_conv_Wp, L3_conv_bp):
    import jax
    import jax.numpy as jnp

    def _L0_conv_ref(A, P1, P3, gamma, beta, permutation_size1, permutation_size2, BATCH_SIZE):
        import jax, jax.numpy as jnp
        import numpy as np
        BN_EPS = 1e-05
        A1 = jnp.einsum('noi,bint->bont', P1, A)
        A3 = jnp.einsum('noi,bin->bon', P3, A.mean(-1))
        x = A1 + 0.1 * A3[..., None]
        x = jax.nn.relu(x)
        mean = x.mean(axis=(0, 2, 3), keepdims=True)
        var = x.var(axis=(0, 2, 3), keepdims=True)
        xn = (x - mean) * jax.lax.rsqrt(var + BN_EPS)
        return xn * gamma[None, :, None, None] + beta[None, :, None, None]

    def _L1_conv_ref(kemb, emb_W, emb_b, mult_W, mult_b, out_W, out_b):
        import jax, jax.numpy as jnp
        import numpy as np
        H = 64

        def dense(x, W, b):
            return jax.nn.silu(x @ W + b)

        def mlp2(x, Ws, bs):
            h = dense(x, Ws[0], bs[0])
            return dense(h, Ws[1], bs[1])

        def residual(x, Ws, bs):
            return x + mlp2(x, Ws, bs)
        self_message = mlp2(kemb, emb_W[0], emb_b[0])
        kemb_0 = mlp2(kemb, emb_W[1], emb_b[1])
        kemb_1 = mlp2(kemb, emb_W[2], emb_b[2])
        kemb_multed = jnp.einsum('bikh,bkjh->bijh', kemb_0, kemb_1)
        kemb_multed = residual(kemb_multed, mult_W[0], mult_b[0])
        kemb_multed = residual(kemb_multed, mult_W[1], mult_b[1])
        return residual(self_message * kemb_multed, out_W, out_b)

    def _L2_conv_ref(x, W, b):
        import jax
        import jax.numpy as jnp
        import numpy as np
        from jax import lax
        B, L, A, C = (32, 64, 32, 64)
        KT = 3
        length, n_agents = (x.shape[1], x.shape[2])
        xc = jnp.transpose(x, (0, 3, 1, 2))
        res = xc
        pad_t = (KT - 1) // 2
        y = lax.conv_general_dilated(xc, W, window_strides=(1, 1), padding=[(pad_t, pad_t), (0, 0)], dimension_numbers=('NCHW', 'OIHW', 'NCHW')) + b[None, :, None, None]
        agent_sum = jnp.sum(y, axis=3, keepdims=True)
        time_sum = jnp.sum(y, axis=2, keepdims=True)
        scale = (length + n_agents - 2) ** 0.5
        g = (agent_sum + time_sum - y) / scale
        out = jax.nn.relu(g + res)
        return jnp.transpose(out, (0, 2, 3, 1))

    def _L3_conv_ref(x, Wf, bf, k0, k1, k2, Wh, bh, gamma, beta, Wp, bp):
        import jax, jax.numpy as jnp
        import numpy as np
        B, H, W, C = (16, 48, 48, 64)
        FOCAL_LEVEL = 3
        FOCAL_WINDOW = 3
        FOCAL_FACTOR = 2
        LN_EPS = 0.001

        def dwconv_same(x, k):
            return jax.lax.conv_general_dilated(x, k, window_strides=(1, 1), padding='SAME', dimension_numbers=('NHWC', 'HWIO', 'NHWC'), feature_group_count=x.shape[-1])
        gelu = lambda t: jax.nn.gelu(t, approximate=False)
        y = jnp.einsum('bhwc,cd->bhwd', x, Wf) + bf
        q = y[..., :C]
        ctx = y[..., C:2 * C]
        gates = y[..., 2 * C:]
        ctx_all = jnp.zeros_like(ctx)
        for l, k in enumerate((k0, k1, k2)):
            ctx = gelu(dwconv_same(ctx, k))
            ctx_all = ctx_all + ctx * gates[..., l:l + 1]
        ctx_global = gelu(jnp.mean(ctx, axis=(1, 2), keepdims=True))
        ctx_all = ctx_all + ctx_global * gates[..., FOCAL_LEVEL:]
        modulator = jnp.einsum('bhwc,cd->bhwd', ctx_all, Wh) + bh
        x_out = q * modulator
        mu = jnp.mean(x_out, axis=-1, keepdims=True)
        var = jnp.mean(jnp.square(x_out - mu), axis=-1, keepdims=True)
        x_out = (x_out - mu) * jax.lax.rsqrt(var + LN_EPS) * gamma + beta
        x_out = jnp.einsum('bhwc,cd->bhwd', x_out, Wp) + bp
        return x_out

    def _gn(v, G=32, eps=1e-05):
        B_, H_, W_, C_ = v.shape
        g = v.reshape(B_, H_, W_, G, C_ // G)
        m = jnp.mean(g, axis=(1, 2, 4), keepdims=True)
        s = jnp.var(g, axis=(1, 2, 4), keepdims=True)
        return ((g - m) / jnp.sqrt(s + eps)).reshape(v.shape)

    def _ln_c(v, eps=1e-06):
        m = jnp.mean(v, axis=-1, keepdims=True)
        s = jnp.var(v, axis=-1, keepdims=True)
        return (v - m) / jnp.sqrt(s + eps)

    def _ln_t(v, eps=1e-05):
        m = jnp.mean(v, axis=-1, keepdims=True)
        s = jnp.var(v, axis=-1, keepdims=True)
        return (v - m) / jnp.sqrt(s + eps)

    def _to_tokens(v):
        B_, H_, W_, C_ = v.shape
        return v.reshape(B_, H_ * W_, C_)

    def _from_tokens(t, like):
        return t.reshape(like.shape)
    x = x + _L0_conv_ref(_gn(x), L0_conv_P1, L0_conv_P3, L0_conv_gamma, L0_conv_beta, 32, 64, 32)
    x = x + _L1_conv_ref(_gn(x), L1_conv_emb_W, L1_conv_emb_b, L1_conv_mult_W, L1_conv_mult_b, L1_conv_out_W, L1_conv_out_b)
    x = x + _L2_conv_ref(_gn(x), L2_conv_W, L2_conv_b)
    x = x + _L3_conv_ref(_gn(x), L3_conv_Wf, L3_conv_bf, L3_conv_k0, L3_conv_k1, L3_conv_k2, L3_conv_Wh, L3_conv_bh, L3_conv_gamma, L3_conv_beta, L3_conv_Wp, L3_conv_bp)
    return x

_drawn_inputs = setup_inputs


def setup_inputs(seed=0):
    import zlib

    import numpy as np

    out = dict(_drawn_inputs(seed))
    spreads = {'L0_conv_gamma': (1.0, 0.2),
     'L0_conv_beta': (0.0, 0.1),
     'L1_conv_emb_b': (0.0, 0.1),
     'L1_conv_mult_b': (0.0, 0.314),
     'L1_conv_out_b': (0.0, 0.1),
     'L3_conv_bf': (0.0, 0.406),
     'L3_conv_bh': (0.0, 0.1),
     'L3_conv_gamma': (1.0, 0.6),
     'L3_conv_beta': (0.0, 0.8),
     'L3_conv_bp': (0.0, 0.1)}
    factors = {'L0_conv_P3': 4.898,
     'L3_conv_k0': 8.0,
     'L3_conv_k1': 8.0,
     'L3_conv_k2': 64.0,
     'L3_conv_Wh': 8.0}
    for name, (base, spread) in spreads.items():
        noise = np.random.default_rng([zlib.crc32(name.encode()), seed]).standard_normal(out[name].shape)
        drawn = base * np.exp(spread * noise) if base else spread * noise
        out[name] = jnp.asarray(drawn.astype(out[name].dtype))
    for name, factor in factors.items():
        out[name] = (out[name] * factor).astype(out[name].dtype)
    return out
```

```python
from contextlib import ExitStack

import concourse.bass as bass
from concourse import mybir

P = 128
F32 = mybir.dt.float32
BF16 = mybir.dt.bfloat16
ALU = mybir.AluOpType
ACT = mybir.ActivationFunctionType
AX = mybir.AxisListType

B, H, W, C = 32, 32, 32, 64
BH = 2
NS = B // BH
TOK = H * W
W4 = P // H
WB = W // W4
HALF = 512
EPS_GN = 1e-5
EPS_BN = 1e-5
EPS_LN = 1e-3

XCH = 4
NCH = B // XCH
NB8 = 8
GS = 4
NG = NS // GS
HS = 8
NHALF = NS // HS
NB = BH * HS
COLS = WB * NB
LEVELS = 3
KERNELS = (3, 5, 7)
UCH = 8
RING = 2
NU = C // UCH
NJ = 3 * W4
UH = 2 * H - 1
WIN = H * UCH
BAND = NJ * UH * UCH
QP = 32
HSL = 2 * HS
TSTAGES = 6


def conv_preact_kernel(nc, x, P1, P3, bn_gamma, bn_beta, emb_W, emb_b, mult_W, mult_b, out_W, out_b,
                       cW, cb, Wf, bf, k0, k1, k2, Wh, bh_, ln_gamma, ln_beta, Wp, bp, out):
    band_dram = nc.dram_tensor("band_tables", (LEVELS, NU, W4, BAND), F32, kind="Internal")

    ctx = ExitStack()
    with ctx:
        def sb(name, shape, dt=F32):
            return ctx.enter_context(nc.sbuf_tensor(name, shape, dt))

        named = {}

        def sem(name):
            if name not in named:
                named[name] = ctx.enter_context(nc.semaphore(name))
            return named[name]

        XB = sb("XB", [P, NS * TOK])
        WK = sb("WK", [P, 24 * TOK])
        RG = sb("RG", [P, RING, NJ * WIN])
        WT = sb("WT", [P, 18, P])
        WCG = sb("WCG", [P, P + 8])
        ROWB = sb("ROWB", [P, 2 * P + P + 8], BF16)
        ident = sb("ident", [P, P])
        ones = sb("ones", [P, P])
        onesb = sb("onesb", [P, P], BF16)
        pairm = sb("pairm", [P, P])
        rowm = sb("rowm", [P, P])
        meanm = sb("meanm", [P, P])
        centm = sb("centm", [P, P])
        small = sb("small", [P, 32])
        BC = sb("BC", [P, 24])
        st = sb("st", [P, HS, 12])
        mv = sb("mv", [P, HS, 2])
        me = sb("me", [P, 2, HS])
        gm = sb("gm", [P, 4, HS])
        mhalf = sb("mhalf", [P, TOK])
        gates = sb("gates", [P, 4, COLS])
        xs = sb("xs", [P, GS, H])
        xh = sb("xh", [P, 3, GS, W])
        tt = sb("tt", [P, GS, W])
        mh8 = sb("mh8", [P, HS])

        ps = ctx.enter_context(nc.psum_tensor("ps", [P, 8, HALF], F32))

        def unit(u):
            return ps[:, 2 * u:2 * u + 2, :].rearrange("p a n -> p (a n)")

        EB, MB, OB, CB, QB, HB, LG, LB, PB, BG, BB, CB63, PB2 = 0, 6, 10, 12, 13, 14, 15, 16, 17, 18, 19, 20, 21
        WE, WM, WO, WC, WQ, WHI, WPI = 0, 6, 10, 12, 15, 16, 17

        XA = XB[:, :].rearrange("p (b k c) -> p b k c", b=B, k=WB)
        AF = WK[:, 0:B * WB * C]
        AV = AF.rearrange("p (s k g c) -> p g s k c", g=BH, s=NS, k=WB)

        def A(b0, n, k=slice(0, WB)):
            return AV[:, b0 // NS, b0 % NS:b0 % NS + n, k, :]
        SWB = WK[:, 16384:18432]
        SQ = [WK[:, 18432 + 2048 * i:20480 + 2048 * i] for i in range(2)]
        MEANE = WK[:, 22528:24576]
        RGF = RG[:, :, :].rearrange("p r n -> p (r n)")
        P1N, P3N, P1T, P3T = (RGF[:, 1024 * i:1024 * (i + 1)].rearrange("p (k m) -> p k m", k=WB) for i in range(4))
        CWN = RGF[:, 4096:4096 + 3 * P].rearrange("p (t m) -> p t m", t=3)
        CWR = RGF[:, 4480:4480 + 3 * C]
        SUMA = RGF[:, 4672:4672 + B * WB].rearrange("p (b k) -> p b k", b=B)
        BAND_SB = WK[:, 0:2 * BAND].rearrange("p (l n) -> p l n", l=2)
        TAPS = (0, 9, 34, 83)
        KT = WK[:, 12096:12096 + TAPS[LEVELS] * UCH]
        ROWF = WK[:, 12800:12800 + 392]
        ROWR = WK[:, 13200:13200 + 392]
        ROWH = WK[:, 13600:13600 + 392].bitcast(BF16).rearrange("p (a n) -> p a n", a=2)

        def buf(i):
            return WK[:, 4096 * i:4096 * (i + 1)].rearrange("p (s n) -> p s n", s=GS)

        G, HA, HBF, SELF, K0T, K1T = (buf(i) for i in range(6))
        E1, M, T1 = G, K0T, HBF
        HBR = HBF.rearrange("p s n -> p (s n)").rearrange("p (h s w) -> p h s w", h=H, s=GS)
        HAR = HA.rearrange("p s n -> p (s n)").rearrange("p (w s h) -> p w s h", w=W, s=GS)
        XBS = XB[:, :].rearrange("p (s n) -> p s n", s=NS)

        BUF1 = WK[:, 0:8192]
        BUF2 = WK[:, 8192:16384]
        ALL = WK[:, 16384:24576]
        RSUM = BUF1[:, 7168:8192]
        GLOB = BUF1[:, 6144:7168]

        def ctxv(b):
            return b.rearrange("p (g c n) -> p g c n", g=BH, c=C)

        TMP = mhalf
        MBT, QT, XO, SQT, SD, XN, YT, OT = ([BUF2[:, 1024 * i + 512 * j:1024 * i + 512 * j + 512] for j in range(2)]
                                            for i in range(8))

        block = ctx.enter_context(nc.Block())

        n_w_dmas = 0

        @block.sync
        def _(sp):
            for ch in range(NCH):
                for w4 in range(W4):
                    sp.dma_start(XA[H * w4:H * (w4 + 1), XCH * ch:XCH * (ch + 1), :, :].rearrange("p b k c -> p b (k c)"),
                                 x[XCH * ch:XCH * (ch + 1), :, WB * w4:WB * (w4 + 1), :].rearrange("b h k c -> h b (k c)")
                                 ).then_inc(sem(f"x_loaded{ch}"), 16)
            for l in range(LEVELS):
                sp.wait_ge(sem("band_copied"), W4 * (l + 1))
                for w in range(W4):
                    sp.dma_start(band_dram.ap()[l, :, w, :], BAND_SB[QP * w:QP * w + NU, l % 2, :]
                                 ).then_inc(sem("band_stored0" if l == 0 else "band_stored"), 16)
            sp.wait_ge(sem("band_stored0"), 16 * W4)
            sp.wait_ge(sem("band_stored"), 16 * (LEVELS - 1) * W4)
            with sp.Fori(0, NHALF) as hf:
                for l in range(LEVELS):
                    for q in range(NU):
                        n = l * NU + q
                        if n < RING:
                            sp.wait_ge(sem("coef3_mm"), hf + 1)
                        else:
                            sp.wait_ge(sem("conv_mm"), hf * LEVELS * NU + n - RING + 1)
                        for j in range(NJ):
                            src = bass.AP(tensor=band_dram.ap().tensor,
                                          offset=(l * NU + q) * W4 * BAND + (j * UH + H - 1) * UCH,
                                          ap=[[BAND, W4], [-UCH, H], [1, WIN]])
                            sp.dma_start(RG[:, n % RING, WIN * j:WIN * (j + 1)], src
                                         ).then_inc(sem(f"ring_loaded{n % RING}"), 16)
                for i in range(HSL):
                    s, hh = i // 2, i % 2
                    sp.wait_ge(sem("ot_ready"), hf * HSL + i + 1)
                    for bh in range(BH):
                        dst = out.rearrange("(g f s) h (a q t) c -> f g s a h q (t c)", g=BH, f=NHALF, a=2, q=W4)
                        sp.dma_start(dst[bass.ds(hf, 1), bh, s, hh, :, :, :].rearrange("f h q n -> (f h) q n"),
                                     OT[i % 2][:, 256 * bh:256 * (bh + 1)]).then_inc(sem(f"stored{i % 2}"), 16)
            for j in range(2):
                sp.wait_ge(sem(f"stored{j}"), NHALF * HSL // 2 * 16 * BH)

        @block.gpsimd
        def _(pool):
            nc.gpsimd.memset(WT[:, :, :], 0.0).then_inc(sem("zeroed"), 1)
            nc.gpsimd.memset(WCG[:, :], 0.0).then_inc(sem("zeroed"), 1)
            nc.gpsimd.memset(RGF[:, 0:2048], 0.0).then_inc(sem("zeroed"), 1)
            nc.gpsimd.memset(CWN, 0.0).then_inc(sem("zeroed"), 1)
            nc.gpsimd.memset(ident[:, :], 0.0).then_inc(sem("ident_zero"), 1)
            pool.wait_ge(sem("ident_zero"), 1)
            nc.gpsimd.affine_select(out=ident[:, :], in_=ident[:, :], compare_op=ALU.not_equal, fill=1.0, base=0,
                                    pattern=[[-1, P]], channel_multiplier=1).then_inc(sem("ident_set"), 1)
            nc.gpsimd.memset(mhalf[:, :], -0.5).then_inc(sem("mhalf_set"), 1)
            nc.gpsimd.memset(mh8[:, :], -0.5).then_inc(sem("mhalf_set"), 1)
            pool.wait_ge(sem("taps_loaded"), 16 * LEVELS * W4)
            for l, kk in enumerate(KERNELS):
                r = kk // 2
                if l == 2:
                    pool.wait_ge(sem("band_stored0"), 16 * W4)
                nc.gpsimd.memset(BAND_SB[:, l % 2, :], 0.0).then_inc(sem("band_zero"), 1)
                pool.wait_ge(sem("band_zero"), l + 1)
                taps = KT[:, UCH * TAPS[l]:UCH * TAPS[l + 1]].rearrange("p (a b c) -> p b a c", a=kk, b=kk)
                for w in range(W4):
                    p = slice(QP * w, QP * w + NU)
                    table = BAND_SB[p, l % 2, :].rearrange("p (j u c) -> p j u c", j=NJ, u=UH)
                    nc.gpsimd.tensor_copy(table[:, w + W4 - r:w + W4 + r + 1, H - 1 - r:H + r, :], taps[p]
                                          ).then_inc(sem("band_copied"), 1)
                    pool.wait_ge(sem("band_copied"), W4 * l + w + 1)
            pool.wait_ge(sem("mhalf_set"), 2)
            pool.wait_ge(sem("var0_ready"), 1)
            nc.gpsimd.tensor_tensor(SQ[1][:, 0:1024], SQ[0][:, 1024:2048], mhalf[:, :], ALU.pow).then_inc(sem("rstd0"), 1)
            pool.wait_ge(sem("bnvar_ready"), 1)
            nc.gpsimd.tensor_tensor(small[:, 4:5], small[:, 3:4], mhalf[:, 0:1], ALU.pow).then_inc(sem("bnrstd"), 1)
            with pool.Fori(0, NG) as g:
                for n in range(2):
                    pool.wait_ge(sem("gnvar"), 2 * g + n + 1)
                    nc.gpsimd.tensor_tensor(gm[:, 3, 0:GS], gm[:, 2, 0:GS], mh8[:, 0:GS], ALU.pow
                                            ).then_inc(sem("gnrstd"), 1)
            with pool.Fori(0, NHALF) as hf:
                pool.wait_ge(sem("gnvar3"), hf + 1)
                nc.gpsimd.tensor_tensor(gm[:, 3, :], gm[:, 2, :], mh8[:, :], ALU.pow).then_inc(sem("gnrstd3"), 1)

        @block.scalar
        def _(act):
            ctx.enter_context(nc.allow_non_contiguous_dma(reason="short loads of biases and taps"))
            for l, (kk, k) in enumerate(zip(KERNELS, (k0, k1, k2))):
                for w in range(W4):
                    src = bass.AP(tensor=k.tensor, offset=k.offset + (kk * kk - 1) * C,
                                  ap=[[UCH, NU], [-C, kk * kk], [1, UCH]])
                    act.dma_start(KT[QP * w:QP * w + NU, UCH * TAPS[l]:UCH * TAPS[l + 1]].rearrange("p (t c) -> p t c", c=UCH),
                                  src).then_inc(sem("taps_loaded"), 16)
            act.wait_ge(sem("zeroed"), 4)
            for w4 in range(W4):
                p = slice(H * w4, H * (w4 + 1))
                act.dma_start(P1N[p, :, H * w4:H * (w4 + 1)],
                              P1[WB * w4:WB * (w4 + 1), :, :].rearrange("k o i -> o k i")).then_inc(sem("p_loaded"), 16)
                act.dma_start(P3N[p, :, H * w4:H * (w4 + 1)],
                              P3[WB * w4:WB * (w4 + 1), :, :].rearrange("k o i -> o k i")).then_inc(sem("p_loaded"), 16)
                act.dma_start(BC[p, BG:BG + 1], bn_gamma.rearrange("(h o) -> h o", o=1)).then_inc(sem("w_loaded"), 16)
                act.dma_start(BC[p, BB:BB + 1], bn_beta.rearrange("(h o) -> h o", o=1)).then_inc(sem("w_loaded"), 16)
            for bh in range(BH):
                p = slice(C * bh, C * (bh + 1))
                for dst, src in (
                    (WT[p, WE:WE + 6, p], emb_W.rearrange("l j i o -> i (l j) o")),
                    (WT[p, WM:WM + 4, p], mult_W.rearrange("l j i o -> i (l j) o")),
                    (WT[p, WO:WO + 2, p], out_W.rearrange("j i o -> i j o")),
                    (WT[p, WQ, p], Wf[:, 0:C]),
                    (WT[p, WHI, p], Wh), (WT[p, WPI, p], Wp),
                    (WCG[p, p], Wf[:, C:2 * C]), (WCG[p, P + 4 * bh:P + 4 * bh + 4], Wf[:, 2 * C:2 * C + 4]),
                    (CWR[p, :], cW.rearrange("o i t u -> o (i t u)")),
                    (BC[p, EB:EB + 6], emb_b.rearrange("l j o -> o (l j)")),
                    (BC[p, MB:MB + 4], mult_b.rearrange("l j o -> o (l j)")),
                    (BC[p, OB:OB + 2], out_b.rearrange("j o -> o j")),
                    (BC[p, CB:CB + 1], cb.rearrange("(c o) -> c o", o=1)),
                    (BC[p, QB:QB + 1], bf[0:C].rearrange("(c o) -> c o", o=1)),
                    (BC[p, HB:HB + 1], bh_.rearrange("(c o) -> c o", o=1)),
                    (BC[p, LG:LG + 1], ln_gamma.rearrange("(c o) -> c o", o=1)),
                    (BC[p, LB:LB + 1], ln_beta.rearrange("(c o) -> c o", o=1)),
                    (BC[p, PB:PB + 1], bp.rearrange("(c o) -> c o", o=1)),
                ):
                    act.dma_start(dst, src).then_inc(sem("w_loaded"), 16)
            n_w = 2 * W4 + BH * 18
            n = 0
            for bh in range(BH):
                for at, src in ((C * bh, emb_b[1, 1]), (P + C * bh, emb_b[2, 1]), (2 * P + C * bh, bf[C:2 * C]),
                                (3 * P + 4 * bh, bf[2 * C:2 * C + 4])):
                    k = src.shape[0]
                    act.dma_start(ROWF[:, at:at + k],
                                  bass.AP(tensor=src.tensor, offset=src.offset, ap=[[0, P], [1, k]])
                                  ).then_inc(sem("row_loaded"), 16)

            for ch in range(NCH):
                act.wait_ge(sem(f"x_loaded{ch}"), 16 * W4)
                if ch >= 2:
                    act.wait_ge(sem("sq_used"), ch - 1)
                nc.scalar.activation(SQ[ch % 2], XA[:, XCH * ch:XCH * (ch + 1), :, :].rearrange("p b k c -> p (b k c)"),
                                     ACT.Square).then_inc(sem("sq_ready"), 1)
            for n in range(16):
                b8, k = n // 4, 2 * (n % 4)
                act.wait_ge(sem("relu_mm"), n + 1)
                r0 = A(NB8 * b8, NB8, slice(k, k + 2))
                nc.scalar.activation(r0.rearrange("p b k c -> p k b c"),
                                     unit(n % 4).rearrange("p (k b c) -> p k b c", k=2, b=NB8), ACT.Relu,
                                     accum_out=xs[:, 0, n:n + 1]).then_inc(sem("relu_done"), 1)
                act.wait_ge(sem("relu_done"), n + 1)
                nc.scalar.activation(unit(n % 4).rearrange("p (k b c) -> p k b c", k=2, b=NB8),
                                     r0.rearrange("p b k c -> p k b c"), ACT.Square,
                                     accum_out=xs[:, 1, n:n + 1]).then_inc(sem("relu_sq"), 1)
            act.wait_ge(sem("bn_coef"), 1)
            for i in range(16):
                v = AF[:, 1024 * i:1024 * (i + 1)]
                nc.scalar.activation(v, v, ACT.Identity, bias=small[:, 6:7], scale=small[:, 5:6]).then_inc(sem("bn_applied"), 1)
            for s in range(1, NS, 2):
                act.wait_ge(sem("xt_mm"), s + 1)
                nc.scalar.activation(XBS[:, s, :].rearrange("p (h a k) -> p k a h", h=H, a=W4),
                                     unit(s % 4).rearrange("p (k a h) -> p k a h", k=WB, a=W4),
                                     ACT.Copy).then_inc(sem("xt_out_a"), 1)

            with act.Fori(0, NG) as g:
                def silu(stage, dst, bias=None, free=None, src=lambda v: v):
                    for u in range(GS):
                        act.wait_ge(sem(stage + "_mm"), GS * g + u + 1)
                        if free is not None:
                            act.wait_ge(sem(free), GS * g + u + 1)
                        nc.scalar.activation(dst(u), src(unit(u)), ACT.Silu,
                                             bias=0.0 if bias is None else BC[:, bias:bias + 1]
                                             ).then_inc(sem(stage + "_out"), 1)

                def slot(b):
                    return lambda u: b[:, u, :]

                silu("s1", slot(HA), EB + 0)
                silu("k1", lambda u: HBR[:, :, u, :], EB + 2, src=lambda v: v.rearrange("p (h w) -> p h w", h=H))
                silu("s2", slot(SELF), EB + 1)
                silu("k2", slot(K0T))
                silu("l1", lambda u: HAR[:, :, u, :], EB + 4, src=lambda v: v.rearrange("p (h w) -> p w h", h=H))
                silu("l2", slot(K1T))
                for m in range(2):
                    silu(f"m{m}a", slot(HA), MB + 2 * m)
                    silu(f"m{m}b", slot(T1), MB + 2 * m + 1, free=None if m == 0 else "res0")
                silu("oa", slot(HA), OB)
                silu("ob", slot(T1), OB + 1, free="res1")
                act.wait_ge(sem("t_mm"), g + 1)
                nc.scalar.activation(tt[:, :, :].rearrange("p s w -> p (s w)"), ps[:, 7, 0:GS * W], ACT.Identity,
                                     bias=BC[:, CB63:CB63 + 1]).then_inc(sem("t_out"), 1)

            with act.Fori(0, NHALF) as hf:
                for n in range(1, 2 * HS, 2):
                    s, k = n // 2, 4 * (n % 2)
                    act.wait_ge(sem("proj_mm"), hf * 2 * HS + n + 1)
                    src = unit(n % 4).rearrange("p (k m) -> p k m", k=4)
                    for bh in range(BH):
                        last = nc.scalar.activation(
                            BUF1.rearrange("p (g c k s) -> p g k c s", g=BH, c=C, k=WB)[:, bh, k:k + 4, :, s],
                            src[:, :, C * bh:C * (bh + 1)], ACT.Copy)
                    nc.scalar.activation(
                        gates[:, :, :].rearrange("p l (g k s) -> p k g l s", k=WB, g=BH)[:, k:k + 4, :, :, s],
                        src[:, :, P:P + 8].rearrange("p k (g l) -> p k g l", g=BH), ACT.Copy).then_inc(sem("proj_out_a"), 1)
                for l in range(LEVELS):
                    dst = (BUF2, BUF1, BUF2)[l]
                    for cu in range(NU):
                        n = l * NU + cu
                        act.wait_ge(sem("conv_mm"), hf * LEVELS * NU + n + 1)
                        if l == 2:
                            act.wait_ge(sem("gated"), hf * LEVELS * NU + cu + 1)
                        nc.scalar.activation(ctxv(dst)[:, :, UCH * cu:UCH * (cu + 1), :].rearrange("p g c n -> p c g n"),
                                             unit(n % 4).rearrange("p (c g n) -> p c g n", c=UCH, g=BH), ACT.Gelu
                                             ).then_inc(sem("conv_out"), 1)
                act.wait_ge(sem("glob_mm"), hf + 1)
                nc.scalar.activation(GLOB, unit(0), ACT.Gelu, scale=1.0 / TOK).then_inc(sem("glob_out"), 1)
                for n in range(HSL + TSTAGES - 1):
                    def at(stage, i, name):
                        act.wait_ge(sem(name), hf * HSL + i + 1)

                    i = n
                    if i < HSL:
                        at(0, i, "mb_mm")
                        nc.scalar.activation(MBT[i % 2].rearrange("p (h k q) -> p k q h", h=H, q=W4),
                                             ps[:, 0, :].rearrange("p (k q h) -> p k q h", k=4, h=H),
                                             ACT.Copy).then_inc(sem("mb_ready"), 1)
                    i = n - 1
                    if 0 <= i < HSL:
                        at(1, i, "q_mm")
                        if i >= 2:
                            act.wait_ge(sem("xo_ready"), hf * HSL + i - 1)
                        nc.scalar.activation(QT[i % 2], ps[:, 1, :], ACT.Identity,
                                             bias=BC[:, QB:QB + 1]).then_inc(sem("q_ready"), 1)
                    i = n - 2
                    if 0 <= i < HSL:
                        at(2, i, "xc_mm")
                        nc.scalar.activation(SQT[i % 2], ps[:, 3 + i % 2, :], ACT.Square).then_inc(sem("sqt_ready"), 1)
                    i = n - 3
                    if 0 <= i < HSL:
                        at(3, i, "var_mm")
                        if i >= 2:
                            act.wait_ge(sem("xn_ready"), hf * HSL + i - 1)
                        nc.scalar.activation(SD[i % 2], ps[:, 5, :], ACT.Sqrt, bias=BC[:, 22:23]).then_inc(sem("sd_ready"), 1)
                    i = n - 5
                    if 0 <= i < HSL:
                        at(5, i, "ot_mm")
                        if i >= 2:
                            act.wait_ge(sem(f"stored{i % 2}"), (hf * (HSL // 2) + i // 2) * 16 * BH)
                        nc.scalar.activation(OT[i % 2].rearrange("p (g t c) -> p t g c", g=BH, t=4),
                                             ps[:, 7, :].rearrange("p (t g c) -> p t g c", t=4, g=BH),
                                             ACT.Copy).then_inc(sem("ot_ready"), 1)
                for j in range(2):
                    act.wait_ge(sem(f"stored{j}"), (hf + 1) * (HSL // 2) * 16 * BH)

        @block.vector
        def _(dve):
            count = [0]

            def link(ins, chain="dve_chain", base=0):
                count[0] += 1
                ins.then_inc(sem(chain), 1)
                dve.wait_ge(sem(chain), base + count[0])

            def take_wait(column):
                nc.vector.memset(small[:, column:column + 1], 0.0)

            TS, TT, STT = nc.vector.tensor_scalar, nc.vector.tensor_tensor, nc.vector.scalar_tensor_tensor
            cp = nc.vector.tensor_copy
            nc.vector.memset(ones[:, :], 1.0).then_inc(sem("ones_set"), 1)
            nc.vector.memset(onesb[:, :], 1.0).then_inc(sem("ones_set"), 1)
            nc.vector.memset(BC[:, 22:23], EPS_LN).then_inc(sem("eps_set"), 1)
            link(nc.vector.memset(meanm[:, :], 0.0))
            link(nc.vector.memset(meanm[0:C, 0:C], 1.0 / C))
            nc.vector.memset(meanm[C:P, C:P], 1.0 / C).then_inc(sem("dve_chain"), 1)
            count[0] += 1
            dve.wait_ge(sem("ident_set"), 1)
            dve.wait_ge(sem("dve_chain"), count[0])
            TT(centm[:, :], ident[:, :], meanm[:, :], ALU.subtract).then_inc(sem("mats_set"), 1)
            link(nc.vector.tensor_reduce(xh[:, 0, 0:2, :].rearrange("p a b -> p (a b)"),
                                         ident[:, :].rearrange("p (g j) -> p g j", j=2), AX.X, ALU.add))
            TS(pairm[:, :].rearrange("p (g j) -> p g j", j=2),
               xh[:, 0, 0:2, :].rearrange("p a (b o) -> p (a b) o", o=1).to_broadcast([P, 64, 2]), 0.5, None, ALU.mult
               ).then_inc(sem("mats_set"), 1)
            link(nc.vector.tensor_reduce(xh[:, 1, 0, :], ident[:, :].rearrange("p (a h) -> p h a", a=W4), AX.X, ALU.add))
            cp(rowm[:, :].rearrange("p (a h) -> p a h", a=W4), xh[:, 1, 0:1, :].to_broadcast([P, W4, H])
               ).then_inc(sem("mats_set"), 1)
            dve.wait_ge(sem("row_loaded"), 16 * 8)
            link(nc.vector.memset(ROWB[:, :], 0.0))
            link(TS(ROWR, ROWF, 1.0 / 32, None, ALU.mult))
            link(cp(ROWB[0:32, :], ROWR[0:32, :]))
            link(cp(ROWH[:, 0, :], ROWR))
            link(TT(ROWR, ROWR, ROWH[:, 0, :], ALU.subtract))
            link(cp(ROWB[32:64, :], ROWR[32:64, :]))
            link(cp(ROWH[:, 1, :], ROWR))
            link(TT(ROWR, ROWR, ROWH[:, 1, :], ALU.subtract))
            cp(ROWB[64:96, :], ROWR[64:96, :]).then_inc(sem("rowb_set"), 1)
            dve.wait_ge(sem("w_loaded"), 16 * (2 * W4 + BH * 18))
            for bh in range(BH):
                p = slice(C * bh, C * (bh + 1))
                cp(CWN[p, :, p], CWR[p, :].rearrange("p (i t) -> p t i", t=3)).then_inc(sem("cwn_ready"), 1)
            dve.wait_ge(sem("pt_mm"), 1)
            cp(P1T.rearrange("p k m -> p (k m)"), unit(0)).then_inc(sem("pt_ready"), 1)
            TS(P3T.rearrange("p k m -> p (k m)"), unit(1), 0.1 / C, None, ALU.mult).then_inc(sem("pt_ready"), 1)
            scale = (H + W - 2) ** 0.5
            TS(WT[:, WC:WC + 3, :].rearrange("p t m -> p (t m)"), ps[:, 4, 0:3 * P], 1.0 / scale, None, ALU.mult
               ).then_inc(sem("pt_ready"), 1)
            TS(BC[:, CB63:CB63 + 1], BC[:, CB:CB + 1], (H + W - 1) / scale, None, ALU.mult).then_inc(sem("bc_ready"), 1)
            dve.wait_ge(sem("pb_mm"), 1)
            TT(BC[:, PB2:PB2 + 1], ps[:, 5, 0:1], BC[:, PB:PB + 1], ALU.add).then_inc(sem("bc_ready"), 1)
            TS(WT[:, WPI, :], WT[:, WPI, :], BC[:, LG:LG + 1], None, ALU.mult).then_inc(sem("bc_ready"), 1)

            swb = SWB.rearrange("p (b c) -> p b c", b=B)
            for ch in range(NCH):
                dve.wait_ge(sem(f"x_loaded{ch}"), 16 * W4)
                nc.vector.tensor_reduce(swb[:, XCH * ch:XCH * (ch + 1), :],
                                        XA[:, XCH * ch:XCH * (ch + 1), :, :].rearrange("p b k c -> p b c k"),
                                        AX.X, ALU.add).then_inc(sem("swb_ready"), 1)
            mean, msq, rstd = SQ[0][:, 0:1024], SQ[1][:, 1024:2048], SQ[1][:, 0:1024]
            var = SQ[0][:, 1024:2048]
            dve.wait_ge(sem("sum0_mm"), 1)
            pairs = ps[:, 4:8, :].rearrange("p a (g j) -> p (a g) j", j=2)
            link(nc.vector.tensor_reduce(mean, pairs, AX.X, ALU.add))
            pairs = ps[:, 0:4, :].rearrange("p a (g j) -> p (a g) j", j=2)
            link(nc.vector.tensor_reduce(var, pairs, AX.X, ALU.add))
            link(TS(mean, mean, 1.0 / (2 * TOK), None, ALU.mult))
            link(TT(msq, mean, mean, ALU.mult))
            link(STT(out=var, in0=var, scalar=1.0 / (2 * TOK), in1=msq, op0=ALU.mult, op1=ALU.subtract))
            TS(var, var, 0.0, EPS_GN, ALU.max, ALU.add).then_inc(sem("var0_ready"), 1)
            one = mean.rearrange("p (g o) -> p g o", o=1)
            link(cp(MEANE.rearrange("p (g j) -> p g j", j=2), one.to_broadcast([P, 1024, 2])))
            dve.wait_ge(sem("rstd0"), 1)
            one = rstd.rearrange("p (g o) -> p g o", o=1)
            link(cp(SWB.rearrange("p (g j) -> p g j", j=2), one.to_broadcast([P, 1024, 2])))
            dve.wait_ge(sem("band_stored"), 16 * (LEVELS - 1) * W4)
            dve.wait_ge(sem("rowb_set"), 1)
            for ch in range(NCH):
                b = slice(XCH * ch, XCH * (ch + 1))
                m_b = MEANE.rearrange("p (b o c) -> p b o c", b=B, o=1)[:, b].to_broadcast([P, XCH, WB, C])
                r_b = SWB.rearrange("p (b o c) -> p b o c", b=B, o=1)[:, b].to_broadcast([P, XCH, WB, C])
                a = A(XCH * ch, XCH)
                link(TT(a, XA[:, b], m_b, ALU.subtract))
                link(TT(a, a, r_b, ALU.mult))
                nc.vector.tensor_reduce(SUMA[:, b, :], a, AX.X, ALU.add).then_inc(sem("a_ready"), 1)
            dve.wait_ge(sem("relu_sq"), 16)
            link(nc.vector.tensor_reduce(small[:, 0:2], xs[:, 0:2, 0:16], AX.X, ALU.add))
            nc.vector.tensor_copy(small[:, 8:10], small[:, 0:2]).then_inc(sem("bnsum_ready"), 1)
            dve.wait_ge(sem("bn_mm"), 1)
            nbn = B * W * C
            link(TS(small[:, 0:2], ps[:, 0, 0:2], 1.0 / nbn, None, ALU.mult))
            link(TT(small[:, 2:3], small[:, 0:1], small[:, 0:1], ALU.mult))
            link(TT(small[:, 3:4], small[:, 1:2], small[:, 2:3], ALU.subtract))
            TS(small[:, 3:4], small[:, 3:4], 0.0, EPS_BN, ALU.max, ALU.add).then_inc(sem("bnvar_ready"), 1)
            dve.wait_ge(sem("bnrstd"), 1)
            link(TT(small[:, 5:6], small[:, 4:5], BC[:, BG:BG + 1], ALU.mult))
            link(TT(small[:, 7:8], small[:, 5:6], small[:, 0:1], ALU.mult))
            TT(small[:, 6:7], BC[:, BB:BB + 1], small[:, 7:8], ALU.subtract).then_inc(sem("bn_coef"), 1)
            for i in range(16):
                dve.wait_ge(sem("bn_applied"), i + 1)
                v = AF[:, 1024 * i:1024 * (i + 1)].rearrange("p (k g c) -> p k g c", k=WB, g=BH)
                TT(v, v, XA.rearrange("p (g s) k c -> p s k g c", g=BH)[:, i], ALU.add).then_inc(sem("x1_ready"), 1)
            for s in range(0, NS, 2):
                dve.wait_ge(sem("xt_mm"), s + 1)
                cp(XBS[:, s, :].rearrange("p (h a k) -> p k a h", h=H, a=W4),
                   unit(s % 4).rearrange("p (k a h) -> p k a h", k=WB, a=W4)).then_inc(sem("xt_out_d"), 1)
            dve.wait_ge(sem("xt_out_a"), NS // 2)

            def group_norm(base, ns, first, lk, stats, coef, pool_sem, ready, coef_n, dst, order=lambda v: v):
                take_wait(30)
                for s in range(ns):
                    for j in range(2):
                        nc.vector.bn_stats(st[:, s, 6 * j:6 * j + 6],
                                           XBS[:, bass.ds(first + s, 1), HALF * j:HALF * (j + 1)].rearrange("p o n -> p (o n)")
                                           ).then_inc(sem("bn_stats"), 1)
                nstat[0] += 2 * ns
                dve.wait_ge(sem("bn_stats"), stat_base() + nstat[0])
                take_wait(31)
                for s in range(ns):
                    ins = nc.vector.bn_aggr(mv[:, s, :], st[:, s, :])
                lk(ins)
                lk(cp(me[:, 0, 0:ns], mv[:, 0:ns, 0]))
                lk(TT(me[:, 1, 0:ns], me[:, 0, 0:ns], me[:, 0, 0:ns], ALU.mult))
                TT(me[:, 1, 0:ns], me[:, 1, 0:ns], mv[:, 0:ns, 1], ALU.add).then_inc(sem(stats), 1)
                dve.wait_ge(sem(coef), coef_n)
                v = ps[:, 0, 0:2 * HS].rearrange("p (a s) -> p a s", a=2)
                lk(cp(gm[:, 0:2, 0:ns], v[:, :, 0:ns]))
                lk(TT(gm[:, 2, 0:ns], gm[:, 0, 0:ns], gm[:, 0, 0:ns], ALU.mult))
                lk(TT(gm[:, 1, 0:ns], gm[:, 1, 0:ns], gm[:, 2, 0:ns], ALU.subtract))
                TS(gm[:, 2, 0:ns], gm[:, 1, 0:ns], 0.0, EPS_GN, ALU.max, ALU.add).then_inc(sem(pool_sem[0]), 1)
                dve.wait_ge(sem(pool_sem[1]), coef_n)
                for s in range(ns):
                    apply_norm(s, first, dst, ready, order)

            def apply_norm(s, first, dst, ready, order=lambda v: v):
                TS(dst(s), order(XBS[:, bass.ds(first + s, 1), :].rearrange("p o n -> p (o n)")), gm[:, 0, s:s + 1],
                   gm[:, 3, s:s + 1], ALU.subtract, ALU.mult).then_inc(sem(ready), 1)

            CHAIN_B = 30
            STATS_B = 4 * GS
            with dve.Fori(0, NG) as g:
                count[0] = 0
                nstat = [0]

                def stat_base():
                    return g * STATS_B

                def lk(ins):
                    link(ins, "chain_b", g * CHAIN_B)

                first = g * GS
                group_norm(0, GS, first, lk, "stats_ready", "coef_mm", ("gnvar", "gnrstd"), "g_ready",
                           2 * g + 1, lambda s: G[:, s, :])
                for u in range(GS):
                    dve.wait_ge(sem("ein_mm"), GS * g + u + 1)
                    e1 = E1.rearrange("p s n -> p (s n)").rearrange("p (j q) -> p q j", j=W)
                    cp(e1[:, 32 * u:32 * (u + 1), :], unit(u).rearrange("p (q j) -> p q j", j=W)
                       ).then_inc(sem("ein_out"), 1)
                for u in range(GS):
                    dve.wait_ge(sem("tr_mm"), GS * g + u + 1)
                    m = M.rearrange("p s (i j) -> p j s i", i=H)
                    cp(m[:, 8 * u:8 * (u + 1), :, :], unit(u).rearrange("p (j s i) -> p j s i", j=8, s=GS)
                       ).then_inc(sem("tr_out"), 1)
                for m in range(2):
                    for u in range(GS):
                        dve.wait_ge(sem(f"m{m}b_out"), GS * g + u + 1)
                        ins = TT(M[:, u, :], M[:, u, :], T1[:, u, :], ALU.add)
                        ins.then_inc(sem(f"res{m}"), 1)
                for u in range(GS):
                    dve.wait_ge(sem("res1"), GS * g + u + 1)
                    TT(M[:, u, :], M[:, u, :], SELF[:, u, :], ALU.mult).then_inc(sem("z1_ready"), 1)
                for u in range(GS):
                    xg = XBS[:, bass.ds(first + u, 1), :].rearrange("p o n -> p (o n)")
                    dve.wait_ge(sem("ob_out"), GS * g + u + 1)
                    lk(TT(M[:, u, :], M[:, u, :], T1[:, u, :], ALU.add))
                    lk(TT(xg, xg, M[:, u, :], ALU.add))
                group_norm(1, GS, first, lk, "stats_ready", "coef_mm", ("gnvar", "gnrstd"), "g3_ready",
                           2 * g + 2, lambda s: G[:, s, :])
                dve.wait_ge(sem("g3_ready"), GS * g + GS)
                g4 = G.rearrange("p s (h w) -> p s h w", h=H)
                for u in range(GS):
                    nc.vector.tensor_reduce(xh[:, 1, u, :], g4[:, u].rearrange("p h w -> p w h"), AX.X, ALU.add)
                    ins = nc.vector.tensor_reduce(xs[:, u, :], g4[:, u], AX.X, ALU.add)
                lk(ins)
                TT(xh[:, 0], xh[:, 1], g4[:, :, H - 1, :], ALU.subtract).then_inc(sem("xh_ready"), 1)
                TT(xh[:, 2], xh[:, 1], g4[:, :, 0, :], ALU.subtract).then_inc(sem("xh_ready"), 1)
                for u in range(GS):
                    TT(HA[:, u, :].rearrange("p (h w) -> p h w", h=H),
                       xs[:, u, :].rearrange("p (h o) -> p h o", o=1).to_broadcast([P, H, W]), g4[:, u], ALU.subtract
                       ).then_inc(sem("z_ready"), 1)
                dve.wait_ge(sem("t_out"), g + 1)
                dve.wait_ge(sem("xh_ready"), 2 * g + 2)
                for u in range(GS):
                    ins = TT(g4[:, u], g4[:, u], tt[:, u:u + 1, :].to_broadcast([P, H, W]), ALU.add)
                lk(ins)
                for u in range(GS):
                    xg = XBS[:, bass.ds(first + u, 1), :].rearrange("p o n -> p (o n)")
                    dve.wait_ge(sem("y_mm"), GS * g + u + 1)
                    lk(TT(G[:, u, :], unit(u), G[:, u, :], ALU.add))
                    count[0] += 1
                    STT(out=xg, in0=G[:, u, :], scalar=0.0, in1=xg, op0=ALU.max, op1=ALU.add).then_inc(sem("chain_b"), 1)
                dve.wait_ge(sem("chain_b"), g * CHAIN_B + count[0])
                assert count[0] == CHAIN_B, count[0]

            CHAIN_C = 38
            with dve.Fori(0, NHALF) as hf:
                count[0] = 0
                nstat = [0]

                def stat_base():
                    return NG * STATS_B + hf * 2 * HS

                def lk(ins):
                    link(ins, "chain_c", hf * CHAIN_C)

                first = hf * HS
                group_norm(2, HS, first, lk, "stats3_ready", "coef3_mm", ("gnvar3", "gnrstd3"), "g4_ready",
                           hf + 1, lambda s: BUF2[:, 1024 * s:1024 * (s + 1)].rearrange("p (k q h) -> p h k q", k=WB, h=H),
                           lambda v: v.rearrange("p (h k q) -> p h k q", h=H, k=WB))
                for n in range(0, 2 * HS, 2):
                    s, k = n // 2, 4 * (n % 2)
                    dve.wait_ge(sem("proj_mm"), hf * 2 * HS + n + 1)
                    src = unit(n % 4).rearrange("p (k m) -> p k m", k=4)
                    for bh in range(BH):
                        cp(BUF1.rearrange("p (g c k s) -> p g k c s", g=BH, c=C, k=WB)[:, bh, k:k + 4, :, s],
                           src[:, :, C * bh:C * (bh + 1)])
                    cp(gates[:, :, :].rearrange("p l (g k s) -> p k g l s", k=WB, g=BH)[:, k:k + 4, :, :, s],
                       src[:, :, P:P + 8].rearrange("p k (g l) -> p k g l", g=BH)).then_inc(sem("proj_out_d"), 1)
                dve.wait_ge(sem("proj_out_a"), hf * HS + HS)
                dve.wait_ge(sem("proj_out_d"), hf * HS + HS)
                for l in range(LEVELS):
                    src = (BUF2, BUF1, BUF2)[l]
                    gate = gates[:, l, :].rearrange("p (g o n) -> p g o n", g=BH, o=1).to_broadcast([P, BH, UCH, COLS // BH])
                    for cu in range(NU):
                        n = l * NU + cu
                        dve.wait_ge(sem("conv_out"), hf * LEVELS * NU + n + 1)
                        v = ctxv(src)[:, :, UCH * cu:UCH * (cu + 1), :]
                        a = ctxv(ALL)[:, :, UCH * cu:UCH * (cu + 1), :]
                        t = TMP[:, :].rearrange("p (g c n) -> p g c n", g=BH, c=UCH)
                        if l == 0:
                            TT(a, v, gate, ALU.mult).then_inc(sem("gated"), 1)
                        else:
                            TT(t, v, gate, ALU.mult).then_inc(sem("tmp_ready"), 1)
                            dve.wait_ge(sem("tmp_ready"), (hf * 2 + l - 1) * NU + cu + 1)
                            TT(a, a, t, ALU.add).then_inc(sem("gated"), 1)
                            dve.wait_ge(sem("gated"), hf * LEVELS * NU + n + 1)
                        if l == LEVELS - 1:
                            if cu == 0:
                                dve.wait_ge(sem("conv_mm"), hf * LEVELS * NU + LEVELS * NU)
                            for bh in range(BH):
                                nc.vector.tensor_reduce(
                                    RSUM.rearrange("p (g c s) -> p g c s", g=BH, c=C)[:, bh, UCH * cu:UCH * (cu + 1), :],
                                    v[:, bh].rearrange("p c (k s) -> p c s k", s=HS), AX.X, ALU.add
                                    ).then_inc(sem("rsum_ready"), 1)
                dve.wait_ge(sem("glob_out"), hf + 1)
                for bh in range(BH):
                    for cu in range(NU):
                        a = ctxv(ALL)[:, bh, UCH * cu:UCH * (cu + 1), :].rearrange("p c (k s) -> p c k s", s=HS)
                        t = TMP[:, HALF * (cu % 2):HALF * (cu % 2 + 1)].rearrange("p (c k s) -> p c k s", c=UCH, s=HS)
                        gl = GLOB.rearrange("p (g c o s) -> p g c o s", g=BH, c=C, o=1)[:, bh, UCH * cu:UCH * (cu + 1)]
                        gt = gates[:, 3:4, 64 * bh:64 * (bh + 1)].rearrange("p o (k s) -> p o k s", s=HS)
                        lk(TT(t, gl.to_broadcast([P, UCH, WB, HS]), gt.to_broadcast([P, UCH, WB, HS]), ALU.mult))
                        lk(TT(a, a, t, ALU.add))
                for s in range(HS):
                    apply_norm(s, first, lambda s: BUF1[:, 1024 * s:1024 * (s + 1)], "g4b_ready")
                for n in range(HSL + TSTAGES - 1):
                    i = n - 1
                    if 0 <= i < HSL:
                        dve.wait_ge(sem("q_ready"), hf * HSL + i + 1)
                        dve.wait_ge(sem("mod_mm"), hf * HSL + i + 1)
                        STT(out=XO[i % 2], in0=ps[:, 2, :], scalar=BC[:, HB:HB + 1], in1=QT[i % 2],
                            op0=ALU.add, op1=ALU.mult).then_inc(sem("xo_ready"), 1)
                    i = n - 3
                    if 0 <= i < HSL:
                        dve.wait_ge(sem("sd_ready"), hf * HSL + i + 1)
                        nc.vector.reciprocal(SD[i % 2], SD[i % 2]).then_inc(sem("rs_ready"), 1)
                        dve.wait_ge(sem("rs_ready"), hf * HSL + i + 1)
                        TT(XN[i % 2], ps[:, 3 + i % 2, :], SD[i % 2], ALU.mult).then_inc(sem("xn_ready"), 1)
                    i = n - 4
                    if 0 <= i < HSL:
                        s, hh = i // 2, i % 2
                        dve.wait_ge(sem("y_mm2"), hf * HSL + i + 1)
                        xg = XBS[:, bass.ds(first + s, 1), :].rearrange("p o (h a w) -> p (o h) a w", h=H, a=2)[:, :, hh, :]
                        STT(out=YT[i % 2].rearrange("p (h w) -> p h w", h=H),
                            in0=ps[:, 6, :].rearrange("p (h w) -> p h w", h=H), scalar=BC[:, PB2:PB2 + 1],
                            in1=xg, op0=ALU.add, op1=ALU.add).then_inc(sem("yt_ready"), 1)
                for j in range(2):
                    dve.wait_ge(sem(f"stored{j}"), (hf + 1) * (HSL // 2) * 16 * BH)
                assert count[0] == CHAIN_C, count[0]

        @block.tensor
        def _(pe):
            def mm(out, lhsT, rhs, start=True, stop=True):
                return nc.tensor.matmul(out, lhsT, rhs, start=start, stop=stop)

            pe.wait_ge(sem("ident_set"), 1)
            pe.wait_ge(sem("p_loaded"), 16 * 2 * W4)
            pe.wait_ge(sem("w_loaded"), 16 * (2 * W4 + BH * 18))
            pe.wait_ge(sem("cwn_ready"), BH)
            for k in range(WB):
                nc.tensor.transpose(unit(0)[:, P * k:P * (k + 1)], P1N[:, k, :], ident[:, :])
                nc.tensor.transpose(unit(1)[:, P * k:P * (k + 1)], P3N[:, k, :], ident[:, :])
            for t in range(3):
                last = nc.tensor.transpose(ps[:, 4, P * t:P * (t + 1)], CWN[:, t, :], ident[:, :])
            last.then_inc(sem("pt_mm"), 1)
            mm(ps[:, 5, 0:1], WT[:, WPI, :], BC[:, LB:LB + 1]).then_inc(sem("pb_mm"), 1)
            pe.wait_ge(sem("pt_ready"), 3)
            pe.wait_ge(sem("bc_ready"), 3)
            pe.wait_ge(sem("ones_set"), 2)
            for ch in range(NCH):
                pe.wait_ge(sem("sq_ready"), ch + 1)
                q = SQ[ch % 2].rearrange("p (b k c) -> p b k c", b=XCH, k=WB)
                for k in range(WB):
                    last = mm(ps[:, ch // 2, 256 * (ch % 2):256 * (ch % 2 + 1)], ones[:, :], q[:, :, k, :],
                              start=k == 0, stop=k == WB - 1)
                last.then_inc(sem("sq_used"), 1)
            pe.wait_ge(sem("swb_ready"), NCH)
            for i in range(4):
                last = mm(ps[:, 4 + i, :], ones[:, :], SWB[:, HALF * i:HALF * (i + 1)])
            last.then_inc(sem("sum0_mm"), 1)
            pe.wait_ge(sem("mats_set"), 3)
            for n in range(16):
                b8, k = n // 4, 2 * (n % 4)
                b = slice(NB8 * b8, NB8 * (b8 + 1))
                pe.wait_ge(sem("a_ready"), 2 * (b8 + 1))
                if n >= 4:
                    pe.wait_ge(sem("relu_sq"), n - 3)
                for j in range(2):
                    o = ps[:, 2 * (n % 4) + j, :]
                    mm(o, P1T[:, k + j, :], A(NB8 * b8, NB8, k + j), True, False)
                    last = mm(o, P3T[:, k + j, :],
                              SUMA[:, b, k + j:k + j + 1].to_broadcast([P, NB8, C]), False, True)
                last.then_inc(sem("relu_mm"), 1)
            pe.wait_ge(sem("bnsum_ready"), 1)
            pe.wait_ge(sem("relu_sq"), 16)
            mm(ps[:, 0, 0:2], rowm[:, :], small[:, 8:10]).then_inc(sem("bn_mm"), 1)
            pe.wait_ge(sem("x1_ready"), 16)
            for s in range(NS):
                if s >= 4:
                    pe.wait_ge(sem("xt_out_d" if s % 2 == 0 else "xt_out_a"), (s - 4) // 2 + 1)
                for k in range(WB):
                    last = nc.tensor.transpose(unit(s % 4)[:, P * k:P * (k + 1)], AF[:, 1024 * s + P * k:1024 * s + P * (k + 1)], ident[:, :])
                last.then_inc(sem("xt_mm"), 1)
            pe.wait_ge(sem("xt_out_a"), NS // 2)
            pe.wait_ge(sem("xt_out_d"), NS // 2)
            pe.wait_ge(sem("rowb_set"), 1)

            with pe.Fori(0, NG) as g:
                def coef(n):
                    pe.wait_ge(sem("stats_ready"), 2 * g + n + 1)
                    v = ps[:, 0, 0:2 * HS].rearrange("p (a s) -> p a s", a=2)[:, :, 0:GS]
                    mm(v, pairm[:, :], me[:, :, 0:GS]).then_inc(sem("coef_mm"), 1)

                def dense(stage, w, src, waits):
                    for u in range(GS):
                        for name, all_slots in waits:
                            pe.wait_ge(sem(name), GS * g + (GS if all_slots else u + 1))
                        for j in range(2):
                            last = mm(ps[:, 2 * u + j, :], WT[:, w, :], src[:, u, HALF * j:HALF * (j + 1)])
                        last.then_inc(sem(stage + "_mm"), 1)

                def dense_t(stage, w, row, src, waits):
                    for u in range(GS):
                        for name, all_slots in waits:
                            pe.wait_ge(sem(name), GS * g + (GS if all_slots else u + 1))
                        for j in range(2):
                            mm(ps[:, 2 * u + j, :].rearrange("p (k m) -> p k m", k=4), onesb[:, :],
                               ROWB[:, row:row + P].rearrange("p (o m) -> p o m", o=1).to_broadcast([P, 4, P]), True, False)
                            for k in range(4):
                                last = mm(ps[:, 2 * u + j, P * k:P * (k + 1)], src(8 * u + 4 * j + k), WT[:, w, :],
                                          False, k == 3)
                        last.then_inc(sem(stage + "_mm"), 1)

                coef(0)
                dense("s1", WE + 0, G, [("g_ready", False)])
                dense("k1", WE + 2, G, [("s1_out", False)])
                dense("s2", WE + 1, HA, [("k1_out", False)])
                dense_t("k2", WE + 3, 0, lambda i: HBR[:, i].rearrange("p s w -> p (s w)"), [("s2_out", False), ("k1_out", True)])
                dense("l1", WE + 4, G, [("k2_out", False)])
                dense_t("l2", WE + 5, P, lambda i: HAR[:, i].rearrange("p s h -> p (s h)"), [("l1_out", False), ("l1_out", True)])
                k0 = K0T.rearrange("p s n -> p (s n)").rearrange("p (i q) -> p i q", i=H)
                k1 = K1T.rearrange("p s n -> p (s n)").rearrange("p (j q) -> p j q", j=W)
                for u in range(GS):
                    pe.wait_ge(sem("mats_set"), 3)
                    pe.wait_ge(sem("l2_out"), GS * g + GS)
                    for q in range(32):
                        for s in range(GS):
                            p = slice(32 * s, 32 * (s + 1))
                            last = mm(ps[p, 2 * u + q // 16, 32 * (q % 16):32 * (q % 16 + 1)],
                                      k0[p, :, 32 * u + q], k1[p, :, 32 * u + q])
                    last.then_inc(sem("ein_mm"), 1)
                e1 = E1.rearrange("p s n -> p (s n)").rearrange("p (j q) -> p j q", j=W)
                for u in range(GS):
                    pe.wait_ge(sem("ein_out"), GS * g + GS)
                    for k in range(8):
                        last = nc.tensor.transpose(unit(u)[:, P * k:P * (k + 1)], e1[:, 8 * u + k, :], ident[:, :])
                    last.then_inc(sem("tr_mm"), 1)
                dense("m0a", WM + 0, M, [("tr_out", True)])
                dense("m0b", WM + 1, HA, [("m0a_out", False)])
                dense("m1a", WM + 2, M, [("m0b_out", False), ("res0", False)])
                dense("m1b", WM + 3, HA, [("m1a_out", False)])
                dense("oa", WO + 0, M, [("m1b_out", False), ("z1_ready", False)])
                dense("ob", WO + 1, HA, [("oa_out", False)])
                pe.wait_ge(sem("ob_out"), GS * g + GS)
                coef(1)
                pe.wait_ge(sem("xh_ready"), 2 * g + 2)
                for t in range(3):
                    last = mm(ps[:, 7, 0:GS * W], WT[:, WC + t, :], xh[:, t, :, :].rearrange("p s w -> p (s w)"),
                              t == 0, t == 2)
                last.then_inc(sem("t_mm"), 1)
                z = HA.rearrange("p s (h w) -> p s h w", h=H)
                for u in range(GS):
                    pe.wait_ge(sem("z_ready"), GS * g + u + 1)
                    if u == GS - 1:
                        pe.wait_ge(sem("t_out"), g + 1)
                    for j in range(2):
                        h0, h1 = 16 * j, 16 * (j + 1)
                        for n, t in enumerate((1, 0, 2)):
                            lo, hi = max(h0, 1 - t), min(h1, H + 1 - t)
                            last = mm(ps[:, 2 * u + j, W * (lo - h0):W * (hi - h0)], WT[:, WC + t, :],
                                      z[:, u, lo + t - 1:hi + t - 1, :].rearrange("p h w -> p (h w)"), n == 0, n == 2)
                    last.then_inc(sem("y_mm"), 1)

            with pe.Fori(0, NHALF) as hf:
                pe.wait_ge(sem("stats3_ready"), hf + 1)
                v = ps[:, 0, 0:2 * HS].rearrange("p (a s) -> p a s", a=2)
                mm(v, pairm[:, :], me[:, :, :]).then_inc(sem("coef3_mm"), 1)
                g4 = BUF2.rearrange("p (s k n) -> p s k n", s=HS, k=WB)
                for n in range(2 * HS):
                    s, k0_ = n // 2, 4 * (n % 2)
                    pe.wait_ge(sem("g4_ready"), hf * HS + s + 1)
                    if n >= 4:
                        pe.wait_ge(sem("proj_out_d" if n % 2 == 0 else "proj_out_a"), hf * HS + (n - 4) // 2 + 1)
                    for j in range(2):
                        o = ps[:, 2 * (n % 4) + j, :].rearrange("p (k m) -> p k m", k=2)[:, :, 0:P + 8]
                        mm(o, onesb[:, :], ROWB[:, 2 * P:3 * P + 8].rearrange("p (o m) -> p o m", o=1
                                                                             ).to_broadcast([P, 2, P + 8]), True, False)
                        for i in range(2):
                            last = mm(o[:, i, :], g4[:, s, k0_ + 2 * j + i], WCG[:, :], False, i == 1)
                    last.then_inc(sem("proj_mm"), 1)
                pe.wait_ge(sem("proj_out_d"), hf * HS + HS)
                pe.wait_ge(sem("proj_out_a"), hf * HS + HS)
                for l in range(LEVELS):
                    src = ctxv((BUF1, BUF2, BUF1)[l])
                    for cu in range(NU):
                        n = l * NU + cu
                        if n >= 4:
                            pe.wait_ge(sem("conv_out"), hf * LEVELS * NU + n - 3)
                        if l >= 1:
                            pe.wait_ge(sem("conv_out"), hf * LEVELS * NU + n - NU + 1)
                        pe.wait_ge(sem(f"ring_loaded{n % RING}"),
                                   16 * NJ * (hf * (LEVELS * NU // RING) + n // RING + 1))
                        band = RG[:, n % RING, :].rearrange("p (j m c) -> p j m c", j=NJ // W4, c=UCH)
                        for c in range(UCH):
                            o = ps[:, 2 * (n % 4) + c // 4, COLS * (c % 4):COLS * (c % 4 + 1)
                                   ].rearrange("p (g n) -> p g n", g=BH)
                            v = src[:, :, UCH * cu + c, :]
                            mm(o, band[:, 1, :, c], v, True, False)
                            mm(o[:, :, 0:HS * (WB - 1)], band[:, 0, :, c], v[:, :, HS:], False, False)
                            last = mm(o[:, :, HS:], band[:, 2, :, c], v[:, :, 0:HS * (WB - 1)], False, True)
                        last.then_inc(sem("conv_mm"), 1)
                pe.wait_ge(sem("rsum_ready"), (hf + 1) * BH * NU)
                pe.wait_ge(sem("conv_out"), hf * LEVELS * NU + LEVELS * NU)
                for j in range(2):
                    last = mm(ps[:, j, :], ones[:, :], RSUM[:, HALF * j:HALF * (j + 1)])
                last.then_inc(sem("glob_mm"), 1)
                pe.wait_ge(sem("glob_out"), hf + 1)
                al = ALL.rearrange("p (m k s) -> p s k m", k=WB, s=HS)
                g4 = BUF1.rearrange("p (s h a w) -> p s a h w", s=HS, h=H, a=2)
                for n in range(HSL + TSTAGES - 1):
                    i = n - 5
                    if 0 <= i < HSL:
                        pe.wait_ge(sem("yt_ready"), hf * HSL + i + 1)
                        if i >= 1:
                            pe.wait_ge(sem("ot_ready"), hf * HSL + i)
                        y = YT[i % 2].rearrange("p (n t) -> p t n", t=4)
                        for t in range(4):
                            last = nc.tensor.transpose(ps[:, 7, P * t:P * (t + 1)], y[:, t, :], ident[:, :])
                        last.then_inc(sem("ot_mm"), 1)
                    i = n - 4
                    if 0 <= i < HSL:
                        pe.wait_ge(sem("xn_ready"), hf * HSL + i + 1)
                        if i >= 1:
                            pe.wait_ge(sem("yt_ready"), hf * HSL + i)
                        mm(ps[:, 6, :], WT[:, WPI, :], XN[i % 2]).then_inc(sem("y_mm2"), 1)
                    i = n - 3
                    if 0 <= i < HSL:
                        pe.wait_ge(sem("sqt_ready"), hf * HSL + i + 1)
                        if i >= 1:
                            pe.wait_ge(sem("sd_ready"), hf * HSL + i)
                        mm(ps[:, 5, :], meanm[:, :], SQT[i % 2]).then_inc(sem("var_mm"), 1)
                    i = n - 2
                    if 0 <= i < HSL:
                        pe.wait_ge(sem("xo_ready"), hf * HSL + i + 1)
                        if i >= 2:
                            pe.wait_ge(sem("xn_ready"), hf * HSL + i - 1)
                        mm(ps[:, 3 + i % 2, :], centm[:, :], XO[i % 2]).then_inc(sem("xc_mm"), 1)
                    i = n - 1
                    if 0 <= i < HSL:
                        s, hh = i // 2, i % 2
                        pe.wait_ge(sem("g4b_ready"), hf * HS + s + 1)
                        if i >= 1:
                            pe.wait_ge(sem("q_ready"), hf * HSL + i)
                        mm(ps[:, 1, :], WT[:, WQ, :], g4[:, s, hh]).then_inc(sem("q_mm"), 1)
                        pe.wait_ge(sem("mb_ready"), hf * HSL + i + 1)
                        if i >= 1:
                            pe.wait_ge(sem("xo_ready"), hf * HSL + i)
                        mm(ps[:, 2, :], WT[:, WHI, :], MBT[i % 2]).then_inc(sem("mod_mm"), 1)
                    i = n
                    if i < HSL:
                        s, hh = i // 2, i % 2
                        if i == 0:
                            pe.wait_ge(sem("g4b_ready"), hf * HS + 1)
                        if i >= 1:
                            pe.wait_ge(sem("mb_ready"), hf * HSL + i)
                        for k in range(4):
                            last = nc.tensor.transpose(ps[:, 0, P * k:P * (k + 1)], al[:, s, 4 * hh + k], ident[:, :])
                        last.then_inc(sem("mb_mm"), 1)
                pe.wait_ge(sem("ot_ready"), hf * HSL + HSL)


_INS = ['x', 'L0_conv_P1', 'L0_conv_P3', 'L0_conv_gamma', 'L0_conv_beta', 'L1_conv_emb_W', 'L1_conv_emb_b',
        'L1_conv_mult_W', 'L1_conv_mult_b', 'L1_conv_out_W', 'L1_conv_out_b', 'L2_conv_W', 'L2_conv_b',
        'L3_conv_Wf', 'L3_conv_bf', 'L3_conv_k0', 'L3_conv_k1', 'L3_conv_k2', 'L3_conv_Wh', 'L3_conv_bh',
        'L3_conv_gamma', 'L3_conv_beta', 'L3_conv_Wp', 'L3_conv_bp']
_OUTS = [((32, 32, 32, 64), 'float32')]


def kernel(**inputs):
    import numpy as _np
    import concourse.bacc as _bacc
    from concourse import mybir as _mybir
    from concourse.bass_utils import run_bass_kernel_spmd as _run

    nc = _bacc.Bacc("TRN2", target_bir_lowering=False, num_devices=1)
    arrays, args = {}, []
    for name in _INS:
        a = _np.ascontiguousarray(inputs[name])
        arrays[f"in_{name}_dram"] = a
        args.append(nc.dram_tensor(f"in_{name}_dram", a.shape, _mybir.dt.from_np(a.dtype), kind="ExternalInput").ap())
    for i, (shape, dtype) in enumerate(_OUTS):
        dt = _mybir.dt.from_np(_np.dtype(dtype))
        args.append(nc.dram_tensor(f"out_{i}_dram", shape, dt, kind="ExternalOutput").ap())
    conv_preact_kernel(nc, *args)
    r = _run(nc, [arrays], core_ids=[0])
    return r.results[0]["out_0_dram"]
```

```python
from contextlib import ExitStack

import concourse.bass as bass
from concourse import mybir

P = 128
F32 = mybir.dt.float32
BF16 = mybir.dt.bfloat16
ALU = mybir.AluOpType
ACT = mybir.ActivationFunctionType
AX = mybir.AxisListType

B, H, W, C = 32, 32, 32, 64
BH = 2
NS = B // BH
TOK = H * W
W4 = P // H
WB = W // W4
HALF = 512
EPS_GN = 1e-5
EPS_BN = 1e-5
EPS_LN = 1e-3

XCH = 4
NCH = B // XCH
NB8 = 8
GS = 4
NG = NS // GS
HS = 8
NHALF = NS // HS
COLS = WB * B
LEVELS = 3
KERNELS = (3, 5, 7)
UCH = 8
RING = 2
NU = C // UCH
NJ = 3 * W4
UH = 2 * H - 1
WIN = H * UCH
BAND = NJ * UH * UCH
QP = 32
SUB = UCH * COLS // 1024
NSTEP = LEVELS * NU
NHS = 2 * NS
STAGES = 5
PEELED = 6


def conv_steps(engine, step):
    step(0, 0, 0, 0, 0, None, None)
    step(1, 0, 1, 0, 1, 0, None)
    step(0, 1, 2, 1, 0, None, 0)
    with engine.Fori(0, (NU - 2) // 2) as it:
        for j in range(2 * LEVELS):
            l = 2 - j % LEVELS
            n = 6 * it + (3 + j)
            step(l, 2 * it + (2 + j // LEVELS - l), n, 3 * it + (3 + j) // 2, (3 + j) % 2, n - 2, n - 3)
    n = NSTEP - 3
    step(2, NU - 2, n, n // 2, n % 2, n - 2, n - 3)
    step(1, NU - 1, n + 1, (n + 1) // 2, (n + 1) % 2, n - 1, n - 2)
    step(2, NU - 1, n + 2, (n + 2) // 2, n % 2, n + 1, n)


def half_slots(engine, step):
    def known(n):
        return lambda d: ((n - d) // 2, (n - d) % 2, n - d) if 0 <= n - d < NHS else None

    def looped(it, m):
        return lambda d: (it + (m - d) // 2, (m - d) % 2, 2)

    for n in range(PEELED):
        step(known(n))
    with engine.Fori(0, (NHS - PEELED) // 2) as it:
        for j in range(2):
            step(looped(it, PEELED + j))
    for n in range(NHS, NHS + STAGES - 1):
        step(known(n))


def conv_preact_kernel(nc, x, P1, P3, bn_gamma, bn_beta, emb_W, emb_b, mult_W, mult_b, out_W, out_b,
                       cW, cb, Wf, bf, k0, k1, k2, Wh, bh_, ln_gamma, ln_beta, Wp, bp, out):
    band_dram = nc.dram_tensor("band_tables", (LEVELS, NU, W4, BAND), F32, kind="Internal")

    ctx = ExitStack()
    with ctx:
        def sb(name, shape, dt=F32):
            return ctx.enter_context(nc.sbuf_tensor(name, shape, dt))

        named = {}

        def sem(name):
            if name not in named:
                named[name] = ctx.enter_context(nc.semaphore(name))
            return named[name]

        XB = sb("XB", [P, NS * TOK])
        WK = sb("WK", [P, 24 * TOK])
        RG = sb("RG", [P, RING, NJ * WIN])
        WT = sb("WT", [P, 18, P])
        WCG = sb("WCG", [P, P + 8])
        ROWB = sb("ROWB", [P, 2 * P + P + 8], BF16)
        ident = sb("ident", [P, P])
        ones = sb("ones", [P, P])
        onesb = sb("onesb", [P, P], BF16)
        pairm = sb("pairm", [P, P])
        rowm = sb("rowm", [P, P])
        meanm = sb("meanm", [P, P])
        centm = sb("centm", [P, P])
        small = sb("small", [P, 32])
        BC = sb("BC", [P, 24])
        st = sb("st", [P, HS, 12])
        mv = sb("mv", [P, HS, 2])
        me = sb("me", [P, 2, HS])
        gm = sb("gm", [P, 4, HS])
        TMP = sb("TMP", [P, HALF])
        gm3 = sb("gm3", [P, 2, NS])
        sd = sb("sd", [P, 2, 8])
        rs = sb("rs", [P, 2, 8])
        gates = sb("gates", [P, 4, COLS])
        xs = sb("xs", [P, GS, H])
        xh = sb("xh", [P, 3, GS, W])
        tt = sb("tt", [P, GS, W])
        mh8 = sb("mh8", [P, HS])

        ps = ctx.enter_context(nc.psum_tensor("ps", [P, 8, HALF], F32))

        def unit(u):
            return ps[:, 2 * u:2 * u + 2, :].rearrange("p a n -> p (a n)")

        EB, MB, OB, CB, QB, HB, LG, LB, PB, BG, BB, CB63, PB2 = 0, 6, 10, 12, 13, 14, 15, 16, 17, 18, 19, 20, 21
        WE, WM, WO, WC, WQ, WHI, WPI = 0, 6, 10, 12, 15, 16, 17

        XA = XB[:, :].rearrange("p (b k c) -> p b k c", b=B, k=WB)
        AF = WK[:, 0:B * WB * C]
        AV = AF.rearrange("p (s k g c) -> p g s k c", g=BH, s=NS, k=WB)

        def A(b0, n, k=slice(0, WB)):
            return AV[:, b0 // NS, b0 % NS:b0 % NS + n, k, :]
        SWB = WK[:, 16384:18432]
        SQ = [WK[:, 18432 + 2048 * i:20480 + 2048 * i] for i in range(2)]
        MEANE = WK[:, 22528:24576]
        RGF = RG[:, :, :].rearrange("p r n -> p (r n)")
        P1N, P3N, P1T, P3T = (RGF[:, 1024 * i:1024 * (i + 1)].rearrange("p (k m) -> p k m", k=WB) for i in range(4))
        CWN = RGF[:, 4096:4096 + 3 * P].rearrange("p (t m) -> p t m", t=3)
        CWR = RGF[:, 4480:4480 + 3 * C]
        SUMA = RGF[:, 4672:4672 + B * WB].rearrange("p (b k) -> p b k", b=B)
        BAND_SB = WK[:, 0:2 * BAND].rearrange("p (l n) -> p l n", l=2)
        TAPS = (0, 9, 34, 83)
        KT = WK[:, 12096:12096 + TAPS[LEVELS] * UCH]
        ROWF = WK[:, 12800:12800 + 392]
        ROWR = WK[:, 13200:13200 + 392]
        ROWH = WK[:, 13600:13600 + 392].bitcast(BF16).rearrange("p (a n) -> p a n", a=2)

        def buf(i):
            return WK[:, 4096 * i:4096 * (i + 1)].rearrange("p (s n) -> p s n", s=GS)

        G, HA, HBF, SELF, K0T, K1T = (buf(i) for i in range(6))
        E1, M, T1 = G, K0T, HBF
        HBR = HBF.rearrange("p s n -> p (s n)").rearrange("p (h s w) -> p h s w", h=H, s=GS)
        HAR = HA.rearrange("p s n -> p (s n)").rearrange("p (w s h) -> p w s h", w=W, s=GS)
        XBS = XB[:, :].rearrange("p (s n) -> p s n", s=NS)

        CTX = WK[:, 0:16384]
        G4 = WK[:, 16384:24576].rearrange("p (s n) -> p s n", s=HS)
        CT = [WK[:, 16384 + 2048 * l:18432 + 2048 * l] for l in range(LEVELS)]
        RSUM = WK[:, 22528:24576]
        GLOB = CT[0]

        def ctxv(b, c=C):
            return b.rearrange("p (g c n) -> p g c n", g=BH, c=c)

        MBT, QT, XO, SQT, XR, OT = ([WK[:, 18432 + 1024 * i + HALF * j:18432 + 1024 * i + HALF * (j + 1)] for j in range(2)]
                                    for i in range(6))
        AS, TG, G4B = ([RGF[:, 1024 * i + HALF * j:1024 * i + HALF * (j + 1)] for j in range(2)] for i in range(3))

        block = ctx.enter_context(nc.Block())

        @block.sync
        def _(sp):
            for ch in range(NCH):
                for w4 in range(W4):
                    sp.dma_start(XA[H * w4:H * (w4 + 1), XCH * ch:XCH * (ch + 1), :, :].rearrange("p b k c -> p b (k c)"),
                                 x[XCH * ch:XCH * (ch + 1), :, WB * w4:WB * (w4 + 1), :].rearrange("b h k c -> h b (k c)")
                                 ).then_inc(sem(f"x_loaded{ch}"), 16)
            for l in range(LEVELS):
                sp.wait_ge(sem("band_copied"), W4 * (l + 1))
                for w in range(W4):
                    sp.dma_start(band_dram.ap()[l, :, w, :], BAND_SB[QP * w:QP * w + NU, l % 2, :]
                                 ).then_inc(sem("band_stored0" if l == 0 else "band_stored"), 16)
            sp.wait_ge(sem("band_stored0"), 16 * W4)
            sp.wait_ge(sem("band_stored"), 16 * (LEVELS - 1) * W4)
            sp.wait_ge(sem("relu_mm"), 16)

            def load_bands(l, cu, n):
                slot = n % RING
                if n >= RING:
                    sp.wait_ge(sem("conv_mm"), SUB * n - SUB * (RING - 1))
                for j in range(NJ):
                    src = bass.AP(tensor=band_dram.ap().tensor,
                                  offset=cu * (W4 * BAND) + (l * NU * W4 * BAND + (j * UH + H - 1) * UCH),
                                  ap=[[BAND, W4], [-UCH, H], [1, WIN]])
                    sp.dma_start(RG[:, slot, WIN * j:WIN * (j + 1)], src).then_inc(sem(f"ring_loaded{slot}"), 16)

            order = [(l, r - l) for r in range(NU + LEVELS - 1) for l in (2, 1, 0) if 0 <= r - l < NU]
            for n, (l, cu) in enumerate(order):
                load_bands(l, cu, n)

            def store(item):
                if item(4):
                    s, hh, low = item(4)
                    sp.wait_ge(sem("ot_ready"), 2 * s + hh + 1)
                    for bh in range(BH):
                        dst = out.rearrange("(g s) h (a q t) c -> g s a h q (t c)", g=BH, a=2, q=W4)
                        sp.dma_start(dst[bh, bass.ds(s, 1), hh, :, :, :].rearrange("o h q n -> (o h) q n"),
                                     OT[hh][:, 256 * bh:256 * (bh + 1)]).then_inc(sem(f"stored{hh}"), 16)

            half_slots(sp, store)
            for j in range(2):
                sp.wait_ge(sem(f"stored{j}"), NS * 16 * BH)

        @block.gpsimd
        def _(pool):
            nc.gpsimd.memset(WT[:, :, :], 0.0).then_inc(sem("zeroed"), 1)
            nc.gpsimd.memset(WCG[:, :], 0.0).then_inc(sem("zeroed"), 1)
            nc.gpsimd.memset(RGF[:, 0:2048], 0.0).then_inc(sem("zeroed"), 1)
            nc.gpsimd.memset(CWN, 0.0).then_inc(sem("zeroed"), 1)
            nc.gpsimd.memset(ident[:, :], 0.0).then_inc(sem("ident_zero"), 1)
            pool.wait_ge(sem("ident_zero"), 1)
            nc.gpsimd.affine_select(out=ident[:, :], in_=ident[:, :], compare_op=ALU.not_equal, fill=1.0, base=0,
                                    pattern=[[-1, P]], channel_multiplier=1).then_inc(sem("ident_set"), 1)
            nc.gpsimd.memset(mh8[:, :], -0.5).then_inc(sem("mhalf_set"), 1)
            pool.wait_ge(sem("taps_loaded"), 16 * LEVELS * W4)
            for l, kk in enumerate(KERNELS):
                r = kk // 2
                if l == 2:
                    pool.wait_ge(sem("band_stored0"), 16 * W4)
                nc.gpsimd.memset(BAND_SB[:, l % 2, :], 0.0).then_inc(sem("band_zero"), 1)
                pool.wait_ge(sem("band_zero"), l + 1)
                taps = KT[:, UCH * TAPS[l]:UCH * TAPS[l + 1]].rearrange("p (a b c) -> p b a c", a=kk, b=kk)
                for w in range(W4):
                    p = slice(QP * w, QP * w + NU)
                    table = BAND_SB[p, l % 2, :].rearrange("p (j u c) -> p j u c", j=NJ, u=UH)
                    nc.gpsimd.tensor_copy(table[:, w + W4 - r:w + W4 + r + 1, H - 1 - r:H + r, :], taps[p]
                                          ).then_inc(sem("band_copied"), 1)
                    pool.wait_ge(sem("band_copied"), W4 * l + w + 1)
            pool.wait_ge(sem("mhalf_set"), 1)
            pool.wait_ge(sem("bnvar_ready"), 1)
            nc.gpsimd.tensor_tensor(small[:, 4:5], small[:, 3:4], mh8[:, 0:1], ALU.pow).then_inc(sem("bnrstd"), 1)
            with pool.Fori(0, NG) as g:
                for n in range(2):
                    pool.wait_ge(sem("gnvar"), 2 * g + n + 1)
                    nc.gpsimd.tensor_tensor(gm[:, 3, 0:GS], gm[:, 2, 0:GS], mh8[:, 0:GS], ALU.pow
                                            ).then_inc(sem("gnrstd"), 1)
            with pool.Fori(0, NHALF) as hf:
                pool.wait_ge(sem("gnvar3"), hf + 1)
                nc.gpsimd.tensor_tensor(gm[:, 3, :], gm[:, 2, :], mh8[:, :], ALU.pow).then_inc(sem("gnrstd3"), 1)
            pool.wait_ge(sem("gated"), NSTEP)
            pool.wait_ge(sem("glob_out"), 2)
            gl = GLOB.rearrange("p (g c s) -> p g c s", g=BH, c=C)
            gt = gates[:, 3, :].rearrange("p (g k s) -> p k g s", g=BH, k=WB)
            al = CTX.rearrange("p (g c k s) -> p k g c s", g=BH, c=C, k=WB)

            def global_context(item):
                if item(0):
                    s, hh, low = item(0)
                    t = TG[hh].rearrange("p (k g c) -> p k g c", k=4, g=BH)
                    one = bass.ds(s, 1)
                    g_b = gl[:, :, :, one].rearrange("p g c o -> p o g c").to_broadcast([P, 4, BH, C])
                    t_b = gt[:, 4 * hh:4 * hh + 4, :, one].to_broadcast([P, 4, BH, C])
                    nc.gpsimd.tensor_tensor(t, g_b, t_b, ALU.mult).then_inc(sem("tg_ready"), 1)
                    pool.wait_ge(sem("tg_ready"), 2 * s + hh + 1)
                    if low >= 2:
                        pool.wait_ge(sem("mb_mm"), 2 * s + hh - 1)
                    nc.gpsimd.tensor_tensor(AS[hh].rearrange("p (k g c) -> p k g c", k=4, g=BH), t,
                                            al[:, 4 * hh:4 * hh + 4, :, :, one].rearrange("p k g c o -> p k g (c o)"),
                                            ALU.add).then_inc(sem("as_ready"), 1)
                    pool.wait_ge(sem("as_ready"), 2 * s + hh + 1)

            half_slots(pool, global_context)

        @block.scalar
        def _(act):
            ctx.enter_context(nc.allow_non_contiguous_dma(reason="short loads of biases and taps"))
            for l, (kk, k) in enumerate(zip(KERNELS, (k0, k1, k2))):
                for w in range(W4):
                    src = bass.AP(tensor=k.tensor, offset=k.offset + (kk * kk - 1) * C,
                                  ap=[[UCH, NU], [-C, kk * kk], [1, UCH]])
                    act.dma_start(KT[QP * w:QP * w + NU, UCH * TAPS[l]:UCH * TAPS[l + 1]].rearrange("p (t c) -> p t c", c=UCH),
                                  src).then_inc(sem("taps_loaded"), 16)
            act.wait_ge(sem("zeroed"), 4)
            for w4 in range(W4):
                p = slice(H * w4, H * (w4 + 1))
                act.dma_start(P1N[p, :, H * w4:H * (w4 + 1)],
                              P1[WB * w4:WB * (w4 + 1), :, :].rearrange("k o i -> o k i")).then_inc(sem("p_loaded"), 16)
                act.dma_start(P3N[p, :, H * w4:H * (w4 + 1)],
                              P3[WB * w4:WB * (w4 + 1), :, :].rearrange("k o i -> o k i")).then_inc(sem("p_loaded"), 16)
                act.dma_start(BC[p, BG:BG + 1], bn_gamma.rearrange("(h o) -> h o", o=1)).then_inc(sem("w_loaded"), 16)
                act.dma_start(BC[p, BB:BB + 1], bn_beta.rearrange("(h o) -> h o", o=1)).then_inc(sem("w_loaded"), 16)
            for bh in range(BH):
                p = slice(C * bh, C * (bh + 1))
                for dst, src in (
                    (WT[p, WE:WE + 6, p], emb_W.rearrange("l j i o -> i (l j) o")),
                    (WT[p, WM:WM + 4, p], mult_W.rearrange("l j i o -> i (l j) o")),
                    (WT[p, WO:WO + 2, p], out_W.rearrange("j i o -> i j o")),
                    (WT[p, WQ, p], Wf[:, 0:C]),
                    (WT[p, WHI, p], Wh), (WT[p, WPI, p], Wp),
                    (WCG[p, p], Wf[:, C:2 * C]), (WCG[p, P + 4 * bh:P + 4 * bh + 4], Wf[:, 2 * C:2 * C + 4]),
                    (CWR[p, :], cW.rearrange("o i t u -> o (i t u)")),
                    (BC[p, EB:EB + 6], emb_b.rearrange("l j o -> o (l j)")),
                    (BC[p, MB:MB + 4], mult_b.rearrange("l j o -> o (l j)")),
                    (BC[p, OB:OB + 2], out_b.rearrange("j o -> o j")),
                    (BC[p, CB:CB + 1], cb.rearrange("(c o) -> c o", o=1)),
                    (BC[p, QB:QB + 1], bf[0:C].rearrange("(c o) -> c o", o=1)),
                    (BC[p, HB:HB + 1], bh_.rearrange("(c o) -> c o", o=1)),
                    (BC[p, LG:LG + 1], ln_gamma.rearrange("(c o) -> c o", o=1)),
                    (BC[p, LB:LB + 1], ln_beta.rearrange("(c o) -> c o", o=1)),
                    (BC[p, PB:PB + 1], bp.rearrange("(c o) -> c o", o=1)),
                ):
                    act.dma_start(dst, src).then_inc(sem("w_loaded"), 16)
            n_w = 2 * W4 + BH * 18
            n = 0
            for bh in range(BH):
                for at, src in ((C * bh, emb_b[1, 1]), (P + C * bh, emb_b[2, 1]), (2 * P + C * bh, bf[C:2 * C]),
                                (3 * P + 4 * bh, bf[2 * C:2 * C + 4])):
                    k = src.shape[0]
                    act.dma_start(ROWF[:, at:at + k],
                                  bass.AP(tensor=src.tensor, offset=src.offset, ap=[[0, P], [1, k]])
                                  ).then_inc(sem("row_loaded"), 16)

            for ch in range(NCH):
                act.wait_ge(sem(f"x_loaded{ch}"), 16 * W4)
                if ch >= 2:
                    act.wait_ge(sem("sq_used"), ch - 1)
                nc.scalar.activation(SQ[ch % 2], XA[:, XCH * ch:XCH * (ch + 1), :, :].rearrange("p b k c -> p (b k c)"),
                                     ACT.Square).then_inc(sem("sq_ready"), 1)
            act.wait_ge(sem("var0_ready"), 1)
            nc.scalar.activation(SQ[1][:, 0:1024], SQ[0][:, 1024:2048], ACT.Sqrt).then_inc(sem("sd0"), 1)
            for n in range(16):
                b8, k = n // 4, 2 * (n % 4)
                act.wait_ge(sem("relu_mm"), n + 1)
                r0 = A(NB8 * b8, NB8, slice(k, k + 2))
                nc.scalar.activation(r0.rearrange("p b k c -> p k b c"),
                                     unit(n % 4).rearrange("p (k b c) -> p k b c", k=2, b=NB8), ACT.Relu,
                                     accum_out=xs[:, 0, n:n + 1]).then_inc(sem("relu_done"), 1)
                act.wait_ge(sem("relu_done"), n + 1)
                nc.scalar.activation(unit(n % 4).rearrange("p (k b c) -> p k b c", k=2, b=NB8),
                                     r0.rearrange("p b k c -> p k b c"), ACT.Square,
                                     accum_out=xs[:, 1, n:n + 1]).then_inc(sem("relu_sq"), 1)
            act.wait_ge(sem("bn_coef"), 1)
            for i in range(16):
                v = AF[:, 1024 * i:1024 * (i + 1)]
                nc.scalar.activation(v, v, ACT.Identity, bias=small[:, 6:7], scale=small[:, 5:6]).then_inc(sem("bn_applied"), 1)
            for s in range(1, NS, 2):
                act.wait_ge(sem("xt_mm"), s + 1)
                nc.scalar.activation(XBS[:, s, :].rearrange("p (h a k) -> p k a h", h=H, a=W4),
                                     unit(s % 4).rearrange("p (k a h) -> p k a h", k=WB, a=W4),
                                     ACT.Copy).then_inc(sem("xt_out_a"), 1)

            with act.Fori(0, NG) as g:
                def silu(stage, dst, bias=None, free=None, src=lambda v: v):
                    for u in range(GS):
                        act.wait_ge(sem(stage + "_mm"), GS * g + u + 1)
                        if free is not None:
                            act.wait_ge(sem(free), GS * g + u + 1)
                        nc.scalar.activation(dst(u), src(unit(u)), ACT.Silu,
                                             bias=0.0 if bias is None else BC[:, bias:bias + 1]
                                             ).then_inc(sem(stage + "_out"), 1)

                def slot(b):
                    return lambda u: b[:, u, :]

                silu("s1", slot(HA), EB + 0)
                silu("k1", lambda u: HBR[:, :, u, :], EB + 2, src=lambda v: v.rearrange("p (h w) -> p h w", h=H))
                silu("s2", slot(SELF), EB + 1)
                silu("k2", slot(K0T))
                silu("l1", lambda u: HAR[:, :, u, :], EB + 4, src=lambda v: v.rearrange("p (h w) -> p w h", h=H))
                silu("l2", slot(K1T))
                for m in range(2):
                    silu(f"m{m}a", slot(HA), MB + 2 * m)
                    silu(f"m{m}b", slot(T1), MB + 2 * m + 1, free=None if m == 0 else "res0")
                silu("oa", slot(HA), OB)
                silu("ob", slot(T1), OB + 1, free="res1")
                act.wait_ge(sem("t_mm"), g + 1)
                nc.scalar.activation(tt[:, :, :].rearrange("p s w -> p (s w)"), ps[:, 7, 0:GS * W], ACT.Identity,
                                     bias=BC[:, CB63:CB63 + 1]).then_inc(sem("t_out"), 1)

            with act.Fori(0, NHALF) as hf:
                for n in range(1, 2 * HS, 2):
                    s, k = n // 2, 4 * (n % 2)
                    act.wait_ge(sem("proj_mm"), hf * 2 * HS + n + 1)
                    src = unit(n % 4).rearrange("p (k m) -> p k m", k=4)
                    one = bass.ds(hf * HS + s, 1)
                    for bh in range(BH):
                        last = nc.scalar.activation(
                            CTX.rearrange("p (g c k s) -> p g k c s", g=BH, c=C, k=WB
                                          )[:, bh, k:k + 4, :, one].rearrange("p k c o -> p k (c o)"),
                            src[:, :, C * bh:C * (bh + 1)], ACT.Copy)
                    nc.scalar.activation(
                        gates[:, :, :].rearrange("p l (g k s) -> p k g l s", k=WB, g=BH
                                                 )[:, k:k + 4, :, :, one].rearrange("p k g l o -> p k g (l o)"),
                        src[:, :, P:P + 8].rearrange("p k (g l) -> p k g l", g=BH), ACT.Copy).then_inc(sem("proj_out_a"), 1)

            def gelu(l, cu, n, uses, odd, ready, prev):
                for j in range(SUB):
                    act.wait_ge(sem("conv_mm"), SUB * n + j + 1)
                    if prev is not None and j == 0:
                        act.wait_ge(sem("gated"), prev + 1)
                    c = UCH // SUB
                    nc.scalar.activation(ctxv(CT[l], UCH)[:, :, c * j:c * (j + 1), :].rearrange("p g c n -> p c g n"),
                                         unit(2 * odd + j).rearrange("p (c g n) -> p c g n", c=c, g=BH), ACT.Gelu
                                         ).then_inc(sem("conv_out"), 1)

            conv_steps(act, gelu)
            act.wait_ge(sem("glob_mm"), 1)
            act.wait_ge(sem("gated"), NSTEP)
            for j in range(2):
                nc.scalar.activation(GLOB[:, 1024 * j:1024 * (j + 1)], unit(j), ACT.Gelu, scale=1.0 / TOK
                                     ).then_inc(sem("glob_out"), 1)

            def tail(item):
                if item(1):
                    s, hh, low = item(1)
                    act.wait_ge(sem("mb_mm"), 2 * s + hh + 1)
                    if low >= 2:
                        act.wait_ge(sem("mod_mm"), 2 * s + hh - 1)
                    nc.scalar.activation(MBT[hh].rearrange("p (h k q) -> p k q h", h=H, q=W4),
                                         ps[:, 0, :].rearrange("p (k q h) -> p k q h", k=4, h=H),
                                         ACT.Copy).then_inc(sem("mb_ready"), 1)
                if item(2):
                    s, hh, low = item(2)
                    act.wait_ge(sem("q_mm"), 2 * s + hh + 1)
                    if low >= 2:
                        act.wait_ge(sem("xo_ready"), 2 * s + hh - 1)
                    nc.scalar.activation(QT[hh], ps[:, 1, :], ACT.Identity, bias=BC[:, QB:QB + 1]).then_inc(sem("q_ready"), 1)
                if item(3):
                    s, hh, low = item(3)
                    act.wait_ge(sem("xc_mm"), 2 * s + hh + 1)
                    if low >= 2:
                        act.wait_ge(sem("var_mm"), 2 * s + hh - 1)
                    nc.scalar.activation(SQT[hh], ps[:, 3, :], ACT.Square).then_inc(sem("sqt_ready"), 1)
                    if low >= 2:
                        act.wait_ge(sem("xres_mm"), 2 * s + hh - 1)
                    xg = XBS[:, bass.ds(s, 1), :].rearrange("p o (h a w) -> p (o h) a w", h=H, a=2)[:, :, hh, :]
                    nc.scalar.activation(XR[hh].rearrange("p (h w) -> p h w", h=H), xg, ACT.Identity,
                                         bias=BC[:, PB2:PB2 + 1]).then_inc(sem("xr_ready"), 1)
                if item(4):
                    s, hh, low = item(4)
                    act.wait_ge(sem("var_mm"), 2 * s + hh + 1)
                    if low >= 2:
                        act.wait_ge(sem("rs_ready"), 2 * s + hh - 1)
                    nc.scalar.activation(sd[:, hh, :], ps[:, 4, 0:8], ACT.Sqrt, bias=BC[:, 22:23]).then_inc(sem("sd_ready"), 1)

            half_slots(act, tail)

        @block.vector
        def _(dve):
            count = [0]

            def link(ins, chain="dve_chain", base=0):
                count[0] += 1
                ins.then_inc(sem(chain), 1)
                dve.wait_ge(sem(chain), base + count[0])

            def take_wait(column):
                nc.vector.memset(small[:, column:column + 1], 0.0)

            TS, TT, STT = nc.vector.tensor_scalar, nc.vector.tensor_tensor, nc.vector.scalar_tensor_tensor
            cp = nc.vector.tensor_copy
            nc.vector.memset(ones[:, :], 1.0).then_inc(sem("ones_set"), 1)
            nc.vector.memset(onesb[:, :], 1.0).then_inc(sem("ones_set"), 1)
            nc.vector.memset(BC[:, 22:23], EPS_LN).then_inc(sem("eps_set"), 1)
            link(nc.vector.memset(meanm[:, :], 0.0))
            link(nc.vector.memset(meanm[0:C, 0:C], 1.0 / C))
            nc.vector.memset(meanm[C:P, C:P], 1.0 / C).then_inc(sem("dve_chain"), 1)
            count[0] += 1
            dve.wait_ge(sem("ident_set"), 1)
            dve.wait_ge(sem("dve_chain"), count[0])
            TT(centm[:, :], ident[:, :], meanm[:, :], ALU.subtract).then_inc(sem("mats_set"), 1)
            link(nc.vector.tensor_reduce(xh[:, 0, 0:2, :].rearrange("p a b -> p (a b)"),
                                         ident[:, :].rearrange("p (g j) -> p g j", j=2), AX.X, ALU.add))
            TS(pairm[:, :].rearrange("p (g j) -> p g j", j=2),
               xh[:, 0, 0:2, :].rearrange("p a (b o) -> p (a b) o", o=1).to_broadcast([P, 64, 2]), 0.5, None, ALU.mult
               ).then_inc(sem("mats_set"), 1)
            link(nc.vector.tensor_reduce(xh[:, 1, 0, :], ident[:, :].rearrange("p (a h) -> p h a", a=W4), AX.X, ALU.add))
            cp(rowm[:, :].rearrange("p (a h) -> p a h", a=W4), xh[:, 1, 0:1, :].to_broadcast([P, W4, H])
               ).then_inc(sem("mats_set"), 1)
            dve.wait_ge(sem("row_loaded"), 16 * 8)
            link(nc.vector.memset(ROWB[:, :], 0.0))
            link(TS(ROWR, ROWF, 1.0 / 32, None, ALU.mult))
            link(cp(ROWB[0:32, :], ROWR[0:32, :]))
            link(cp(ROWH[:, 0, :], ROWR))
            link(TT(ROWR, ROWR, ROWH[:, 0, :], ALU.subtract))
            link(cp(ROWB[32:64, :], ROWR[32:64, :]))
            link(cp(ROWH[:, 1, :], ROWR))
            link(TT(ROWR, ROWR, ROWH[:, 1, :], ALU.subtract))
            cp(ROWB[64:96, :], ROWR[64:96, :]).then_inc(sem("rowb_set"), 1)
            dve.wait_ge(sem("w_loaded"), 16 * (2 * W4 + BH * 18))
            for bh in range(BH):
                p = slice(C * bh, C * (bh + 1))
                cp(CWN[p, :, p], CWR[p, :].rearrange("p (i t) -> p t i", t=3)).then_inc(sem("cwn_ready"), 1)
            dve.wait_ge(sem("pt_mm"), 1)
            cp(P1T.rearrange("p k m -> p (k m)"), unit(0)).then_inc(sem("pt_ready"), 1)
            TS(P3T.rearrange("p k m -> p (k m)"), unit(1), 0.1 / C, None, ALU.mult).then_inc(sem("pt_ready"), 1)
            scale = (H + W - 2) ** 0.5
            TS(WT[:, WC:WC + 3, :].rearrange("p t m -> p (t m)"), ps[:, 4, 0:3 * P], 1.0 / scale, None, ALU.mult
               ).then_inc(sem("pt_ready"), 1)
            TS(BC[:, CB63:CB63 + 1], BC[:, CB:CB + 1], (H + W - 1) / scale, None, ALU.mult).then_inc(sem("bc_ready"), 1)
            dve.wait_ge(sem("pb_mm"), 1)
            TT(BC[:, PB2:PB2 + 1], ps[:, 5, 0:1], BC[:, PB:PB + 1], ALU.add).then_inc(sem("bc_ready"), 1)
            TS(WT[:, WPI, :], WT[:, WPI, :], BC[:, LG:LG + 1], None, ALU.mult).then_inc(sem("bc_ready"), 1)
            dve.wait_ge(sem("wpc_mm"), 1)
            cp(WT[:, WPI, :], ps[:, 6, 0:P]).then_inc(sem("bc_ready"), 1)

            swb = SWB.rearrange("p (b c) -> p b c", b=B)
            for ch in range(NCH):
                dve.wait_ge(sem(f"x_loaded{ch}"), 16 * W4)
                nc.vector.tensor_reduce(swb[:, XCH * ch:XCH * (ch + 1), :],
                                        XA[:, XCH * ch:XCH * (ch + 1), :, :].rearrange("p b k c -> p b c k"),
                                        AX.X, ALU.add).then_inc(sem("swb_ready"), 1)
            mean, msq, rstd = SQ[0][:, 0:1024], SQ[1][:, 1024:2048], SQ[1][:, 0:1024]
            var = SQ[0][:, 1024:2048]
            dve.wait_ge(sem("sum0_mm"), 1)
            pairs = ps[:, 4:8, :].rearrange("p a (g j) -> p (a g) j", j=2)
            link(nc.vector.tensor_reduce(mean, pairs, AX.X, ALU.add))
            pairs = ps[:, 0:4, :].rearrange("p a (g j) -> p (a g) j", j=2)
            link(nc.vector.tensor_reduce(var, pairs, AX.X, ALU.add))
            link(TS(mean, mean, 1.0 / (2 * TOK), None, ALU.mult))
            link(TT(msq, mean, mean, ALU.mult))
            link(STT(out=var, in0=var, scalar=1.0 / (2 * TOK), in1=msq, op0=ALU.mult, op1=ALU.subtract))
            TS(var, var, 0.0, EPS_GN, ALU.max, ALU.add).then_inc(sem("var0_ready"), 1)
            one = mean.rearrange("p (g o) -> p g o", o=1)
            link(cp(MEANE.rearrange("p (g j) -> p g j", j=2), one.to_broadcast([P, 1024, 2])))
            dve.wait_ge(sem("sd0"), 1)
            link(nc.vector.reciprocal(rstd, rstd))
            one = rstd.rearrange("p (g o) -> p g o", o=1)
            link(cp(SWB.rearrange("p (g j) -> p g j", j=2), one.to_broadcast([P, 1024, 2])))
            dve.wait_ge(sem("band_stored"), 16 * (LEVELS - 1) * W4)
            dve.wait_ge(sem("rowb_set"), 1)
            for ch in range(NCH):
                b = slice(XCH * ch, XCH * (ch + 1))
                m_b = MEANE.rearrange("p (b o c) -> p b o c", b=B, o=1)[:, b].to_broadcast([P, XCH, WB, C])
                r_b = SWB.rearrange("p (b o c) -> p b o c", b=B, o=1)[:, b].to_broadcast([P, XCH, WB, C])
                a = A(XCH * ch, XCH)
                link(TT(a, XA[:, b], m_b, ALU.subtract))
                link(TT(a, a, r_b, ALU.mult))
                nc.vector.tensor_reduce(SUMA[:, b, :], a, AX.X, ALU.add).then_inc(sem("a_ready"), 1)
            dve.wait_ge(sem("relu_sq"), 16)
            link(nc.vector.tensor_reduce(small[:, 0:2], xs[:, 0:2, 0:16], AX.X, ALU.add))
            nc.vector.tensor_copy(small[:, 8:10], small[:, 0:2]).then_inc(sem("bnsum_ready"), 1)
            dve.wait_ge(sem("bn_mm"), 1)
            nbn = B * W * C
            link(TS(small[:, 0:2], ps[:, 0, 0:2], 1.0 / nbn, None, ALU.mult))
            link(TT(small[:, 2:3], small[:, 0:1], small[:, 0:1], ALU.mult))
            link(TT(small[:, 3:4], small[:, 1:2], small[:, 2:3], ALU.subtract))
            TS(small[:, 3:4], small[:, 3:4], 0.0, EPS_BN, ALU.max, ALU.add).then_inc(sem("bnvar_ready"), 1)
            dve.wait_ge(sem("bnrstd"), 1)
            link(TT(small[:, 5:6], small[:, 4:5], BC[:, BG:BG + 1], ALU.mult))
            link(TT(small[:, 7:8], small[:, 5:6], small[:, 0:1], ALU.mult))
            TT(small[:, 6:7], BC[:, BB:BB + 1], small[:, 7:8], ALU.subtract).then_inc(sem("bn_coef"), 1)
            for i in range(16):
                dve.wait_ge(sem("bn_applied"), i + 1)
                v = AF[:, 1024 * i:1024 * (i + 1)].rearrange("p (k g c) -> p k g c", k=WB, g=BH)
                TT(v, v, XA.rearrange("p (g s) k c -> p s k g c", g=BH)[:, i], ALU.add).then_inc(sem("x1_ready"), 1)
            for s in range(0, NS, 2):
                dve.wait_ge(sem("xt_mm"), s + 1)
                cp(XBS[:, s, :].rearrange("p (h a k) -> p k a h", h=H, a=W4),
                   unit(s % 4).rearrange("p (k a h) -> p k a h", k=WB, a=W4)).then_inc(sem("xt_out_d"), 1)
            dve.wait_ge(sem("xt_out_a"), NS // 2)

            def group_norm(base, ns, first, lk, stats, coef, pool_sem, ready, coef_n, dst, order=lambda v: v,
                           keep=None):
                take_wait(30)
                for s in range(ns):
                    for j in range(2):
                        nc.vector.bn_stats(st[:, s, 6 * j:6 * j + 6],
                                           XBS[:, bass.ds(first + s, 1), HALF * j:HALF * (j + 1)].rearrange("p o n -> p (o n)")
                                           ).then_inc(sem("bn_stats"), 1)
                nstat[0] += 2 * ns
                dve.wait_ge(sem("bn_stats"), stat_base() + nstat[0])
                take_wait(31)
                for s in range(ns):
                    ins = nc.vector.bn_aggr(mv[:, s, :], st[:, s, :])
                lk(ins)
                lk(cp(me[:, 0, 0:ns], mv[:, 0:ns, 0]))
                lk(TT(me[:, 1, 0:ns], me[:, 0, 0:ns], me[:, 0, 0:ns], ALU.mult))
                TT(me[:, 1, 0:ns], me[:, 1, 0:ns], mv[:, 0:ns, 1], ALU.add).then_inc(sem(stats), 1)
                dve.wait_ge(sem(coef), coef_n)
                v = ps[:, 0, 0:2 * HS].rearrange("p (a s) -> p a s", a=2)
                lk(cp(gm[:, 0:2, 0:ns], v[:, :, 0:ns]))
                lk(TT(gm[:, 2, 0:ns], gm[:, 0, 0:ns], gm[:, 0, 0:ns], ALU.mult))
                lk(TT(gm[:, 1, 0:ns], gm[:, 1, 0:ns], gm[:, 2, 0:ns], ALU.subtract))
                TS(gm[:, 2, 0:ns], gm[:, 1, 0:ns], 0.0, EPS_GN, ALU.max, ALU.add).then_inc(sem(pool_sem[0]), 1)
                dve.wait_ge(sem(pool_sem[1]), coef_n)
                for s in range(ns):
                    apply_norm(s, first, dst, ready, order)
                if keep is not None:
                    lk(cp(gm3[:, :, keep], gm[:, 0:4:3, 0:ns]))

            def apply_norm(s, first, dst, ready, order=lambda v: v):
                TS(dst(s), order(XBS[:, bass.ds(first + s, 1), :].rearrange("p o n -> p (o n)")), gm[:, 0, s:s + 1],
                   gm[:, 3, s:s + 1], ALU.subtract, ALU.mult).then_inc(sem(ready), 1)

            CHAIN_B = 30
            STATS_B = 4 * GS
            with dve.Fori(0, NG) as g:
                count[0] = 0
                nstat = [0]

                def stat_base():
                    return g * STATS_B

                def lk(ins):
                    link(ins, "chain_b", g * CHAIN_B)

                first = g * GS
                group_norm(0, GS, first, lk, "stats_ready", "coef_mm", ("gnvar", "gnrstd"), "g_ready",
                           2 * g + 1, lambda s: G[:, s, :])
                for u in range(GS):
                    dve.wait_ge(sem("ein_mm"), GS * g + u + 1)
                    e1 = E1.rearrange("p s n -> p (s n)").rearrange("p (j q) -> p q j", j=W)
                    cp(e1[:, 32 * u:32 * (u + 1), :], unit(u).rearrange("p (q j) -> p q j", j=W)
                       ).then_inc(sem("ein_out"), 1)
                for u in range(GS):
                    dve.wait_ge(sem("tr_mm"), GS * g + u + 1)
                    m = M.rearrange("p s (i j) -> p j s i", i=H)
                    cp(m[:, 8 * u:8 * (u + 1), :, :], unit(u).rearrange("p (j s i) -> p j s i", j=8, s=GS)
                       ).then_inc(sem("tr_out"), 1)
                for m in range(2):
                    for u in range(GS):
                        dve.wait_ge(sem(f"m{m}b_out"), GS * g + u + 1)
                        ins = TT(M[:, u, :], M[:, u, :], T1[:, u, :], ALU.add)
                        ins.then_inc(sem(f"res{m}"), 1)
                for u in range(GS):
                    dve.wait_ge(sem("res1"), GS * g + u + 1)
                    TT(M[:, u, :], M[:, u, :], SELF[:, u, :], ALU.mult).then_inc(sem("z1_ready"), 1)
                for u in range(GS):
                    xg = XBS[:, bass.ds(first + u, 1), :].rearrange("p o n -> p (o n)")
                    dve.wait_ge(sem("ob_out"), GS * g + u + 1)
                    lk(TT(M[:, u, :], M[:, u, :], T1[:, u, :], ALU.add))
                    lk(TT(xg, xg, M[:, u, :], ALU.add))
                group_norm(1, GS, first, lk, "stats_ready", "coef_mm", ("gnvar", "gnrstd"), "g3_ready",
                           2 * g + 2, lambda s: G[:, s, :])
                dve.wait_ge(sem("g3_ready"), GS * g + GS)
                g4 = G.rearrange("p s (h w) -> p s h w", h=H)
                for u in range(GS):
                    nc.vector.tensor_reduce(xh[:, 1, u, :], g4[:, u].rearrange("p h w -> p w h"), AX.X, ALU.add)
                    ins = nc.vector.tensor_reduce(xs[:, u, :], g4[:, u], AX.X, ALU.add)
                lk(ins)
                TT(xh[:, 0], xh[:, 1], g4[:, :, H - 1, :], ALU.subtract).then_inc(sem("xh_ready"), 1)
                TT(xh[:, 2], xh[:, 1], g4[:, :, 0, :], ALU.subtract).then_inc(sem("xh_ready"), 1)
                for u in range(GS):
                    TT(HA[:, u, :].rearrange("p (h w) -> p h w", h=H),
                       xs[:, u, :].rearrange("p (h o) -> p h o", o=1).to_broadcast([P, H, W]), g4[:, u], ALU.subtract
                       ).then_inc(sem("z_ready"), 1)
                dve.wait_ge(sem("t_out"), g + 1)
                dve.wait_ge(sem("xh_ready"), 2 * g + 2)
                for u in range(GS):
                    ins = TT(g4[:, u], g4[:, u], tt[:, u:u + 1, :].to_broadcast([P, H, W]), ALU.add)
                lk(ins)
                for u in range(GS):
                    xg = XBS[:, bass.ds(first + u, 1), :].rearrange("p o n -> p (o n)")
                    dve.wait_ge(sem("y_mm"), GS * g + u + 1)
                    lk(TT(G[:, u, :], unit(u), G[:, u, :], ALU.add))
                    count[0] += 1
                    STT(out=xg, in0=G[:, u, :], scalar=0.0, in1=xg, op0=ALU.max, op1=ALU.add).then_inc(sem("chain_b"), 1)
                dve.wait_ge(sem("chain_b"), g * CHAIN_B + count[0])
                assert count[0] == CHAIN_B, count[0]

            CHAIN_C = 7
            with dve.Fori(0, NHALF) as hf:
                count[0] = 0
                nstat = [0]

                def stat_base():
                    return NG * STATS_B + hf * 2 * HS

                def lk(ins):
                    link(ins, "chain_c", hf * CHAIN_C)

                first = hf * HS
                group_norm(2, HS, first, lk, "stats3_ready", "coef3_mm", ("gnvar3", "gnrstd3"), "g4_ready",
                           hf + 1, lambda s: G4[:, s, :].rearrange("p (k q h) -> p h k q", k=WB, h=H),
                           lambda v: v.rearrange("p (h k q) -> p h k q", h=H, k=WB), keep=bass.ds(first, HS))
                for n in range(0, 2 * HS, 2):
                    s, k = n // 2, 4 * (n % 2)
                    dve.wait_ge(sem("proj_mm"), hf * 2 * HS + n + 1)
                    src = unit(n % 4).rearrange("p (k m) -> p k m", k=4)
                    one = bass.ds(first + s, 1)
                    for bh in range(BH):
                        cp(CTX.rearrange("p (g c k s) -> p g k c s", g=BH, c=C, k=WB
                                         )[:, bh, k:k + 4, :, one].rearrange("p k c o -> p k (c o)"),
                           src[:, :, C * bh:C * (bh + 1)])
                    cp(gates[:, :, :].rearrange("p l (g k s) -> p k g l s", k=WB, g=BH
                                                )[:, k:k + 4, :, :, one].rearrange("p k g l o -> p k g (l o)"),
                       src[:, :, P:P + 8].rearrange("p k (g l) -> p k g l", g=BH)).then_inc(sem("proj_out_d"), 1)
                assert count[0] == CHAIN_C, count[0]
            dve.wait_ge(sem("proj_out_a"), NHALF * HS)
            dve.wait_ge(sem("proj_out_d"), NHALF * HS)

            def gate_and_add(l, cu, n, uses, odd, ready, prev):
                dve.wait_ge(sem("conv_out"), SUB * n + SUB)
                if not (isinstance(n, int) and n == 0):
                    dve.wait_ge(sem("gated"), n)
                v = ctxv(CT[l], UCH)
                a = CTX.rearrange("p (g u c n) -> p u g c n", g=BH, u=NU, c=UCH)[:, bass.ds(cu, 1)
                                                                                  ].rearrange("p o g c n -> p (o g) c n")
                gate = gates[:, l, :].rearrange("p (g o n) -> p g o n", g=BH, o=1)
                if l == 0:
                    TT(a, v, gate.to_broadcast([P, BH, UCH, COLS // BH]), ALU.mult).then_inc(sem("gated"), 1)
                elif l == 1:
                    for g in range(BH):
                        for j in range(2):
                            c = slice(4 * j, 4 * (j + 1))
                            t = TMP[:, :].rearrange("p (c n) -> p c n", c=4)
                            piece = 2 * g + j
                            if piece > 0:
                                dve.wait_ge(sem("tmp_added"), 3 * cu + piece)
                            TT(t, v[:, g, c, :], gate[:, g].to_broadcast([P, 4, COLS // BH]), ALU.mult
                               ).then_inc(sem("tmp_ready"), 1)
                            dve.wait_ge(sem("tmp_ready"), 4 * cu + (piece + 1))
                            TT(a[:, g, c, :], a[:, g, c, :], t, ALU.add
                               ).then_inc(sem("tmp_added" if piece < 3 else "gated"), 1)
                else:
                    for g in range(BH):
                        r = RSUM.rearrange("p (g u c s) -> p g u c s", g=BH, u=NU, c=UCH)[:, g, bass.ds(cu, 1)]
                        nc.vector.tensor_reduce(r.rearrange("p o c s -> p (o c) s"),
                                                v[:, g].rearrange("p c (k s) -> p c s k", s=NS), AX.X, ALU.add
                                                ).then_inc(sem("rsum_ready"), 1)
                    dve.wait_ge(sem("rsum_ready"), BH * cu + BH)
                    TT(v, v, gate.to_broadcast([P, BH, UCH, COLS // BH]), ALU.mult).then_inc(sem("ct2_gated"), 1)
                    dve.wait_ge(sem("ct2_gated"), cu + 1)
                    TT(a, a, v, ALU.add).then_inc(sem("gated"), 1)

            conv_steps(dve, gate_and_add)
            dve.wait_ge(sem("glob_out"), 2)

            def tail(item):
                if item(2):
                    s, hh, low = item(2)
                    dve.wait_ge(sem("q_ready"), 2 * s + hh + 1)
                    dve.wait_ge(sem("mod_mm"), 2 * s + hh + 1)
                    if low >= 2:
                        dve.wait_ge(sem("y_mm2"), 2 * s + hh - 1)
                    STT(out=XO[hh], in0=ps[:, 2, :], scalar=BC[:, HB:HB + 1], in1=QT[hh],
                        op0=ALU.add, op1=ALU.mult).then_inc(sem("xo_ready"), 1)
                if item(1):
                    s, hh, low = item(1)
                    if low >= 2:
                        dve.wait_ge(sem("q_mm"), 2 * s + hh - 1)
                    one = bass.ds(s, 1)
                    xg = XBS[:, one, :].rearrange("p o (h a w) -> p (o h) a w", h=H, a=2)[:, :, hh, :]
                    TS(G4B[hh].rearrange("p (h w) -> p h w", h=H), xg, gm3[:, 0, one], gm3[:, 1, one],
                       ALU.subtract, ALU.mult).then_inc(sem("g4b_ready"), 1)
                if item(4):
                    s, hh, low = item(4)
                    dve.wait_ge(sem("sd_ready"), 2 * s + hh + 1)
                    nc.vector.reciprocal(rs[:, hh, :], sd[:, hh, :]).then_inc(sem("rs_ready"), 1)
                    dve.wait_ge(sem("rs_ready"), 2 * s + hh + 1)
                    dve.wait_ge(sem("y_mm2"), 2 * s + hh + 1)
                    if low >= 2:
                        dve.wait_ge(sem(f"stored{hh}"), s * (16 * BH))
                    ot = OT[hh].rearrange("p (g t c) -> p t g c", g=BH, t=4)
                    r = rs[:, hh, :].rearrange("p (t g o) -> p t g o", t=4, g=BH).to_broadcast([P, 4, BH, C])
                    TT(ot, ps[:, 5 + 2 * hh, :].rearrange("p (t g c) -> p t g c", t=4, g=BH), r, ALU.mult
                       ).then_inc(sem("scaled"), 1)
                    dve.wait_ge(sem("scaled"), 2 * s + hh + 1)
                    dve.wait_ge(sem("xres_mm"), 2 * s + hh + 1)
                    TT(ot, ot, ps[:, 6, :].rearrange("p (t g c) -> p t g c", t=4, g=BH), ALU.add
                       ).then_inc(sem("ot_ready"), 1)

            half_slots(dve, tail)

        @block.tensor
        def _(pe):
            def mm(out, lhsT, rhs, start=True, stop=True):
                return nc.tensor.matmul(out, lhsT, rhs, start=start, stop=stop)

            pe.wait_ge(sem("ident_set"), 1)
            pe.wait_ge(sem("p_loaded"), 16 * 2 * W4)
            pe.wait_ge(sem("w_loaded"), 16 * (2 * W4 + BH * 18))
            pe.wait_ge(sem("cwn_ready"), BH)
            for k in range(WB):
                nc.tensor.transpose(unit(0)[:, P * k:P * (k + 1)], P1N[:, k, :], ident[:, :])
                nc.tensor.transpose(unit(1)[:, P * k:P * (k + 1)], P3N[:, k, :], ident[:, :])
            for t in range(3):
                last = nc.tensor.transpose(ps[:, 4, P * t:P * (t + 1)], CWN[:, t, :], ident[:, :])
            last.then_inc(sem("pt_mm"), 1)
            mm(ps[:, 5, 0:1], WT[:, WPI, :], BC[:, LB:LB + 1]).then_inc(sem("pb_mm"), 1)
            pe.wait_ge(sem("pt_ready"), 3)
            pe.wait_ge(sem("bc_ready"), 3)
            pe.wait_ge(sem("mats_set"), 3)
            mm(ps[:, 6, 0:P], centm[:, :], WT[:, WPI, :]).then_inc(sem("wpc_mm"), 1)
            pe.wait_ge(sem("ones_set"), 2)
            pe.wait_ge(sem("bc_ready"), 4)
            for ch in range(NCH):
                pe.wait_ge(sem("sq_ready"), ch + 1)
                q = SQ[ch % 2].rearrange("p (b k c) -> p b k c", b=XCH, k=WB)
                for k in range(WB):
                    last = mm(ps[:, ch // 2, 256 * (ch % 2):256 * (ch % 2 + 1)], ones[:, :], q[:, :, k, :],
                              start=k == 0, stop=k == WB - 1)
                last.then_inc(sem("sq_used"), 1)
            pe.wait_ge(sem("swb_ready"), NCH)
            for i in range(4):
                last = mm(ps[:, 4 + i, :], ones[:, :], SWB[:, HALF * i:HALF * (i + 1)])
            last.then_inc(sem("sum0_mm"), 1)
            pe.wait_ge(sem("mats_set"), 3)
            for n in range(16):
                b8, k = n // 4, 2 * (n % 4)
                b = slice(NB8 * b8, NB8 * (b8 + 1))
                pe.wait_ge(sem("a_ready"), 2 * (b8 + 1))
                if n >= 4:
                    pe.wait_ge(sem("relu_sq"), n - 3)
                for j in range(2):
                    o = ps[:, 2 * (n % 4) + j, :]
                    mm(o, P1T[:, k + j, :], A(NB8 * b8, NB8, k + j), True, False)
                    last = mm(o, P3T[:, k + j, :],
                              SUMA[:, b, k + j:k + j + 1].to_broadcast([P, NB8, C]), False, True)
                last.then_inc(sem("relu_mm"), 1)
            pe.wait_ge(sem("bnsum_ready"), 1)
            pe.wait_ge(sem("relu_sq"), 16)
            mm(ps[:, 0, 0:2], rowm[:, :], small[:, 8:10]).then_inc(sem("bn_mm"), 1)
            pe.wait_ge(sem("x1_ready"), 16)
            for s in range(NS):
                if s >= 4:
                    pe.wait_ge(sem("xt_out_d" if s % 2 == 0 else "xt_out_a"), (s - 4) // 2 + 1)
                for k in range(WB):
                    last = nc.tensor.transpose(unit(s % 4)[:, P * k:P * (k + 1)], AF[:, 1024 * s + P * k:1024 * s + P * (k + 1)], ident[:, :])
                last.then_inc(sem("xt_mm"), 1)
            pe.wait_ge(sem("xt_out_a"), NS // 2)
            pe.wait_ge(sem("xt_out_d"), NS // 2)
            pe.wait_ge(sem("rowb_set"), 1)

            with pe.Fori(0, NG) as g:
                def coef(n):
                    pe.wait_ge(sem("stats_ready"), 2 * g + n + 1)
                    v = ps[:, 0, 0:2 * HS].rearrange("p (a s) -> p a s", a=2)[:, :, 0:GS]
                    mm(v, pairm[:, :], me[:, :, 0:GS]).then_inc(sem("coef_mm"), 1)

                def dense(stage, w, src, waits):
                    for u in range(GS):
                        for name, all_slots in waits:
                            pe.wait_ge(sem(name), GS * g + (GS if all_slots else u + 1))
                        for j in range(2):
                            last = mm(ps[:, 2 * u + j, :], WT[:, w, :], src[:, u, HALF * j:HALF * (j + 1)])
                        last.then_inc(sem(stage + "_mm"), 1)

                def dense_t(stage, w, row, src, waits):
                    for u in range(GS):
                        for name, all_slots in waits:
                            pe.wait_ge(sem(name), GS * g + (GS if all_slots else u + 1))
                        for j in range(2):
                            mm(ps[:, 2 * u + j, :].rearrange("p (k m) -> p k m", k=4), onesb[:, :],
                               ROWB[:, row:row + P].rearrange("p (o m) -> p o m", o=1).to_broadcast([P, 4, P]), True, False)
                            for k in range(4):
                                last = mm(ps[:, 2 * u + j, P * k:P * (k + 1)], src(8 * u + 4 * j + k), WT[:, w, :],
                                          False, k == 3)
                        last.then_inc(sem(stage + "_mm"), 1)

                coef(0)
                dense("s1", WE + 0, G, [("g_ready", False)])
                dense("k1", WE + 2, G, [("s1_out", False)])
                dense("s2", WE + 1, HA, [("k1_out", False)])
                dense_t("k2", WE + 3, 0, lambda i: HBR[:, i].rearrange("p s w -> p (s w)"), [("s2_out", False), ("k1_out", True)])
                dense("l1", WE + 4, G, [("k2_out", False)])
                dense_t("l2", WE + 5, P, lambda i: HAR[:, i].rearrange("p s h -> p (s h)"), [("l1_out", False), ("l1_out", True)])
                k0 = K0T.rearrange("p s n -> p (s n)").rearrange("p (i q) -> p i q", i=H)
                k1 = K1T.rearrange("p s n -> p (s n)").rearrange("p (j q) -> p j q", j=W)
                for u in range(GS):
                    pe.wait_ge(sem("mats_set"), 3)
                    pe.wait_ge(sem("l2_out"), GS * g + GS)
                    for q in range(32):
                        for s in range(GS):
                            p = slice(32 * s, 32 * (s + 1))
                            last = mm(ps[p, 2 * u + q // 16, 32 * (q % 16):32 * (q % 16 + 1)],
                                      k0[p, :, 32 * u + q], k1[p, :, 32 * u + q])
                    last.then_inc(sem("ein_mm"), 1)
                e1 = E1.rearrange("p s n -> p (s n)").rearrange("p (j q) -> p j q", j=W)
                for u in range(GS):
                    pe.wait_ge(sem("ein_out"), GS * g + GS)
                    for k in range(8):
                        last = nc.tensor.transpose(unit(u)[:, P * k:P * (k + 1)], e1[:, 8 * u + k, :], ident[:, :])
                    last.then_inc(sem("tr_mm"), 1)
                dense("m0a", WM + 0, M, [("tr_out", True)])
                dense("m0b", WM + 1, HA, [("m0a_out", False)])
                dense("m1a", WM + 2, M, [("m0b_out", False), ("res0", False)])
                dense("m1b", WM + 3, HA, [("m1a_out", False)])
                dense("oa", WO + 0, M, [("m1b_out", False), ("z1_ready", False)])
                dense("ob", WO + 1, HA, [("oa_out", False)])
                pe.wait_ge(sem("ob_out"), GS * g + GS)
                coef(1)
                pe.wait_ge(sem("xh_ready"), 2 * g + 2)
                for t in range(3):
                    last = mm(ps[:, 7, 0:GS * W], WT[:, WC + t, :], xh[:, t, :, :].rearrange("p s w -> p (s w)"),
                              t == 0, t == 2)
                last.then_inc(sem("t_mm"), 1)
                z = HA.rearrange("p s (h w) -> p s h w", h=H)
                for u in range(GS):
                    pe.wait_ge(sem("z_ready"), GS * g + u + 1)
                    if u == GS - 1:
                        pe.wait_ge(sem("t_out"), g + 1)
                    for j in range(2):
                        h0, h1 = 16 * j, 16 * (j + 1)
                        for n, t in enumerate((1, 0, 2)):
                            lo, hi = max(h0, 1 - t), min(h1, H + 1 - t)
                            last = mm(ps[:, 2 * u + j, W * (lo - h0):W * (hi - h0)], WT[:, WC + t, :],
                                      z[:, u, lo + t - 1:hi + t - 1, :].rearrange("p h w -> p (h w)"), n == 0, n == 2)
                    last.then_inc(sem("y_mm"), 1)

            with pe.Fori(0, NHALF) as hf:
                pe.wait_ge(sem("stats3_ready"), hf + 1)
                v = ps[:, 0, 0:2 * HS].rearrange("p (a s) -> p a s", a=2)
                mm(v, pairm[:, :], me[:, :, :]).then_inc(sem("coef3_mm"), 1)
                g4 = G4.rearrange("p s (k n) -> p s k n", k=WB)
                for n in range(2 * HS):
                    s, k0_ = n // 2, 4 * (n % 2)
                    pe.wait_ge(sem("g4_ready"), hf * HS + s + 1)
                    if n >= 4:
                        pe.wait_ge(sem("proj_out_d" if n % 2 == 0 else "proj_out_a"), hf * HS + (n - 4) // 2 + 1)
                    for j in range(2):
                        o = ps[:, 2 * (n % 4) + j, :].rearrange("p (k m) -> p k m", k=2)[:, :, 0:P + 8]
                        mm(o, onesb[:, :], ROWB[:, 2 * P:3 * P + 8].rearrange("p (o m) -> p o m", o=1
                                                                             ).to_broadcast([P, 2, P + 8]), True, False)
                        for i in range(2):
                            last = mm(o[:, i, :], g4[:, s, k0_ + 2 * j + i], WCG[:, :], False, i == 1)
                    last.then_inc(sem("proj_mm"), 1)
                pe.wait_ge(sem("proj_out_d"), hf * HS + HS)
                pe.wait_ge(sem("proj_out_a"), hf * HS + HS)

            def conv(l, cu, n, uses, odd, ready, prev):
                slot = odd
                v = ctxv(CTX if l == 0 else CT[l - 1], C if l == 0 else UCH)
                if l >= 1:
                    pe.wait_ge(sem("conv_out"), SUB * ready + SUB)
                pe.wait_ge(sem(f"ring_loaded{slot}"), 16 * NJ * uses + 16 * NJ)
                band = RG[:, slot, :].rearrange("p (j m c) -> p j m c", j=NJ // W4, c=UCH)
                for j in range(SUB):
                    if not (isinstance(n, int) and n < 2):
                        pe.wait_ge(sem("conv_out"), SUB * n + (j - 3))
                    for c in range(UCH // SUB * j, UCH // SUB * (j + 1)):
                        o = ps[:, 4 * slot + c // 2, COLS * (c % 2):COLS * (c % 2 + 1)].rearrange("p (g n) -> p g n", g=BH)
                        if l == 0:
                            x = v.rearrange("p g (u c) n -> p g u c n", u=NU)[:, :, bass.ds(cu, 1), c, :
                                                                               ].rearrange("p g o n -> p g (o n)")
                        else:
                            x = v[:, :, c, :]
                        mm(o, band[:, 1, :, c], x, True, False)
                        mm(o[:, :, 0:NS * (WB - 1)], band[:, 0, :, c], x[:, :, NS:], False, False)
                        last = mm(o[:, :, NS:], band[:, 2, :, c], x[:, :, 0:NS * (WB - 1)], False, True)
                    last.then_inc(sem("conv_mm"), 1)

            conv_steps(pe, conv)
            pe.wait_ge(sem("rsum_ready"), BH * NU)
            for j in range(4):
                last = mm(ps[:, j, :], ones[:, :], RSUM[:, HALF * j:HALF * (j + 1)])
            last.then_inc(sem("glob_mm"), 1)
            pe.wait_ge(sem("glob_out"), 2)

            def tail(item):
                if item(4):
                    s, hh, low = item(4)
                    pe.wait_ge(sem("sqt_ready"), 2 * s + hh + 1)
                    if low >= 1:
                        pe.wait_ge(sem("sd_ready"), 2 * s + hh)
                    q = SQT[hh].rearrange("p (n t) -> p t n", t=4)
                    for t in range(4):
                        last = mm(ps[:, 4, 2 * t:2 * t + 2], q[:, t, :], meanm[:, 0:P:C])
                    last.then_inc(sem("var_mm"), 1)
                    pe.wait_ge(sem("xr_ready"), 2 * s + hh + 1)
                    if low >= 1:
                        pe.wait_ge(sem("ot_ready"), 2 * s + hh)
                    y = XR[hh].rearrange("p (n t) -> p t n", t=4)
                    for t in range(4):
                        last = nc.tensor.transpose(ps[:, 6, P * t:P * (t + 1)], y[:, t, :], ident[:, :])
                    last.then_inc(sem("xres_mm"), 1)
                if item(3):
                    s, hh, low = item(3)
                    pe.wait_ge(sem("xo_ready"), 2 * s + hh + 1)
                    if low >= 1:
                        pe.wait_ge(sem("sqt_ready"), 2 * s + hh)
                    mm(ps[:, 3, :], centm[:, :], XO[hh]).then_inc(sem("xc_mm"), 1)
                    if low >= 2:
                        pe.wait_ge(sem("ot_ready"), 2 * s + hh - 1)
                    y = XO[hh].rearrange("p (n t) -> p t n", t=4)
                    for t in range(4):
                        last = mm(ps[:, 5 + 2 * hh, P * t:P * (t + 1)], y[:, t, :], WT[:, WPI, :])
                    last.then_inc(sem("y_mm2"), 1)
                if item(2):
                    s, hh, low = item(2)
                    pe.wait_ge(sem("g4b_ready"), 2 * s + hh + 1)
                    if low >= 1:
                        pe.wait_ge(sem("q_ready"), 2 * s + hh)
                    mm(ps[:, 1, :], WT[:, WQ, :], G4B[hh]).then_inc(sem("q_mm"), 1)
                    pe.wait_ge(sem("mb_ready"), 2 * s + hh + 1)
                    if low >= 1:
                        pe.wait_ge(sem("xo_ready"), 2 * s + hh)
                    mm(ps[:, 2, :], WT[:, WHI, :], MBT[hh]).then_inc(sem("mod_mm"), 1)
                if item(1):
                    s, hh, low = item(1)
                    pe.wait_ge(sem("as_ready"), 2 * s + hh + 1)
                    if low >= 1:
                        pe.wait_ge(sem("mb_ready"), 2 * s + hh)
                    for k in range(4):
                        last = nc.tensor.transpose(ps[:, 0, P * k:P * (k + 1)], AS[hh][:, P * k:P * (k + 1)], ident[:, :])
                    last.then_inc(sem("mb_mm"), 1)

            half_slots(pe, tail)


_INS = ['x', 'L0_conv_P1', 'L0_conv_P3', 'L0_conv_gamma', 'L0_conv_beta', 'L1_conv_emb_W', 'L1_conv_emb_b',
        'L1_conv_mult_W', 'L1_conv_mult_b', 'L1_conv_out_W', 'L1_conv_out_b', 'L2_conv_W', 'L2_conv_b',
        'L3_conv_Wf', 'L3_conv_bf', 'L3_conv_k0', 'L3_conv_k1', 'L3_conv_k2', 'L3_conv_Wh', 'L3_conv_bh',
        'L3_conv_gamma', 'L3_conv_beta', 'L3_conv_Wp', 'L3_conv_bp']
_OUTS = [((32, 32, 32, 64), 'float32')]


def kernel(**inputs):
    import numpy as _np
    import concourse.bacc as _bacc
    from concourse import mybir as _mybir
    from concourse.bass_utils import run_bass_kernel_spmd as _run

    nc = _bacc.Bacc("TRN2", target_bir_lowering=False, num_devices=1)
    arrays, args = {}, []
    for name in _INS:
        a = _np.ascontiguousarray(inputs[name])
        arrays[f"in_{name}_dram"] = a
        args.append(nc.dram_tensor(f"in_{name}_dram", a.shape, _mybir.dt.from_np(a.dtype), kind="ExternalInput").ap())
    for i, (shape, dtype) in enumerate(_OUTS):
        dt = _mybir.dt.from_np(_np.dtype(dtype))
        args.append(nc.dram_tensor(f"out_{i}_dram", shape, dt, kind="ExternalOutput").ap())
    conv_preact_kernel(nc, *args)
    r = _run(nc, [arrays], core_ids=[0])
    return r.results[0]["out_0_dram"]
```

```python
from contextlib import ExitStack

import concourse.bass as bass
from concourse import mybir

P = 128
F32 = mybir.dt.float32
BF16 = mybir.dt.bfloat16
ALU = mybir.AluOpType
ACT = mybir.ActivationFunctionType
AX = mybir.AxisListType

B, H, W, C = 32, 32, 32, 64
BH = 2
NS = B // BH
TOK = H * W
W4 = P // H
WB = W // W4
HALF = 512
EPS_GN = 1e-5
EPS_BN = 1e-5
EPS_LN = 1e-3

XCH = 4
NCH = B // XCH
NB8 = 8
OWN_CH = 1
POOL_X1 = 2
GS = 4
NG = NS // GS
COLS = WB * B
LEVELS = 3
KERNELS = (3, 5, 7)
UCH = 8
RING = 2
NU = C // UCH
NJ = 3 * W4
UH = 2 * H - 1
WIN = H * UCH
BAND = NJ * UH * UCH
QP = 32
SUB = UCH * COLS // 1024
NSTEP = LEVELS * NU
NHS = 2 * NS
PROJ_EARLY = 4
PROJ_BEFORE = 8
STAGES = 5
PEELED = 6


def halos(l):
    if l == 0:
        return ((0, 2), (0, W4)), ((0, W4), (0, 2))
    if KERNELS[l] // 2 <= 2:
        return ((0, 2), (2, 4)), ((2, 4), (0, 2))
    return ((0, W4), (0, W4)), ((0, W4), (0, 3))


def band_parts(l):
    (n_in, n_out), (p_in, p_out) = halos(l)
    return ([(j, *n_in) for j in range(*n_out)] + [(W4 + j, 0, W4) for j in range(W4)]
            + [(2 * W4 + j, *p_in) for j in range(*p_out)])


def conv_steps(engine, step):
    per = [16 * len(band_parts(l)) for l in range(LEVELS)]
    in_pair = sum(per)
    loads = [0, 0]

    def known(l, cu, n, ready, prev):
        loads[n % 2] += per[l]
        step(l, cu, n, loads[n % 2], n % 2, ready, prev)

    known(0, 0, 0, None, None)
    known(1, 0, 1, 0, None)
    known(0, 1, 2, None, 0)
    with engine.Fori(0, (NU - 2) // 2) as it:
        for j in range(2 * LEVELS):
            l = 2 - j % LEVELS
            n = 6 * it + (3 + j)
            odd = (3 + j) % 2
            loads[odd] += per[l]
            step(l, 2 * it + (2 + j // LEVELS - l), n, in_pair * it + loads[odd], odd, n - 2, n - 3)
    loads = [x + in_pair * ((NU - 2) // 2 - 1) for x in loads]
    n = NSTEP - 3
    known(2, NU - 2, n, n - 2, n - 3)
    known(1, NU - 1, n + 1, n - 1, n - 2)
    known(2, NU - 1, n + 2, n + 1, n)


def half_slots(engine, step):
    def known(n):
        return lambda d: ((n - d) // 2, (n - d) % 2, n - d) if 0 <= n - d < NHS else None

    def looped(it, m):
        return lambda d: (it + (m - d) // 2, (m - d) % 2, 2)

    for n in range(PEELED):
        step(known(n))
    with engine.Fori(0, (NHS - PEELED) // 2) as it:
        for j in range(2):
            step(looped(it, PEELED + j))
    for n in range(NHS, NHS + STAGES - 1):
        step(known(n))


def conv_preact_kernel(nc, x, P1, P3, bn_gamma, bn_beta, emb_W, emb_b, mult_W, mult_b, out_W, out_b,
                       cW, cb, Wf, bf, k0, k1, k2, Wh, bh_, ln_gamma, ln_beta, Wp, bp, out):
    band_dram = nc.dram_tensor("band_tables", (LEVELS, NU, W4, BAND), F32, kind="Internal")

    ctx = ExitStack()
    with ctx:
        def sb(name, shape, dt=F32):
            return ctx.enter_context(nc.sbuf_tensor(name, shape, dt))

        named = {}

        def sem(name):
            if name not in named:
                named[name] = ctx.enter_context(nc.semaphore(name))
            return named[name]

        XB = sb("XB", [P, NS * TOK])
        WK = sb("WK", [P, 24 * TOK])
        RG = sb("RG", [P, RING, NJ * WIN])
        WT = sb("WT", [P, 19, P])
        WCG = sb("WCG", [P, P + 8])
        ROWB = sb("ROWB", [P, 2 * P + P + 8], BF16)
        ident = sb("ident", [P, P])
        ones = sb("ones", [P, P])
        onesb = sb("onesb", [P, P], BF16)
        pairm = sb("pairm", [P, P])
        rowm = sb("rowm", [P, P])
        small = sb("small", [P, 32])
        BC = sb("BC", [P, 24])
        st = sb("st", [P, GS, 12])
        mv = sb("mv", [P, GS, 2])
        me = sb("me", [P, 2, GS])
        gm = sb("gm", [P, 4, GS])
        TMP = sb("TMP", [P, HALF])
        me4 = sb("me4", [P, 2, NS])
        gm4 = sb("gm4", [P, 4, NS])
        sd = sb("sd", [P, 2, 8])
        rs = sb("rs", [P, 2, 8])
        vr = sb("vr", [P, 8])
        gates = sb("gates", [P, 4, COLS])
        xs = sb("xs", [P, GS, H])
        xh = sb("xh", [P, 3, GS, W])
        tt = sb("tt", [P, GS, W])
        mhalf = sb("mhalf", [P, B // 2])
        gn0 = sb("gn0", [P, 6, B // 2])

        ps = ctx.enter_context(nc.psum_tensor("ps", [P, 8, HALF], F32))

        def unit(u):
            return ps[:, 2 * u:2 * u + 2, :].rearrange("p a n -> p (a n)")

        EB, MB, OB, CB, QB, HB, LG, LB, PB, BG, BB, CB63, PB2 = 0, 6, 10, 12, 13, 14, 15, 16, 17, 18, 19, 20, 21
        WE, WM, WO, WC, WQ, WHI, CEN, WPI = 0, 6, 10, 12, 15, 16, 17, 18

        GFL = gates[:, :, :].rearrange("p l n -> p (l n)")
        SUMS = [ps[:, i, 0:B // 2] for i in range(2)]
        XA = XB[:, :].rearrange("p (b k c) -> p b k c", b=B, k=WB)
        AF = WK[:, 0:B * WB * C]
        AV = AF.rearrange("p (s k g c) -> p g s k c", g=BH, s=NS, k=WB)

        def A(b0, n, k=slice(0, WB)):
            return AV[:, b0 // NS, b0 % NS:b0 % NS + n, k, :]

        SWB = WK[:, 16384:18432]
        SWQ = WK[:, 22528:24576]
        RSTDE = SWB
        SQ = [WK[:, 18432 + 2048 * i:20480 + 2048 * i] for i in range(2)]
        MEANE = WK[:, 22528:24576]
        RGF = RG[:, :, :].rearrange("p r n -> p (r n)")
        P1N, P3N, P1T, P3T = (RGF[:, 1024 * i:1024 * (i + 1)].rearrange("p (k m) -> p k m", k=WB) for i in range(4))
        CWN = RGF[:, 4096:4096 + 3 * P].rearrange("p (t m) -> p t m", t=3)
        CWR = RGF[:, 4480:4480 + 3 * C]
        SUMA = RGF[:, 4672:4672 + B * WB].rearrange("p (b k) -> p b k", b=B)
        BAND_SB = WK[:, 0:2 * BAND].rearrange("p (l n) -> p l n", l=2)
        TAPS = (0, 9, 34, 83)
        KT = WK[:, 12096:12096 + TAPS[LEVELS] * UCH]
        ROWF = TMP[:, 0:392]
        ROWR = GFL[:, 0:392]
        meanm = GFL[:, 784:784 + P]
        ROWH = GFL[:, 392:784].bitcast(BF16).rearrange("p (a n) -> p a n", a=2)

        X1_P = [len([k for k in range(i + 1) if k % 4 == POOL_X1]) for i in range(NS)]
        X1_D = [i + 1 - X1_P[i] for i in range(NS)]

        def buf(i):
            return WK[:, 4096 * i:4096 * (i + 1)].rearrange("p (s n) -> p s n", s=GS)

        G = RGF[:, 0:4096].rearrange("p (s n) -> p s n", s=GS)
        E1, HA, HBF, SELF, K0T, K1T = (buf(i) for i in range(6))
        M, T1, Z = K0T, HBF, K1T
        HBR = HBF.rearrange("p s n -> p (s n)").rearrange("p (h s w) -> p h s w", h=H, s=GS)
        HA0 = K1T
        HBR0 = E1.rearrange("p s n -> p (s n)").rearrange("p (h s w) -> p h s w", h=H, s=GS)
        HAR = HA.rearrange("p s n -> p (s n)").rearrange("p (w s h) -> p w s h", w=W, s=GS)
        XBS = XB[:, :].rearrange("p (s n) -> p s n", s=NS)

        CTX = WK[:, 0:16384]
        G4 = K1T
        CT = [WK[:, 16384 + 2048 * l:18432 + 2048 * l] for l in range(LEVELS)]
        RSUM = WK[:, 22528:24576]
        GLOB = CT[0]

        def ctxv(b, c=C):
            return b.rearrange("p (g c n) -> p g c n", g=BH, c=c)

        MBT, QT, XO, SQT, XR, OT = ([WK[:, 18432 + 1024 * i + HALF * j:18432 + 1024 * i + HALF * (j + 1)] for j in range(2)]
                                    for i in range(6))

        def xcy(hh):
            return ps[:, 4 + 2 * hh:6 + 2 * hh, :].rearrange("p a n -> p (a n)").rearrange("p (t i m) -> p t i m", t=4, i=2)

        AS, TG, G4B = ([RGF[:, 1024 * i + HALF * j:1024 * i + HALF * (j + 1)] for j in range(2)] for i in range(3))

        block = ctx.enter_context(nc.Block())

        @block.sync
        def _(sp):
            ctx.enter_context(nc.allow_non_contiguous_dma(reason="short loads of biases and taps"))
            def store_bands(l):
                sp.wait_ge(sem("band_copied"), W4 * (l + 1))
                for w in range(W4):
                    sp.dma_start(band_dram.ap()[l, :, w, :], BAND_SB[QP * w:QP * w + NU, l % 2, :]
                                 ).then_inc(sem("band_stored0" if l == 0 else "band_stored"), 16)

            for ch in range(NCH):
                for w4 in range(W4):
                    sp.dma_start(XA[H * w4:H * (w4 + 1), XCH * ch:XCH * (ch + 1), :, :].rearrange("p b k c -> p b (k c)"),
                                 x[XCH * ch:XCH * (ch + 1), :, WB * w4:WB * (w4 + 1), :].rearrange("b h k c -> h b (k c)")
                                 ).then_inc(sem(f"x_loaded{ch}"), 16)
                if ch == NCH // 2:
                    sp.wait_ge(sem("zeroed"), 5)
                    for w4 in range(W4):
                        p = slice(H * w4, H * (w4 + 1))
                        sp.dma_start(P1N[p, :, H * w4:H * (w4 + 1)],
                                     P1[WB * w4:WB * (w4 + 1), :, :].rearrange("k o i -> o k i")).then_inc(sem("p_loaded"), 16)
                        sp.dma_start(P3N[p, :, H * w4:H * (w4 + 1)],
                                     P3[WB * w4:WB * (w4 + 1), :, :].rearrange("k o i -> o k i")).then_inc(sem("p_loaded"), 16)
                if ch == NCH - 2:
                    store_bands(0)
            store_bands(1)
            def load_weights(name, loads):
                for bh in range(BH):
                    for dst, src in loads(bh, slice(C * bh, C * (bh + 1))):
                        sp.dma_start(dst, src).then_inc(sem(name), 16)

            load_weights("early_loaded", lambda bh, p: (
                (WT[p, WPI, p], Wp),
                (CWR[p, :], cW.rearrange("o i t u -> o (i t u)")),
                (BC[p, CB:CB + 1], cb.rearrange("(c o) -> c o", o=1)),
                (BC[p, LG:LG + 1], ln_gamma.rearrange("(c o) -> c o", o=1)),
                (BC[p, LB:LB + 1], ln_beta.rearrange("(c o) -> c o", o=1)),
                (BC[p, PB:PB + 1], bp.rearrange("(c o) -> c o", o=1))))
            store_bands(2)
            for w4 in range(W4):
                p = slice(H * w4, H * (w4 + 1))
                sp.dma_start(BC[p, BG:BG + 1], bn_gamma.rearrange("(h o) -> h o", o=1)).then_inc(sem("bn_loaded"), 16)
                sp.dma_start(BC[p, BB:BB + 1], bn_beta.rearrange("(h o) -> h o", o=1)).then_inc(sem("bn_loaded"), 16)
            load_weights("row_loaded", lambda bh, p: (
                (ROWF[:, at:at + src.shape[0]],
                 bass.AP(tensor=src.tensor, offset=src.offset, ap=[[0, P], [1, src.shape[0]]]))
                for at, src in ((C * bh, emb_b[1, 1]), (P + C * bh, emb_b[2, 1]), (2 * P + C * bh, bf[C:2 * C]),
                                (3 * P + 4 * bh, bf[2 * C:2 * C + 4]))))
            load_weights("w_loaded", lambda bh, p: (
                (WT[p, WE:WE + 6, p], emb_W.rearrange("l j i o -> i (l j) o")),
                (WT[p, WM:WM + 4, p], mult_W.rearrange("l j i o -> i (l j) o")),
                (WT[p, WO:WO + 2, p], out_W.rearrange("j i o -> i j o")),
                (WT[p, WQ, p], Wf[:, 0:C]),
                (WT[p, WHI, p], Wh),
                (WCG[p, p], Wf[:, C:2 * C]), (WCG[p, P + 4 * bh:P + 4 * bh + 4], Wf[:, 2 * C:2 * C + 4]),
                (BC[p, EB:EB + 6], emb_b.rearrange("l j o -> o (l j)")),
                (BC[p, MB:MB + 4], mult_b.rearrange("l j o -> o (l j)")),
                (BC[p, OB:OB + 2], out_b.rearrange("j o -> o j")),
                (BC[p, QB:QB + 1], bf[0:C].rearrange("(c o) -> c o", o=1)),
                (BC[p, HB:HB + 1], bh_.rearrange("(c o) -> c o", o=1))))
            sp.wait_ge(sem("band_stored0"), 16 * W4)
            sp.wait_ge(sem("band_stored"), 16 * (LEVELS - 1) * W4)
            sp.wait_ge(sem("x3_ready"), NS)

            def load_bands(l, cu, n):
                slot = n % RING
                if n >= RING:
                    sp.wait_ge(sem("conv_mm"), SUB * n - SUB * (RING - 1))
                for j, w0, w1 in band_parts(l):
                    src = bass.AP(tensor=band_dram.ap().tensor,
                                  offset=((l * NU + cu) * W4 + w0) * BAND + (j * UH + H - 1) * UCH,
                                  ap=[[BAND, w1 - w0], [-UCH, H], [1, WIN]])
                    sp.dma_start(RG[H * w0:H * w1, slot, WIN * j:WIN * (j + 1)], src
                                 ).then_inc(sem(f"ring_loaded{slot}"), 16)

            order = [(l, r - l) for r in range(NU + LEVELS - 1) for l in (2, 1, 0) if 0 <= r - l < NU]
            for n, (l, cu) in enumerate(order):
                load_bands(l, cu, n)

            def store(item):
                if item(4):
                    s, hh, low = item(4)
                    sp.wait_ge(sem("ot_ready"), 2 * s + hh + 1)
                    for bh in range(BH):
                        dst = out.rearrange("(g s) h (a q t) c -> g s a h q (t c)", g=BH, a=2, q=W4)
                        sp.dma_start(dst[bh, bass.ds(s, 1), hh, :, :, :].rearrange("o h q n -> (o h) q n"),
                                     OT[hh][:, 256 * bh:256 * (bh + 1)]).then_inc(sem(f"stored{hh}"), 16)

            half_slots(sp, store)
            for j in range(2):
                sp.wait_ge(sem(f"stored{j}"), NS * 16 * BH)

        @block.gpsimd
        def _(pool):
            nc.gpsimd.memset(ident[:, :], 0.0).then_inc(sem("ident_zero"), 1)
            pool.wait_ge(sem("ident_zero"), 1)
            nc.gpsimd.affine_select(out=ident[:, :], in_=ident[:, :], compare_op=ALU.not_equal, fill=1.0, base=0,
                                    pattern=[[-1, P]], channel_multiplier=1).then_inc(sem("ident_set"), 1)
            nc.gpsimd.memset(mhalf[:, :], -0.5).then_inc(sem("mhalf_set"), 1)
            nc.gpsimd.memset(WT[:, 0:CEN, :], 0.0).then_inc(sem("zeroed"), 1)
            nc.gpsimd.memset(WT[:, WPI, :], 0.0).then_inc(sem("zeroed"), 1)
            nc.gpsimd.memset(WCG[:, :], 0.0).then_inc(sem("zeroed"), 1)
            nc.gpsimd.memset(RGF[:, 0:2048], 0.0).then_inc(sem("zeroed"), 1)
            nc.gpsimd.memset(CWN, 0.0).then_inc(sem("zeroed"), 1)
            for l in range(2):
                nc.gpsimd.memset(BAND_SB[:, l, :], 0.0).then_inc(sem("band_zero"), 1)
            pool.wait_ge(sem("taps_loaded"), 16 * LEVELS * W4)
            pool.wait_ge(sem("band_zero"), 2)
            for l, kk in enumerate(KERNELS):
                r = kk // 2
                if l == 2:
                    pool.wait_ge(sem("band_stored0"), 16 * W4)
                    nc.gpsimd.memset(BAND_SB[:, l % 2, :], 0.0).then_inc(sem("band_zero2"), 1)
                    pool.wait_ge(sem("band_zero2"), 1)
                taps = KT[:, UCH * TAPS[l]:UCH * TAPS[l + 1]].rearrange("p (a b c) -> p b a c", a=kk, b=kk)
                for w in range(W4):
                    p = slice(QP * w, QP * w + NU)
                    table = BAND_SB[p, l % 2, :].rearrange("p (j u c) -> p j u c", j=NJ, u=UH)
                    nc.gpsimd.tensor_copy(table[:, w + W4 - r:w + W4 + r + 1, H - 1 - r:H + r, :], taps[p]
                                          ).then_inc(sem("band_copied"), 1)
                    pool.wait_ge(sem("band_copied"), W4 * l + w + 1)
            pool.wait_ge(sem("mhalf_set"), 1)
            pool.wait_ge(sem("var0_ready"), 1)
            nc.gpsimd.tensor_tensor(gn0[:, 3, :], gn0[:, 2, :], mhalf[:, :], ALU.pow).then_inc(sem("rstd0"), 1)
            for ch in range(OWN_CH, NCH):
                pool.wait_ge(sem("meane_ready"), 1 + ch // 4)
                b = slice(XCH * ch, XCH * (ch + 1))
                m_b = MEANE.rearrange("p (b o c) -> p b o c", b=B, o=1)[:, b].to_broadcast([P, XCH, WB, C])
                pool.wait_ge(sem("band_stored"), 16 * (LEVELS - 1) * W4)
                nc.gpsimd.tensor_tensor(A(XCH * ch, XCH), XA[:, b], m_b, ALU.subtract).then_inc(sem("centred"), 1)
            pool.wait_ge(sem("bnvar_ready"), 1)
            nc.gpsimd.tensor_tensor(small[:, 4:5], small[:, 3:4], mhalf[:, 0:1], ALU.pow).then_inc(sem("bnrstd"), 1)
            for i in range(POOL_X1, NS, 4):
                pool.wait_ge(sem("bn_applied"), i + 1)
                v = AF[:, 1024 * i:1024 * (i + 1)].rearrange("p (k g c) -> p k g c", k=WB, g=BH)
                nc.gpsimd.tensor_tensor(v, v, XA.rearrange("p (g s) k c -> p s k g c", g=BH)[:, i], ALU.add
                                        ).then_inc(sem("x1_pool"), 1)
                pool.wait_ge(sem("x1_pool"), i // 4 + 1)
            def norm_pow(n):
                pool.wait_ge(sem("gnvar"), n)
                nc.gpsimd.tensor_tensor(gm[:, 3, :], gm[:, 2, :], mhalf[:, 0:GS], ALU.pow
                                        ).then_inc(sem("gnrstd"), 1)

            with pool.Fori(0, NG - 1) as g:
                for n in range(2):
                    norm_pow(2 * g + n + 1)
            norm_pow(2 * NG - 1)
            for n, c in enumerate((slice(0, NS - GS), slice(NS - GS, NS))):
                if n == 1:
                    norm_pow(2 * NG)
                pool.wait_ge(sem("gnvar4"), n + 1)
                nc.gpsimd.tensor_tensor(gm4[:, 3, c], gm4[:, 2, c], mhalf[:, c], ALU.pow).then_inc(sem("gnrstd4"), 1)
            pool.wait_ge(sem("gated"), NSTEP)
            pool.wait_ge(sem("glob_out"), 2)
            gl = GLOB.rearrange("p (g c s) -> p g c s", g=BH, c=C)
            gt = gates[:, 3, :].rearrange("p (g k s) -> p k g s", g=BH, k=WB)
            al = CTX.rearrange("p (g c k s) -> p k g c s", g=BH, c=C, k=WB)

            def global_context(item):
                if item(0):
                    s, hh, low = item(0)
                    t = TG[hh].rearrange("p (k g c) -> p k g c", k=4, g=BH)
                    one = bass.ds(s, 1)
                    g_b = gl[:, :, :, one].rearrange("p g c o -> p o g c").to_broadcast([P, 4, BH, C])
                    t_b = gt[:, 4 * hh:4 * hh + 4, :, one].to_broadcast([P, 4, BH, C])
                    nc.gpsimd.tensor_tensor(t, g_b, t_b, ALU.mult).then_inc(sem("tg_ready"), 1)
                    pool.wait_ge(sem("tg_ready"), 2 * s + hh + 1)
                    if low >= 2:
                        pool.wait_ge(sem("mb_mm"), 2 * s + hh - 1)
                    nc.gpsimd.tensor_tensor(AS[hh].rearrange("p (k g c) -> p k g c", k=4, g=BH), t,
                                            al[:, 4 * hh:4 * hh + 4, :, :, one].rearrange("p k g c o -> p k g (c o)"),
                                            ALU.add).then_inc(sem("as_ready"), 1)
                    pool.wait_ge(sem("as_ready"), 2 * s + hh + 1)

            half_slots(pool, global_context)

        @block.scalar
        def _(act):
            for l, (kk, k) in enumerate(zip(KERNELS, (k0, k1, k2))):
                for w in range(W4):
                    src = bass.AP(tensor=k.tensor, offset=k.offset + (kk * kk - 1) * C,
                                  ap=[[UCH, NU], [-C, kk * kk], [1, UCH]])
                    act.dma_start(KT[QP * w:QP * w + NU, UCH * TAPS[l]:UCH * TAPS[l + 1]].rearrange("p (t c) -> p t c", c=UCH),
                                  src).then_inc(sem("taps_loaded"), 16)
            for ch in range(NCH):
                act.wait_ge(sem(f"x_loaded{ch}"), 16 * W4)
                if ch >= 2:
                    act.wait_ge(sem("sq_used"), ch - 1)
                nc.scalar.activation(SQ[ch % 2], XA[:, XCH * ch:XCH * (ch + 1), :, :].rearrange("p b k c -> p (b k c)"),
                                     ACT.Square).then_inc(sem("sq_ready"), 1)
            act.wait_ge(sem("pt_mm"), 1)
            nc.scalar.activation(P1T.rearrange("p k m -> p (k m)"), unit(1), ACT.Copy).then_inc(sem("pt_ready"), 1)
            nc.scalar.activation(P3T.rearrange("p k m -> p (k m)"), unit(2), ACT.Copy, scale=0.1 / C
                                 ).then_inc(sem("pt_ready"), 1)
            for i, dst in enumerate((MEANE, RSTDE)):
                for j in range(2):
                    act.wait_ge(sem("spread_mm"), 2 * i + j + 1)
                    nc.scalar.activation(dst[:, 1024 * j:1024 * (j + 1)], unit((2 + j, j)[i]), ACT.Copy
                                         ).then_inc(sem("meane_ready" if i == 0 else "rstde_ready"), 1)
            for n in range(16):
                b8, k = n // 4, 2 * (n % 4)
                act.wait_ge(sem("relu_mm"), n + 1)
                r0 = A(NB8 * b8, NB8, slice(k, k + 2))
                nc.scalar.activation(r0.rearrange("p b k c -> p k b c"),
                                     unit(n % 4).rearrange("p (k b c) -> p k b c", k=2, b=NB8), ACT.Relu,
                                     accum_out=xs[:, 0, n:n + 1]).then_inc(sem("relu_done"), 1)
                act.wait_ge(sem("relu_done"), n + 1)
                nc.scalar.activation(unit(n % 4).rearrange("p (k b c) -> p k b c", k=2, b=NB8),
                                     r0.rearrange("p b k c -> p k b c"), ACT.Square,
                                     accum_out=xs[:, 1, n:n + 1]).then_inc(sem("relu_sq"), 1)
            act.wait_ge(sem("bn_coef"), 1)

            def batch_norm(slots):
                for i in slots:
                    v = AF[:, 1024 * i:1024 * (i + 1)]
                    nc.scalar.activation(v, v, ACT.Identity, bias=small[:, 6:7], scale=small[:, 5:6]
                                         ).then_inc(sem("bn_applied"), 1)

            def to_channels(slots):
                for s in slots:
                    act.wait_ge(sem("xt_mm"), s + 1)
                    act.wait_ge(sem("x1_ready"), X1_D[min(2 * s + 1, NS - 1)])
                    act.wait_ge(sem("x1_pool"), X1_P[min(2 * s + 1, NS - 1)])
                    nc.scalar.activation(XBS[:, s, :].rearrange("p (h a k) -> p k a h", h=H, a=W4),
                                         unit(s % 4).rearrange("p (k a h) -> p k a h", k=WB, a=W4),
                                         ACT.Copy).then_inc(sem("xt_out_a"), 1)

            batch_norm(range(0, NS // 2))
            to_channels((1, 3))
            batch_norm(range(NS // 2, NS))

            def silu(stage, g, dst, bias=None, free=None, src=lambda v: v):
                for u in range(GS):
                    act.wait_ge(sem(stage + "_mm"), GS * g + u + 1)
                    if free is not None and (u == 0 or free[1] == "slot"):
                        act.wait_ge(sem(free[0]), free[2] + (u + 1 if free[1] == "slot" else GS))
                    nc.scalar.activation(dst(u), src(unit(u)), ACT.Silu,
                                         bias=0.0 if bias is None else BC[:, bias:bias + 1]
                                         ).then_inc(sem(stage + "_out"), 1)

            def slot(b):
                return lambda u: b[:, u, :]

            def embed_silu(g):
                silu("s1", g, slot(HA), EB + 0)
                silu("k1", g, lambda u: HBR[:, :, u, :], EB + 2, src=lambda v: v.rearrange("p (h w) -> p h w", h=H),
                     free=("x2_ready", "all", GS * (g - 1)))
                silu("s2", g, slot(SELF), EB + 1)
                silu("l1", g, lambda u: HAR[:, :, u, :], EB + 4, src=lambda v: v.rearrange("p (h w) -> p w h", h=H))
                silu("k2", g, slot(K0T))

            def products_silu(g, more):
                silu("l2", g, slot(K1T))
                for m in range(2):
                    silu(f"m{m}a", g, slot(HA), MB + 2 * m)
                    silu(f"m{m}b", g, slot(T1), MB + 2 * m + 1, free=None if m == 0 else ("res0", "slot", GS * g))
                silu("oa", g, slot(HA), OB)
                silu("ob", g, slot(T1), OB + 1, free=("res1", "slot", GS * g))
                if more:
                    embed_silu(g + 1)
                else:
                    project_out(0, PROJ_BEFORE)
                act.wait_ge(sem("t_mm"), g + 1)
                nc.scalar.activation(tt[:, :, :].rearrange("p s w -> p (s w)"), ps[:, 7, 0:GS * W], ACT.Identity,
                                     bias=BC[:, CB63:CB63 + 1]).then_inc(sem("t_out"), 1)
                if not more:
                    project_out(PROJ_BEFORE, NS)

            def project_out(s0, s1):
                if s0 == 0:
                    act.wait_ge(sem("x2_ready"), GS * NG)
                for n in range(2 * s0, 2 * s1):
                    s, k = n // 2, 4 * (n % 2)
                    act.wait_ge(sem("proj_mm"), n + 1)
                    src = unit(n % 4).rearrange("p (k m) -> p k m", k=4)
                    for bh in range(BH):
                        nc.scalar.activation(
                            CTX.rearrange("p (g c k s) -> p g k c s", g=BH, c=C, k=WB)[:, bh, k:k + 4, :, s],
                            src[:, :, C * bh:C * (bh + 1)], ACT.Copy)
                    nc.scalar.activation(
                        gates[:, :, :].rearrange("p l (g k s) -> p k g l s", k=WB, g=BH)[:, k:k + 4, :, :, s],
                        src[:, :, P:P + 8].rearrange("p k (g l) -> p k g l", g=BH), ACT.Copy).then_inc(sem("proj_out"), 1)

            act.wait_ge(sem("w_loaded"), 16 * 12 * BH)
            silu("s1", 0, slot(HA0), EB + 0)
            silu("k1", 0, lambda u: HBR0[:, :, u, :], EB + 2, src=lambda v: v.rearrange("p (h w) -> p h w", h=H))
            to_channels((5, 7))
            silu("k2", 0, slot(K0T))
            to_channels((9, 11, 13, 15))
            silu("s2", 0, slot(SELF), EB + 1)
            silu("l1", 0, lambda u: HAR[:, :, u, :], EB + 4, src=lambda v: v.rearrange("p (h w) -> p w h", h=H))
            with act.Fori(0, NG - 1) as g:
                products_silu(g, True)
            products_silu(NG - 1, False)

            def gelu(l, cu, n, loads, odd, ready, prev):
                for j in range(SUB):
                    act.wait_ge(sem("conv_mm"), SUB * n + j + 1)
                    if prev is not None and j == 0:
                        act.wait_ge(sem("gated"), prev + 1)
                    c = UCH // SUB
                    nc.scalar.activation(ctxv(CT[l], UCH)[:, :, c * j:c * (j + 1), :].rearrange("p g c n -> p c g n"),
                                         unit(2 * odd + j).rearrange("p (c g n) -> p c g n", c=c, g=BH), ACT.Gelu
                                         ).then_inc(sem("conv_out"), 1)

            conv_steps(act, gelu)
            act.wait_ge(sem("glob_mm"), 1)
            act.wait_ge(sem("gated"), NSTEP)
            for j in range(2):
                nc.scalar.activation(GLOB[:, 1024 * j:1024 * (j + 1)], unit(j), ACT.Gelu, scale=1.0 / TOK
                                     ).then_inc(sem("glob_out"), 1)

            def tail(item):
                if item(2):
                    s, hh, low = item(2)
                    act.wait_ge(sem("q_mm"), 2 * s + hh + 1)
                    if low >= 2:
                        act.wait_ge(sem("xo_ready"), 2 * s + hh - 1)
                    nc.scalar.activation(QT[hh], ps[:, 1, :], ACT.Identity, bias=BC[:, QB:QB + 1]).then_inc(sem("q_ready"), 1)
                if item(1):
                    s, hh, low = item(1)
                    act.wait_ge(sem("mb_mm"), 2 * s + hh + 1)
                    if low >= 2:
                        act.wait_ge(sem("mod_mm"), 2 * s + hh - 1)
                    nc.scalar.activation(MBT[hh].rearrange("p (h k q) -> p k q h", h=H, q=W4),
                                         ps[:, 0, :].rearrange("p (k q h) -> p k q h", k=4, h=H),
                                         ACT.Copy).then_inc(sem("mb_ready"), 1)
                if item(3):
                    s, hh, low = item(3)
                    if low >= 2:
                        act.wait_ge(sem("xres_mm"), 2 * s + hh - 1)
                    xg = XBS[:, bass.ds(s, 1), :].rearrange("p o (h a w) -> p (o h) a w", h=H, a=2)[:, :, hh, :]
                    nc.scalar.activation(XR[hh].rearrange("p (h w) -> p h w", h=H), xg, ACT.Identity,
                                         bias=BC[:, PB2:PB2 + 1]).then_inc(sem("xr_ready"), 1)
                    act.wait_ge(sem("xcy_mm"), 2 * s + hh + 1)
                    if low >= 1:
                        act.wait_ge(sem("var_ready"), 2 * s + hh)
                    nc.scalar.activation(SQT[0].rearrange("p (t m) -> p t m", t=4), xcy(hh)[:, :, 0, :], ACT.Square
                                         ).then_inc(sem("sqt_ready"), 1)
                    act.wait_ge(sem("var_ready"), 2 * s + hh + 1)
                    if low >= 2:
                        act.wait_ge(sem("rs_ready"), 2 * s + hh - 1)
                    nc.scalar.activation(sd[:, hh, :], vr[:, :], ACT.Sqrt, bias=BC[:, 22:23], scale=1.0 / C
                                         ).then_inc(sem("sd_ready"), 1)

            half_slots(act, tail)

        @block.vector
        def _(dve):
            count = [0]

            def link(ins):
                count[0] += 1
                ins.then_inc(sem("dve_chain"), 1)
                dve.wait_ge(sem("dve_chain"), count[0])

            def take_wait(column):
                nc.vector.memset(small[:, column:column + 1], 0.0)

            TS, TT, STT = nc.vector.tensor_scalar, nc.vector.tensor_tensor, nc.vector.scalar_tensor_tensor
            cp = nc.vector.tensor_copy
            nc.vector.memset(ones[:, :], 1.0).then_inc(sem("ones_set"), 1)
            nc.vector.memset(onesb[:, :], 1.0).then_inc(sem("ones_set"), 1)
            nc.vector.memset(BC[:, 22:23], EPS_LN).then_inc(sem("eps_set"), 1)
            link(nc.vector.memset(meanm[:, :], 0.0))
            link(nc.vector.memset(meanm[0:C, 0:C], 1.0 / C))
            nc.vector.memset(meanm[C:P, C:P], 1.0 / C).then_inc(sem("dve_chain"), 1)
            count[0] += 1
            dve.wait_ge(sem("ident_set"), 1)
            dve.wait_ge(sem("dve_chain"), count[0])
            TT(WT[:, CEN, :], ident[:, :], meanm[:, :], ALU.subtract).then_inc(sem("mats_set"), 1)
            link(nc.vector.tensor_reduce(xh[:, 0, 0:2, :].rearrange("p a b -> p (a b)"),
                                         ident[:, :].rearrange("p (g j) -> p g j", j=2), AX.X, ALU.add))
            TS(pairm[:, :].rearrange("p (g j) -> p g j", j=2),
               xh[:, 0, 0:2, :].rearrange("p a (b o) -> p (a b) o", o=1).to_broadcast([P, 64, 2]), 0.5, None, ALU.mult
               ).then_inc(sem("mats_set"), 1)
            link(nc.vector.tensor_reduce(xh[:, 1, 0, :], ident[:, :].rearrange("p (a h) -> p h a", a=W4), AX.X, ALU.add))
            cp(rowm[:, :].rearrange("p (a h) -> p a h", a=W4), xh[:, 1, 0:1, :].to_broadcast([P, W4, H])
               ).then_inc(sem("mats_set"), 1)
            swb = SWB.rearrange("p (b c) -> p b c", b=B)
            for n in range(NCH + 1):
                if n < NCH:
                    ch = n
                    dve.wait_ge(sem(f"x_loaded{ch}"), 16 * W4)
                    nc.vector.tensor_reduce(swb[:, XCH * ch:XCH * (ch + 1), :],
                                            XA[:, XCH * ch:XCH * (ch + 1), :, :].rearrange("p b k c -> p b c k"),
                                            AX.X, ALU.add).then_inc(sem("swb_ready"), 1)
                if n >= 1:
                    ch = n - 1
                    dve.wait_ge(sem("sq_ready"), ch + 1)
                    nc.vector.tensor_reduce(SWQ[:, XCH * C * ch:XCH * C * (ch + 1)].rearrange("p (b c) -> p b c", b=XCH),
                                            SQ[ch % 2].rearrange("p (b k c) -> p b c k", b=XCH, k=WB),
                                            AX.X, ALU.add).then_inc(sem("sq_used"), 1)
            dve.wait_ge(sem("sum0_mm"), 1)
            for i in range(2):
                ins = TS(gn0[:, i, :], SUMS[i], 1.0 / TOK, None, ALU.mult)
            ins.then_inc(sem("mean0_ready"), 1)
            dve.wait_ge(sem("coef0_mm"), 1)
            link(cp(gn0[:, 4:6, :], ps[:, 0, 0:B].rearrange("p (a j) -> p a j", a=2)))
            link(TT(gn0[:, 2, :], gn0[:, 4, :], gn0[:, 4, :], ALU.mult))
            link(TT(gn0[:, 2, :], gn0[:, 5, :], gn0[:, 2, :], ALU.subtract))
            TS(gn0[:, 2, :], gn0[:, 2, :], 0.0, EPS_GN, ALU.max, ALU.add).then_inc(sem("var0_ready"), 1)
            for i, v in enumerate((4, 3)):
                if v == 3:
                    dve.wait_ge(sem("rstd0"), 1)
                for j in range(2):
                    c = slice(8 * j, 8 * (j + 1))
                    TT(SQ[i][:, 1024 * j:1024 * (j + 1)].rearrange("p (j n) -> p j n", n=P),
                       ident[:, :].rearrange("p (o n) -> p o n", o=1).to_broadcast([P, 8, P]),
                       gn0[:, v, c].rearrange("p (j o) -> p j o", o=1).to_broadcast([P, 8, P]), ALU.mult
                       ).then_inc(sem("diag_ready"), 1)
            dve.wait_ge(sem("band_stored"), 16 * (LEVELS - 1) * W4)
            for ch in range(NCH):
                b = slice(XCH * ch, XCH * (ch + 1))
                m_b = MEANE.rearrange("p (b o c) -> p b o c", b=B, o=1)[:, b].to_broadcast([P, XCH, WB, C])
                r_b = RSTDE.rearrange("p (b o c) -> p b o c", b=B, o=1)[:, b].to_broadcast([P, XCH, WB, C])
                a = A(XCH * ch, XCH)
                if ch < OWN_CH:
                    dve.wait_ge(sem("meane_ready"), 1 + ch // 4)
                    link(TT(a, XA[:, b], m_b, ALU.subtract))
                else:
                    dve.wait_ge(sem("centred"), ch - OWN_CH + 1)
                dve.wait_ge(sem("rstde_ready"), 1 + ch // 4)
                link(TT(a, a, r_b, ALU.mult))
                nc.vector.tensor_reduce(SUMA[:, b, :], a, AX.X, ALU.add).then_inc(sem("a_ready"), 1)
            dve.wait_ge(sem("row_loaded"), 16 * 8)
            link(nc.vector.memset(ROWB[:, :], 0.0))
            link(TS(ROWR, ROWF, 1.0 / 32, None, ALU.mult))
            link(cp(ROWB[0:32, :], ROWR[0:32, :]))
            link(cp(ROWH[:, 0, :], ROWR))
            link(TT(ROWR, ROWR, ROWH[:, 0, :], ALU.subtract))
            link(cp(ROWB[32:64, :], ROWR[32:64, :]))
            link(cp(ROWH[:, 1, :], ROWR))
            link(TT(ROWR, ROWR, ROWH[:, 1, :], ALU.subtract))
            cp(ROWB[64:96, :], ROWR[64:96, :]).then_inc(sem("rowb_set"), 1)
            dve.wait_ge(sem("early_loaded"), 16 * 6 * BH)
            for bh in range(BH):
                p = slice(C * bh, C * (bh + 1))
                cp(CWN[p, :, p], CWR[p, :].rearrange("p (i t) -> p t i", t=3)).then_inc(sem("cwn_ready"), 1)
            dve.wait_ge(sem("bn_loaded"), 16 * 2 * W4)
            dve.wait_ge(sem("relu_sq"), 16)
            link(nc.vector.tensor_reduce(small[:, 0:2], xs[:, 0:2, 0:16], AX.X, ALU.add))
            nc.vector.tensor_copy(small[:, 8:10], small[:, 0:2]).then_inc(sem("bnsum_ready"), 1)
            dve.wait_ge(sem("bn_mm"), 1)
            nbn = B * W * C
            link(TS(small[:, 0:2], ps[:, 0, 0:2], 1.0 / nbn, None, ALU.mult))
            link(TT(small[:, 2:3], small[:, 0:1], small[:, 0:1], ALU.mult))
            link(TT(small[:, 3:4], small[:, 1:2], small[:, 2:3], ALU.subtract))
            TS(small[:, 3:4], small[:, 3:4], 0.0, EPS_BN, ALU.max, ALU.add).then_inc(sem("bnvar_ready"), 1)
            dve.wait_ge(sem("bnrstd"), 1)
            link(TT(small[:, 5:6], small[:, 4:5], BC[:, BG:BG + 1], ALU.mult))
            link(TT(small[:, 7:8], small[:, 5:6], small[:, 0:1], ALU.mult))
            TT(small[:, 6:7], BC[:, BB:BB + 1], small[:, 7:8], ALU.subtract).then_inc(sem("bn_coef"), 1)
            scale = (H + W - 2) ** 0.5
            dve.wait_ge(sem("pt2_mm"), 1)
            TS(WT[:, WC:WC + 3, :].rearrange("p t m -> p (t m)"), ps[:, 6, 0:3 * P], 1.0 / scale, None, ALU.mult
               ).then_inc(sem("bc_ready"), 1)
            TS(BC[:, CB63:CB63 + 1], BC[:, CB:CB + 1], (H + W - 1) / scale, None, ALU.mult).then_inc(sem("bc_ready"), 1)
            dve.wait_ge(sem("pb_mm"), 1)
            TT(BC[:, PB2:PB2 + 1], ps[:, 7, 0:1], BC[:, PB:PB + 1], ALU.add).then_inc(sem("bc_ready"), 1)
            TS(WT[:, WPI, :], WT[:, WPI, :], BC[:, LG:LG + 1], None, ALU.mult).then_inc(sem("bc_ready"), 1)
            dve.wait_ge(sem("wpc_mm"), 1)
            cp(WT[:, WPI, :], ps[:, 5, 0:P]).then_inc(sem("bc_ready"), 1)

            def residual1(slots):
                for i in slots:
                    if i % 4 == POOL_X1:
                        continue
                    dve.wait_ge(sem("bn_applied"), i + 1)
                    v = AF[:, 1024 * i:1024 * (i + 1)].rearrange("p (k g c) -> p k g c", k=WB, g=BH)
                    TT(v, v, XA.rearrange("p (g s) k c -> p s k g c", g=BH)[:, i], ALU.add).then_inc(sem("x1_ready"), 1)

            def to_channels(slots):
                for s in slots:
                    dve.wait_ge(sem("xt_mm"), s + 1)
                    dve.wait_ge(sem("x1_ready"), X1_D[min(2 * s + 1, NS - 1)])
                    dve.wait_ge(sem("x1_pool"), X1_P[min(2 * s + 1, NS - 1)])
                    cp(XBS[:, s, :].rearrange("p (h a k) -> p k a h", h=H, a=W4),
                       unit(s % 4).rearrange("p (k a h) -> p k a h", k=WB, a=W4)).then_inc(sem("xt_out_d"), 1)

            residual1(range(0, NS // 2))
            to_channels((0, 2))
            dve.wait_ge(sem("xt_out_a"), 2)
            dve.wait_ge(sem("xt_out_d"), 2)

            def chain(name, base):
                n = [0]

                def lk(ins):
                    n[0] += 1
                    ins.then_inc(sem(name), 1)
                    dve.wait_ge(sem(name), base + n[0])

                return lk, n

            def slot_stats(first, s):
                take_wait(20 + s)
                for j in range(2):
                    nc.vector.bn_stats(st[:, s, 6 * j:6 * j + 6],
                                       XBS[:, bass.ds(first + s, 1), HALF * j:HALF * (j + 1)].rearrange("p o n -> p (o n)")
                                       ).then_inc(sem("bn_stats"), 1)

            def norm_stats(first, lk, stat_count, to, ready):
                for s in range(GS):
                    slot_stats(first, s)
                aggregate(lk, stat_count, to, ready)

            def aggregate(lk, stat_count, to, ready):
                dve.wait_ge(sem("bn_stats"), stat_count)
                take_wait(31)
                for s in range(GS):
                    ins = nc.vector.bn_aggr(mv[:, s, :], st[:, s, :])
                lk(ins)
                lk(cp(to[:, 0, :], mv[:, :, 0]))
                lk(TT(to[:, 1, :], to[:, 0, :], to[:, 0, :], ALU.mult))
                TT(to[:, 1, :], to[:, 1, :], mv[:, :, 1], ALU.add).then_inc(sem(ready), 1)

            def norm_factors(lk, averages, gmv, var):
                lk(cp(gmv[:, 0:2, :], averages))
                lk(TT(gmv[:, 2, :], gmv[:, 0, :], gmv[:, 0, :], ALU.mult))
                lk(TT(gmv[:, 1, :], gmv[:, 1, :], gmv[:, 2, :], ALU.subtract))
                TS(gmv[:, 2, :], gmv[:, 1, :], 0.0, EPS_GN, ALU.max, ALU.add).then_inc(sem(var), 1)

            def averages(bank, n):
                return ps[:, bank, 0:2 * n].rearrange("p (a s) -> p a s", a=2)

            def norm_apply(first, n, dst, ready):
                dve.wait_ge(sem("gnrstd"), n)
                for s in range(GS):
                    TS(dst(s), XBS[:, bass.ds(first + s, 1), :].rearrange("p o n -> p (o n)"), gm[:, 0, s:s + 1],
                       gm[:, 3, s:s + 1], ALU.subtract, ALU.mult).then_inc(sem(ready), 1)

            def norm4_apply(s0, s1):
                for s in range(s0, s1):
                    if s >= GS:
                        dve.wait_ge(sem("proj_mm"), 2 * (s - GS) + 2)
                    TS(G4[:, s % GS, :].rearrange("p (k q h) -> p h k q", k=WB, h=H),
                       XBS[:, s, :].rearrange("p (h k q) -> p h k q", h=H, k=WB), gm4[:, 0, s:s + 1],
                       gm4[:, 3, s:s + 1], ALU.subtract, ALU.mult).then_inc(sem("g4_ready"), 1)

            def slots(b):
                return lambda s: b[:, s, :]

            def layers(g, lk, more, stat_count):
                first = g * GS
                nth = 2 * g + 2 if more else 2 * NG - 1
                if more:
                    norm_stats(first + GS, lk, stat_count + 2 * GS, me[:, :, :], "stats_ready")
                for u in range(GS):
                    dve.wait_ge(sem("ein_mm"), GS * g + u + 1)
                    e1 = E1.rearrange("p s n -> p (s n)").rearrange("p (j q) -> p q j", j=W)
                    cp(e1[:, 32 * u:32 * (u + 1), :], unit(u).rearrange("p (q j) -> p q j", j=W)
                       ).then_inc(sem("ein_out"), 1)
                if more:
                    dve.wait_ge(sem("coef_mm"), nth)
                    norm_factors(lk, averages(7, GS), gm[:, :, :], "gnvar")
                else:
                    dve.wait_ge(sem("coef4_mm"), 1)
                    norm_factors(lk, averages(7, NS - GS), gm4[:, :, 0:NS - GS], "gnvar4")
                for u in range(GS):
                    dve.wait_ge(sem("tr_mm"), GS * g + u + 1)
                    m = M.rearrange("p s (i j) -> p j s i", i=H)
                    cp(m[:, 8 * u:8 * (u + 1), :, :], unit(u).rearrange("p (j s i) -> p j s i", j=8, s=GS)
                       ).then_inc(sem("tr_out"), 1)
                if more:
                    norm_apply(first + GS, nth, slots(G), "g_ready")
                else:
                    dve.wait_ge(sem("gnrstd4"), 1)
                    norm4_apply(0, PROJ_EARLY)
                for u in range(GS):
                    dve.wait_ge(sem("m0b_out"), GS * g + u + 1)
                    TT(M[:, u, :], M[:, u, :], T1[:, u, :], ALU.add).then_inc(sem("res0"), 1)
                for u in range(GS):
                    dve.wait_ge(sem("m1b_out"), GS * g + u + 1)
                    dve.wait_ge(sem("res0"), GS * g + u + 1)
                    TT(M[:, u, :], M[:, u, :], T1[:, u, :], ALU.add).then_inc(sem("res1"), 1)
                    dve.wait_ge(sem("res1"), GS * g + u + 1)
                    TT(M[:, u, :], M[:, u, :], SELF[:, u, :], ALU.mult).then_inc(sem("z1_ready"), 1)
                for u in range(GS):
                    xg = XBS[:, bass.ds(first + u, 1), :].rearrange("p o n -> p (o n)")
                    dve.wait_ge(sem("ob_out"), GS * g + u + 1)
                    lk(TT(M[:, u, :], M[:, u, :], T1[:, u, :], ALU.add))
                    TT(xg, xg, M[:, u, :], ALU.add).then_inc(sem("x2_ready"), 1)
                dve.wait_ge(sem("x2_ready"), GS * g + GS)
                nth = 2 * g + 3 if more else 2 * NG
                stat_count = stat_count + (4 * GS if more else 2 * GS)
                G3, z3 = (E1, Z) if more else (G, M)
                norm_stats(first, lk, stat_count, me[:, :, :], "stats_ready")
                if not more:
                    norm4_apply(4, 6)
                dve.wait_ge(sem("coef_mm"), nth)
                norm_factors(lk, averages(7 if more else 0, GS), gm[:, :, :], "gnvar")
                norm_apply(first, nth, slots(G3), "g3_ready")
                if not more:
                    norm4_apply(6, 8)
                dve.wait_ge(sem("g3_ready"), GS * g + GS)
                g4 = G3.rearrange("p s (h w) -> p s h w", h=H)
                for u in range(GS):
                    nc.vector.tensor_reduce(xh[:, 1, u, :], g4[:, u].rearrange("p h w -> p w h"), AX.X, ALU.add)
                    ins = nc.vector.tensor_reduce(xs[:, u, :], g4[:, u], AX.X, ALU.add)
                lk(ins)
                TT(xh[:, 0], xh[:, 1], g4[:, :, H - 1, :], ALU.subtract).then_inc(sem("xh_ready"), 1)
                TT(xh[:, 2], xh[:, 1], g4[:, :, 0, :], ALU.subtract).then_inc(sem("xh_ready"), 1)
                if not more:
                    norm4_apply(8, PROJ_BEFORE)
                for u in range(GS):
                    TT(z3[:, u, :].rearrange("p (h w) -> p h w", h=H),
                       xs[:, u, :].rearrange("p (h o) -> p h o", o=1).to_broadcast([P, H, W]), g4[:, u], ALU.subtract
                       ).then_inc(sem("z_ready"), 1)
                dve.wait_ge(sem("t_out"), g + 1)
                dve.wait_ge(sem("xh_ready"), 2 * g + 2)
                dve.wait_ge(sem("z_ready"), GS * g + GS)
                for u in range(GS):
                    ins = TT(g4[:, u], g4[:, u], tt[:, u:u + 1, :].to_broadcast([P, H, W]), ALU.add)
                lk(ins)
                if not more:
                    norm4_apply(PROJ_BEFORE, NS - GS)
                for u in range(GS):
                    dve.wait_ge(sem("y_mm"), GS * g + u + 1)
                    TT(G3[:, u, :], unit(u), G3[:, u, :], ALU.add).then_inc(sem("y_out"), 1)
                    dve.wait_ge(sem("y_out"), GS * g + GS + u + 1)
                    xg = XBS[:, bass.ds(first + u, 1), :].rearrange("p o n -> p (o n)")
                    STT(out=xg, in0=G3[:, u, :], scalar=0.0, in1=xg, op0=ALU.max, op1=ALU.add).then_inc(sem("x3_ready"), 1)
                    dve.wait_ge(sem("x3_ready"), GS * g + u + 1)
                    slot_stats(first, u)
                aggregate(lk, stat_count + 2 * GS, me4[:, :, bass.ds(first, GS)], "stats4_ready")

            lk, _ = chain("chain_first", 0)
            norm_stats(0, lk, 2 * GS, me[:, :, :], "stats_ready")
            dve.wait_ge(sem("coef_mm"), 1)
            norm_factors(lk, averages(0, GS), gm[:, :, :], "gnvar")
            norm_apply(0, 1, slots(G), "g_ready")
            residual1(range(NS // 2, NS))
            to_channels(range(4, NS, 2))
            dve.wait_ge(sem("xt_out_a"), NS // 2)
            dve.wait_ge(sem("xt_out_d"), NS // 2)
            dve.wait_ge(sem("l1_out"), GS)
            nc.vector.memset(small[:, 29:30], 0.0).then_inc(sem("y_out"), GS)
            CHAIN_B = 21
            with dve.Fori(0, NG - 1) as g:
                lk, n = chain("chain_b", g * CHAIN_B)
                layers(g, lk, True, 2 * GS + g * 6 * GS)
                assert n[0] == CHAIN_B, n[0]
            lk, n = chain("chain_b", (NG - 1) * CHAIN_B)
            layers(NG - 1, lk, False, 2 * GS + (NG - 1) * 6 * GS)

            dve.wait_ge(sem("coef4_mm"), 2)
            norm_factors(lk, averages(0, GS), gm4[:, :, NS - GS:NS], "gnvar4")
            dve.wait_ge(sem("gnrstd4"), 2)
            norm4_apply(NS - GS, NS)
            dve.wait_ge(sem("proj_out"), 2 * NS)

            def gate_and_add(l, cu, n, loads, odd, ready, prev):
                dve.wait_ge(sem("conv_out"), SUB * n + SUB)
                if not (isinstance(n, int) and n == 0):
                    dve.wait_ge(sem("gated"), n)
                v = ctxv(CT[l], UCH)
                a = CTX.rearrange("p (g u c n) -> p u g c n", g=BH, u=NU, c=UCH)[:, bass.ds(cu, 1)
                                                                                  ].rearrange("p o g c n -> p (o g) c n")
                gate = gates[:, l, :].rearrange("p (g o n) -> p g o n", g=BH, o=1)
                if l == 0:
                    TT(a, v, gate.to_broadcast([P, BH, UCH, COLS // BH]), ALU.mult).then_inc(sem("gated"), 1)
                elif l == 1:
                    for g in range(BH):
                        for j in range(2):
                            c = slice(4 * j, 4 * (j + 1))
                            t = TMP[:, :].rearrange("p (c n) -> p c n", c=4)
                            piece = 2 * g + j
                            if piece > 0:
                                dve.wait_ge(sem("tmp_added"), 3 * cu + piece)
                            TT(t, v[:, g, c, :], gate[:, g].to_broadcast([P, 4, COLS // BH]), ALU.mult
                               ).then_inc(sem("tmp_ready"), 1)
                            dve.wait_ge(sem("tmp_ready"), 4 * cu + (piece + 1))
                            TT(a[:, g, c, :], a[:, g, c, :], t, ALU.add
                               ).then_inc(sem("tmp_added" if piece < 3 else "gated"), 1)
                else:
                    for g in range(BH):
                        r = RSUM.rearrange("p (g u c s) -> p g u c s", g=BH, u=NU, c=UCH)[:, g, bass.ds(cu, 1)]
                        nc.vector.tensor_reduce(r.rearrange("p o c s -> p (o c) s"),
                                                v[:, g].rearrange("p c (k s) -> p c s k", s=NS), AX.X, ALU.add
                                                ).then_inc(sem("rsum_ready"), 1)
                    dve.wait_ge(sem("rsum_ready"), BH * cu + BH)
                    TT(v, v, gate.to_broadcast([P, BH, UCH, COLS // BH]), ALU.mult).then_inc(sem("ct2_gated"), 1)
                    dve.wait_ge(sem("ct2_gated"), cu + 1)
                    TT(a, a, v, ALU.add).then_inc(sem("gated"), 1)

            conv_steps(dve, gate_and_add)
            dve.wait_ge(sem("glob_out"), 2)

            def tail(item):
                if item(2):
                    s, hh, low = item(2)
                    dve.wait_ge(sem("q_ready"), 2 * s + hh + 1)
                    dve.wait_ge(sem("mod_mm"), 2 * s + hh + 1)
                    if low >= 2:
                        dve.wait_ge(sem("xcy_mm"), 2 * s + hh - 1)
                    STT(out=XO[hh], in0=ps[:, 2, :], scalar=BC[:, HB:HB + 1], in1=QT[hh],
                        op0=ALU.add, op1=ALU.mult).then_inc(sem("xo_ready"), 1)
                if item(4):
                    s, hh, low = item(4)
                    dve.wait_ge(sem("sd_ready"), 2 * s + hh + 1)
                    nc.vector.reciprocal(rs[:, hh, :], sd[:, hh, :]).then_inc(sem("rs_ready"), 1)
                    dve.wait_ge(sem("rs_ready"), 2 * s + hh + 1)
                    if low >= 2:
                        dve.wait_ge(sem(f"stored{hh}"), s * (16 * BH))
                    ot = OT[hh].rearrange("p (g t c) -> p t g c", g=BH, t=4)
                    r = rs[:, hh, :].rearrange("p (t g o) -> p t g o", t=4, g=BH).to_broadcast([P, 4, BH, C])
                    TT(ot, xcy(hh)[:, :, 1, :].rearrange("p t (g c) -> p t g c", g=BH), r, ALU.mult
                       ).then_inc(sem("scaled"), 1)
                    dve.wait_ge(sem("scaled"), 2 * s + hh + 1)
                    dve.wait_ge(sem("xres_mm"), 2 * s + hh + 1)
                    TT(ot, ot, ps[:, 3, :].rearrange("p (t g c) -> p t g c", t=4, g=BH), ALU.add
                       ).then_inc(sem("ot_ready"), 1)
                if item(0):
                    s, hh, low = item(0)
                    if low >= 2:
                        dve.wait_ge(sem("q_mm"), 2 * s + hh - 1)
                    one = bass.ds(s, 1)
                    xg = XBS[:, one, :].rearrange("p o (h a w) -> p (o h) a w", h=H, a=2)[:, :, hh, :]
                    TS(G4B[hh].rearrange("p (h w) -> p h w", h=H), xg, gm4[:, 0, one], gm4[:, 3, one],
                       ALU.subtract, ALU.mult).then_inc(sem("g4b_ready"), 1)
                if item(3):
                    s, hh, low = item(3)
                    dve.wait_ge(sem("sqt_ready"), 2 * s + hh + 1)
                    if low >= 1:
                        dve.wait_ge(sem("sd_ready"), 2 * s + hh)
                    nc.vector.tensor_reduce(vr[:, :], SQT[0].rearrange("p (n c) -> p n c", c=C), AX.X, ALU.add
                                            ).then_inc(sem("var_ready"), 1)

            half_slots(dve, tail)

        @block.tensor
        def _(pe):
            def mm(out, lhsT, rhs, start=True, stop=True):
                return nc.tensor.matmul(out, lhsT, rhs, start=start, stop=stop)

            pe.wait_ge(sem("ones_set"), 2)
            for ch in range(NCH):
                if ch == NCH - 2:
                    pe.wait_ge(sem("ident_set"), 1)
                    pe.wait_ge(sem("p_loaded"), 16 * 2 * W4)
                    for k in range(WB):
                        nc.tensor.transpose(unit(1)[:, P * k:P * (k + 1)], P1N[:, k, :], ident[:, :])
                        last = nc.tensor.transpose(unit(2)[:, P * k:P * (k + 1)], P3N[:, k, :], ident[:, :])
                    last.then_inc(sem("pt_mm"), 1)
                for i, (name, v) in enumerate((("swb_ready", SWB), ("sq_used", SWQ))):
                    pe.wait_ge(sem(name), ch + 1)
                    for j in range(2 * ch, 2 * ch + 2):
                        last = mm(SUMS[i][:, j:j + 1], v[:, P * j:P * (j + 1)], ones[:, 0:1])
            last.then_inc(sem("sum0_mm"), 1)
            pe.wait_ge(sem("mats_set"), 3)
            pe.wait_ge(sem("mean0_ready"), 1)
            mm(ps[:, 0, 0:B].rearrange("p (a j) -> p a j", a=2), pairm[:, :], gn0[:, 0:2, :]).then_inc(sem("coef0_mm"), 1)
            pe.wait_ge(sem("pt_ready"), 2)
            for i in range(2):
                for j in range(2):
                    pe.wait_ge(sem("diag_ready"), 2 * i + j + 1)
                    if i == 1:
                        pe.wait_ge(sem("var0_ready"), 1)
                    for n in range(2):
                        last = mm(ps[:, (4, 0)[i] + 2 * j + n, :], ones[:, :],
                                  SQ[i][:, 1024 * j + HALF * n:1024 * j + HALF * (n + 1)])
                    last.then_inc(sem("spread_mm"), 1)
            pe.wait_ge(sem("meane_ready"), 2)
            pe.wait_ge(sem("rstde_ready"), 2)
            for n in range(16):
                b8, k = n // 4, 2 * (n % 4)
                b = slice(NB8 * b8, NB8 * (b8 + 1))
                pe.wait_ge(sem("a_ready"), 2 * (b8 + 1))
                if n >= 4:
                    pe.wait_ge(sem("relu_sq"), n - 3)
                for j in range(2):
                    o = ps[:, 2 * (n % 4) + j, :]
                    mm(o, P1T[:, k + j, :], A(NB8 * b8, NB8, k + j), True, False)
                    last = mm(o, P3T[:, k + j, :],
                              SUMA[:, b, k + j:k + j + 1].to_broadcast([P, NB8, C]), False, True)
                last.then_inc(sem("relu_mm"), 1)
            pe.wait_ge(sem("bnsum_ready"), 1)
            pe.wait_ge(sem("relu_sq"), 16)
            mm(ps[:, 0, 0:2], rowm[:, :], small[:, 8:10]).then_inc(sem("bn_mm"), 1)
            pe.wait_ge(sem("early_loaded"), 16 * 6 * BH)
            pe.wait_ge(sem("cwn_ready"), BH)
            for t in range(3):
                last = nc.tensor.transpose(ps[:, 6, P * t:P * (t + 1)], CWN[:, t, :], ident[:, :])
            last.then_inc(sem("pt2_mm"), 1)
            mm(ps[:, 7, 0:1], WT[:, WPI, :], BC[:, LB:LB + 1]).then_inc(sem("pb_mm"), 1)
            pe.wait_ge(sem("bc_ready"), 4)
            mm(ps[:, 5, 0:P], WT[:, CEN, :], WT[:, WPI, :]).then_inc(sem("wpc_mm"), 1)
            pe.wait_ge(sem("bc_ready"), 5)
            def to_channels(slots):
                for s in slots:
                    pe.wait_ge(sem("x1_ready"), X1_D[s])
                    if X1_P[s] > 0:
                        pe.wait_ge(sem("x1_pool"), X1_P[s])
                    if s in range(4, 8):
                        pe.wait_ge(sem("k1_out"), s - 3)
                    elif s in range(8, 12):
                        pe.wait_ge(sem("k2_out"), s - 7)
                    elif s >= 12:
                        pe.wait_ge(sem("xt_out_d" if s % 2 == 0 else "xt_out_a"), (s - 4) // 2 + 1)
                    for k in range(WB):
                        last = nc.tensor.transpose(unit(s % 4)[:, P * k:P * (k + 1)],
                                                   AF[:, 1024 * s + P * k:1024 * s + P * (k + 1)], ident[:, :])
                    last.then_inc(sem("xt_mm"), 1)

            to_channels(range(0, 4))
            pe.wait_ge(sem("xt_out_d"), 1)

            def coef(n, bank=0):
                pe.wait_ge(sem("stats_ready"), n)
                v = ps[:, bank, 0:2 * GS].rearrange("p (a s) -> p a s", a=2)
                mm(v, pairm[:, :], me[:, :, :]).then_inc(sem("coef_mm"), 1)

            def dense(stage, g, w, src, waits, slots=range(GS)):
                for u in slots:
                    for name, all_slots, *back in waits:
                        pe.wait_ge(sem(name), GS * (g - 1 if back else g) + (GS if all_slots else u + 1))
                    for j in range(2):
                        last = mm(ps[:, 2 * u + j, :], WT[:, w, :], src[:, u, HALF * j:HALF * (j + 1)])
                    last.then_inc(sem(stage + "_mm"), 1)

            def dense_t(stage, g, w, row, src, waits):
                for u in range(GS):
                    for name, all_slots, *back in waits:
                        pe.wait_ge(sem(name), GS * (g - 1 if back else g) + (GS if all_slots else u + 1))
                    for j in range(2):
                        mm(ps[:, 2 * u + j, :].rearrange("p (k m) -> p k m", k=4), onesb[:, :],
                           ROWB[:, row:row + P].rearrange("p (o m) -> p o m", o=1).to_broadcast([P, 4, P]), True, False)
                        for k in range(4):
                            last = mm(ps[:, 2 * u + j, P * k:P * (k + 1)], src(8 * u + 4 * j + k), WT[:, w, :],
                                      False, k == 3)
                    last.then_inc(sem(stage + "_mm"), 1)

            def embed_first(g):
                dense("s1", g, WE + 0, G, [("g_ready", False), ("ob_out", False, "last group")])
                dense("k1", g, WE + 2, G, [("s1_out", False)])

            def embed_second(g):
                dense("s2", g, WE + 1, HA, [("k1_out", False)], range(0, 2))
                pe.wait_ge(sem("k1_out"), GS * g + GS)
                coef(2 * g + 1, 7)
                dense("s2", g, WE + 1, HA, [("k1_out", False)], range(2, 3))
                pe.wait_ge(sem("gnvar"), 2 * g + 1)
                dense("s2", g, WE + 1, HA, [("k1_out", False)], range(3, 4))
                dense("l1", g, WE + 4, G, [("s2_out", False)])
                dense_t("k2", g, WE + 3, 0, lambda i: HBR[:, i].rearrange("p s w -> p (s w)"),
                        [("l1_out", False), ("k1_out", True)])

            def products(g):
                dense_t("l2", g, WE + 5, P, lambda i: HAR[:, i].rearrange("p s h -> p (s h)"),
                        [("y_out", False), ("l1_out", True)])
                k0 = K0T.rearrange("p s n -> p (s n)").rearrange("p (i q) -> p i q", i=H)
                k1 = K1T.rearrange("p s n -> p (s n)").rearrange("p (j q) -> p j q", j=W)
                for u in range(GS):
                    pe.wait_ge(sem("mats_set"), 3)
                    pe.wait_ge(sem("l2_out"), GS * g + GS)
                    for q in range(32):
                        for s in range(GS):
                            p = slice(32 * s, 32 * (s + 1))
                            last = mm(ps[p, 2 * u + q // 16, 32 * (q % 16):32 * (q % 16 + 1)],
                                      k0[p, :, 32 * u + q], k1[p, :, 32 * u + q])
                    last.then_inc(sem("ein_mm"), 1)

            def residuals(g, more):
                pe.wait_ge(sem("ein_out"), GS * g + GS)
                if more:
                    coef(2 * g + 2, 7)
                else:
                    coef4(0, NS - GS, 7)
                e1 = E1.rearrange("p s n -> p (s n)").rearrange("p (j q) -> p j q", j=W)
                for u in range(GS):
                    if u == GS - 1:
                        if more:
                            pe.wait_ge(sem("gnvar"), 2 * g + 2)
                        else:
                            pe.wait_ge(sem("gnvar4"), 1)
                    for k in range(8):
                        last = nc.tensor.transpose(unit(u)[:, P * k:P * (k + 1)], e1[:, 8 * u + k, :], ident[:, :])
                    last.then_inc(sem("tr_mm"), 1)
                dense("m0a", g, WM + 0, M, [("tr_out", True)])
                dense("m0b", g, WM + 1, HA, [("m0a_out", False)])
                dense("m1a", g, WM + 2, M, [("m0b_out", False), ("res0", False)])
                dense("m1b", g, WM + 3, HA, [("m1a_out", False)])
                dense("oa", g, WO + 0, M, [("m1b_out", False), ("z1_ready", False)])
                dense("ob", g, WO + 1, HA, [("oa_out", False)])

            def third_layer(g, more):
                z = (Z if more else M).rearrange("p s (h w) -> p s h w", h=H)
                for u in range(GS):
                    if u == 1:
                        pe.wait_ge(sem("xh_ready"), 2 * g + 2)
                        if more:
                            pe.wait_ge(sem("k2_out"), GS * g + 2 * GS)
                        else:
                            pe.wait_ge(sem("proj_out"), 2 * PROJ_BEFORE)
                        for t in range(3):
                            last = mm(ps[:, 7, 0:GS * W], WT[:, WC + t, :], xh[:, t, :, :].rearrange("p s w -> p (s w)"),
                                      t == 0, t == 2)
                        last.then_inc(sem("t_mm"), 1)
                    pe.wait_ge(sem("z_ready"), GS * g + u + 1)
                    if u == GS - 1:
                        pe.wait_ge(sem("t_out"), g + 1)
                    elif more:
                        pe.wait_ge(sem("k2_out"), GS * g + GS + u + 1)
                    else:
                        pe.wait_ge(sem("proj_out"), 2 * PROJ_BEFORE - GS + u + 1)
                    for j in range(2):
                        h0, h1 = 16 * j, 16 * (j + 1)
                        for n, t in enumerate((1, 0, 2)):
                            lo, hi = max(h0, 1 - t), min(h1, H + 1 - t)
                            last = mm(ps[:, 2 * u + j, W * (lo - h0):W * (hi - h0)], WT[:, WC + t, :],
                                      z[:, u, lo + t - 1:hi + t - 1, :].rearrange("p h w -> p (h w)"), n == 0, n == 2)
                    last.then_inc(sem("y_mm"), 1)

            def coef4(s0, s1, bank):
                pe.wait_ge(sem("stats4_ready"), s1 // GS)
                v = ps[:, bank, 0:2 * (s1 - s0)].rearrange("p (a s) -> p a s", a=2)
                mm(v, pairm[:, :], me4[:, :, s0:s1]).then_inc(sem("coef4_mm"), 1)

            def project(s0, s1):
                g4 = G4.rearrange("p s (k n) -> p s k n", k=WB)
                for n in range(2 * s0, 2 * s1):
                    s, k0_ = n // 2, 4 * (n % 2)
                    pe.wait_ge(sem("g4_ready"), s + 1)
                    if n < 4:
                        pe.wait_ge(sem("ob_out"), GS * (NG - 1) + n + 1)
                    elif 2 * PROJ_BEFORE <= n < 2 * PROJ_BEFORE + 4:
                        pe.wait_ge(sem("y_out"), GS * NG + n - 2 * PROJ_BEFORE + 1)
                    else:
                        pe.wait_ge(sem("proj_out"), n - 3)
                    if n == 2 * PROJ_EARLY:
                        pe.wait_ge(sem("gnvar"), 2 * NG)
                    if n == 2 * (NS - GS):
                        pe.wait_ge(sem("gnvar4"), 2)
                    for j in range(2):
                        o = ps[:, 2 * (n % 4) + j, :].rearrange("p (k m) -> p k m", k=2)[:, :, 0:P + 8]
                        mm(o, onesb[:, :], ROWB[:, 2 * P:3 * P + 8].rearrange("p (o m) -> p o m", o=1
                                                                             ).to_broadcast([P, 2, P + 8]), True, False)
                        for i in range(2):
                            last = mm(o[:, i, :], g4[:, s % GS, k0_ + 2 * j + i], WCG[:, :], False, i == 1)
                    last.then_inc(sem("proj_mm"), 1)

            coef(1)
            pe.wait_ge(sem("w_loaded"), 16 * 12 * BH)
            dense("s1", 0, WE + 0, G, [("g_ready", False)])
            dense("k1", 0, WE + 2, G, [("s1_out", False)])
            to_channels(range(4, 8))
            pe.wait_ge(sem("rowb_set"), 1)
            pe.wait_ge(sem("xt_out_a"), 4)
            pe.wait_ge(sem("xt_out_d"), 4)
            dense_t("k2", 0, WE + 3, 0, lambda i: HBR0[:, i].rearrange("p s w -> p (s w)"), [("k1_out", True)])
            to_channels(range(8, NS))
            pe.wait_ge(sem("xt_out_a"), 8)
            pe.wait_ge(sem("xt_out_d"), 8)
            dense("s2", 0, WE + 1, HA0, [("s1_out", False)])
            dense("l1", 0, WE + 4, G, [("s2_out", False)])
            with pe.Fori(0, NG - 1) as g:
                products(g)
                residuals(g, True)
                embed_first(g + 1)
                embed_second(g + 1)
                third_layer(g, True)
            products(NG - 1)
            residuals(NG - 1, False)
            project(0, PROJ_EARLY)
            pe.wait_ge(sem("proj_out"), 2 * PROJ_EARLY - 3)
            coef(2 * NG)
            project(PROJ_EARLY, PROJ_BEFORE)
            third_layer(NG - 1, False)
            project(PROJ_BEFORE, NS - GS - 1)
            pe.wait_ge(sem("proj_out"), 2 * (NS - GS) - 3)
            coef4(NS - GS, NS, 0)
            project(NS - GS - 1, NS)
            pe.wait_ge(sem("proj_out"), 2 * NS)

            def conv(l, cu, n, loads, odd, ready, prev):
                slot = odd
                v = ctxv(CTX if l == 0 else CT[l - 1], C if l == 0 else UCH)
                if l >= 1:
                    pe.wait_ge(sem("conv_out"), SUB * ready + SUB)
                pe.wait_ge(sem(f"ring_loaded{slot}"), loads)
                band = RG[:, slot, :].rearrange("p (j m c) -> p j m c", j=NJ // W4, c=UCH)
                for j in range(SUB):
                    if not (isinstance(n, int) and n < 2):
                        pe.wait_ge(sem("conv_out"), SUB * n + (j - 3))
                    for c in range(UCH // SUB * j, UCH // SUB * (j + 1)):
                        o = ps[:, 4 * slot + c // 2, COLS * (c % 2):COLS * (c % 2 + 1)].rearrange("p (g n) -> p g n", g=BH)
                        if l == 0:
                            x = v.rearrange("p g (u c) n -> p g u c n", u=NU)[:, :, bass.ds(cu, 1), c, :
                                                                               ].rearrange("p g o n -> p g (o n)")
                        else:
                            x = v[:, :, c, :]
                        mm(o, band[:, 1, :, c], x, True, False)
                        (n_in, n_out), (p_in, p_out) = ([slice(H * a, H * b) for a, b in halo] for halo in halos(l))
                        mm(o[p_out, :, NS:], band[p_in, 2, p_out, c], x[p_in, :, 0:NS * (WB - 1)], False, l == 1)
                        last = mm(o[n_out, :, 0:NS * (WB - 1)], band[n_in, 0, n_out, c], x[n_in, :, NS:], False, True)
                    last.then_inc(sem("conv_mm"), 1)

            conv_steps(pe, conv)
            pe.wait_ge(sem("rsum_ready"), BH * NU)
            for j in range(4):
                last = mm(ps[:, j, :], ones[:, :], RSUM[:, HALF * j:HALF * (j + 1)])
            last.then_inc(sem("glob_mm"), 1)
            pe.wait_ge(sem("glob_out"), 2)

            def tail(item):
                if item(2):
                    s, hh, low = item(2)
                    pe.wait_ge(sem("g4b_ready"), 2 * s + hh + 1)
                    if low >= 1:
                        pe.wait_ge(sem("q_ready"), 2 * s + hh)
                    mm(ps[:, 1, :], WT[:, WQ, :], G4B[hh]).then_inc(sem("q_mm"), 1)
                    pe.wait_ge(sem("mb_ready"), 2 * s + hh + 1)
                    if low >= 1:
                        pe.wait_ge(sem("xo_ready"), 2 * s + hh)
                    mm(ps[:, 2, :], WT[:, WHI, :], MBT[hh]).then_inc(sem("mod_mm"), 1)
                if item(4):
                    s, hh, low = item(4)
                    pe.wait_ge(sem("xr_ready"), 2 * s + hh + 1)
                    if low >= 1:
                        pe.wait_ge(sem("ot_ready"), 2 * s + hh)
                    y = XR[hh].rearrange("p (n t) -> p t n", t=4)
                    for t in range(4):
                        last = nc.tensor.transpose(ps[:, 3, P * t:P * (t + 1)], y[:, t, :], ident[:, :])
                    last.then_inc(sem("xres_mm"), 1)
                if item(1):
                    s, hh, low = item(1)
                    pe.wait_ge(sem("as_ready"), 2 * s + hh + 1)
                    if low >= 1:
                        pe.wait_ge(sem("mb_ready"), 2 * s + hh)
                    for k in range(4):
                        last = nc.tensor.transpose(ps[:, 0, P * k:P * (k + 1)], AS[hh][:, P * k:P * (k + 1)], ident[:, :])
                    last.then_inc(sem("mb_mm"), 1)
                if item(3):
                    s, hh, low = item(3)
                    pe.wait_ge(sem("xo_ready"), 2 * s + hh + 1)
                    if low >= 2:
                        pe.wait_ge(sem("ot_ready"), 2 * s + hh - 1)
                    y = XO[hh].rearrange("p (n t) -> p t n", t=4)
                    for t in range(4):
                        last = mm(xcy(hh)[:, t, :, :], y[:, t, :], WT[:, CEN:CEN + 2, :])
                    last.then_inc(sem("xcy_mm"), 1)

            half_slots(pe, tail)


_INS = ['x', 'L0_conv_P1', 'L0_conv_P3', 'L0_conv_gamma', 'L0_conv_beta', 'L1_conv_emb_W', 'L1_conv_emb_b',
        'L1_conv_mult_W', 'L1_conv_mult_b', 'L1_conv_out_W', 'L1_conv_out_b', 'L2_conv_W', 'L2_conv_b',
        'L3_conv_Wf', 'L3_conv_bf', 'L3_conv_k0', 'L3_conv_k1', 'L3_conv_k2', 'L3_conv_Wh', 'L3_conv_bh',
        'L3_conv_gamma', 'L3_conv_beta', 'L3_conv_Wp', 'L3_conv_bp']
_OUTS = [((32, 32, 32, 64), 'float32')]


def kernel(**inputs):
    import numpy as _np
    import concourse.bacc as _bacc
    from concourse import mybir as _mybir
    from concourse.bass_utils import run_bass_kernel_spmd as _run

    nc = _bacc.Bacc("TRN2", target_bir_lowering=False, num_devices=1)
    arrays, args = {}, []
    for name in _INS:
        a = _np.ascontiguousarray(inputs[name])
        arrays[f"in_{name}_dram"] = a
        args.append(nc.dram_tensor(f"in_{name}_dram", a.shape, _mybir.dt.from_np(a.dtype), kind="ExternalInput").ap())
    for i, (shape, dtype) in enumerate(_OUTS):
        dt = _mybir.dt.from_np(_np.dtype(dtype))
        args.append(nc.dram_tensor(f"out_{i}_dram", shape, dt, kind="ExternalOutput").ap())
    conv_preact_kernel(nc, *args)
    r = _run(nc, [arrays], core_ids=[0])
    return r.results[0]["out_0_dram"]
```
